# Optimizing a Trainium2 kernel written in Bass

```python
import numpy as np
import jax
import jax.numpy as jnp

def _softmax(x, axis=-1):
    return jax.nn.softmax(x, axis=axis)

def _gelu(x):
    return jax.nn.gelu(x, approximate=True)

def _silu(x):
    return jax.nn.silu(x)

def _sigmoid(x):
    return jax.nn.sigmoid(x)

def _layernorm(x, axis=-1, eps=1e-05):
    m = jnp.mean(x, axis=axis, keepdims=True)
    v = jnp.var(x, axis=axis, keepdims=True)
    return (x - m) / jnp.sqrt(v + eps)

def _scatter_add(tgt, idx, src, axis=0):
    return tgt.at[idx].add(src)

def _segment_sum(src, seg, n):
    return jax.ops.segment_sum(src, seg, n)
kernel_name = 'mk_prb_d4_jaxref_r8_773fc1'

def setup_inputs(seed: int=0):
    np.random.seed(seed)
    _w = jnp.asarray

    def _L0_attn_setup():
        import jax, jax.numpy as jnp
        import numpy as np
        D_MODEL = 128
        N_HEADS = 16
        HEAD_DIM = D_MODEL // N_HEADS
        FEATURE_DIM = 64
        BATCH = 4
        SEQ = 512
        key = jax.random.key(seed)
        ks = jax.random.split(key, 8)
        s = 1.0 / np.sqrt(D_MODEL)
        sf = 1.0 / np.sqrt(HEAD_DIM)
        return {'x': jax.random.normal(ks[0], (BATCH, SEQ, D_MODEL), dtype=jnp.float32), 'Wq': jax.random.normal(ks[1], (D_MODEL, D_MODEL), dtype=jnp.float32) * s, 'Wk': jax.random.normal(ks[2], (D_MODEL, D_MODEL), dtype=jnp.float32) * s, 'Wv': jax.random.normal(ks[3], (D_MODEL, D_MODEL), dtype=jnp.float32) * s, 'Wo': jax.random.normal(ks[4], (D_MODEL, D_MODEL), dtype=jnp.float32) * s, 'bo': jax.random.normal(ks[5], (D_MODEL,), dtype=jnp.float32) * s, 'Wf': jax.random.normal(ks[6], (HEAD_DIM, FEATURE_DIM), dtype=jnp.float32) * sf, 'bf': jax.random.normal(ks[7], (FEATURE_DIM,), dtype=jnp.float32) * sf}
    _L0_attn_in = _L0_attn_setup()

    def _L0_ffn_setup():
        import jax, jax.numpy as jnp
        import numpy as np
        NUM_EXPERTS = 8
        TOP_K = 2
        CAPACITY_FACTOR = 1.25
        key = jax.random.key(seed)
        k1, k2, k3, k4, k5 = jax.random.split(key, 5)
        B, S, H, I, E = (4, 256, 128, 512, NUM_EXPERTS)
        return {'hidden_states': jax.random.normal(k1, (B, S, H), dtype=jnp.float32), 'router_gate': jax.random.normal(k2, (H, E), dtype=jnp.float32) * 0.02, 'gate_w': jax.random.normal(k3, (E, H, I), dtype=jnp.float32) * 0.02, 'up_w': jax.random.normal(k4, (E, H, I), dtype=jnp.float32) * 0.02, 'down_w': jax.random.normal(k5, (E, I, H), dtype=jnp.float32) * 0.02}
    _L0_ffn_in = _L0_ffn_setup()

    def _L1_attn_setup():
        import jax, jax.numpy as jnp
        import numpy as np
        B, T, C = (64, 32, 128)
        N_HEAD, HEAD_SIZE, KV_RANK = (16, 64, 128)
        BLOCK_SIZE = 32
        key = jax.random.key(seed)
        ks = jax.random.split(key, 5)
        HD = N_HEAD * HEAD_SIZE

        def init(k, shape):
            fan_in = shape[0]
            bound = 1.0 / np.sqrt(fan_in)
            return jax.random.uniform(k, shape, jnp.float32, -bound, bound)
        return {'x': jax.random.normal(ks[0], (B, T, C), jnp.float32), 'w_kv_down': init(ks[1], (C, KV_RANK)), 'w_kv_up': init(ks[2], (KV_RANK, 2 * HD)), 'w_q': init(ks[3], (C, HD)), 'w_out': init(ks[4], (HD, C))}
    _L1_attn_in = _L1_attn_setup()

    def _L1_ffn_setup():
        import jax, jax.numpy as jnp
        import numpy as np
        CAPACITY_FACTOR = 1.25
        key = jax.random.key(seed)
        k1, k2, k3, k4 = jax.random.split(key, 4)
        B, T, D, F, E = (4, 512, 128, 512, 8)
        s = 0.02
        return {'x': jax.random.normal(k1, (B, T, D), dtype=jnp.float32), 'wg': jax.random.normal(k2, (D, E), dtype=jnp.float32) * s, 'W1': jax.random.normal(k3, (E, D, F), dtype=jnp.float32) * s, 'b1': jnp.zeros((E, F), dtype=jnp.float32), 'W2': jax.random.normal(k4, (E, F, D), dtype=jnp.float32) * s, 'b2': jnp.zeros((E, D), dtype=jnp.float32)}
    _L1_ffn_in = _L1_ffn_setup()

    def _L2_attn_setup():
        import jax, jax.numpy as jnp
        import numpy as np
        NUM_HEADS = 16
        DIM = 128
        key = jax.random.key(seed)
        kx, kwq, kbq, kwk, kbk = jax.random.split(key, 5)
        B, N, C = (2, 256, DIM)
        s = 1.0 / np.sqrt(C)
        return {'x': jax.random.normal(kx, (B, N, C), dtype=jnp.float32), 'Wq': jax.random.normal(kwq, (C, C), dtype=jnp.float32) * s, 'bq': jax.random.normal(kbq, (C,), dtype=jnp.float32) * 0.01, 'Wk': jax.random.normal(kwk, (C, C), dtype=jnp.float32) * s, 'bk': jax.random.normal(kbk, (C,), dtype=jnp.float32) * 0.01}
    _L2_attn_in = _L2_attn_setup()

    def _L2_ffn_setup():
        import math
        import jax, jax.numpy as jnp
        import numpy as np
        NUM_EXPERTS = 8
        CAPACITY_FACTOR = 1.5
        key = jax.random.key(seed)
        ks = jax.random.split(key, 4)
        B, T, D, F, E = (4, 256, 128, 512, NUM_EXPERTS)
        scale = 0.02
        return {'x': jax.random.normal(ks[0], (B, T, D), dtype=jnp.float32), 'router_w': jax.random.normal(ks[1], (E, D), dtype=jnp.float32) * scale, 'w1': jax.random.normal(ks[2], (E, D, F), dtype=jnp.float32) * scale, 'b1': jnp.zeros((E, F), dtype=jnp.float32), 'w2': jax.random.normal(ks[3], (E, F, D), dtype=jnp.float32) * scale, 'b2': jnp.zeros((E, D), dtype=jnp.float32)}
    _L2_ffn_in = _L2_ffn_setup()

    def _L3_attn_setup():
        import jax, jax.numpy as jnp
        import numpy as np
        EPS = 0.0001

        def mp_normalize(x, axis):
            red = int(np.prod([x.shape[a] for a in axis])) if isinstance(axis, (list, tuple)) else x.shape[axis]
            w = jnp.sqrt(jnp.sum(jnp.square(x.astype(jnp.float32)), axis=axis, keepdims=True))
            w = EPS + w / np.sqrt(red)
            return x / w.astype(x.dtype)

        def mp_linear(x, w, gain):
            fan_in = w.shape[1]
            wn = mp_normalize(w.astype(jnp.float32), axis=(1,)) * (gain / np.sqrt(fan_in))
            return jnp.einsum('bse,oe->bso', x, wn.astype(x.dtype))

        def attention(query, gain, w_q, w_k, w_v, w_o, num_heads=16, attn_balance=0.5):
            B, S, E = query.shape
            hd = E // num_heads
            res = query
            q = mp_linear(query, w_q, gain).reshape(B, S, num_heads, hd).transpose(0, 2, 1, 3)
            k = mp_linear(query, w_k, gain).reshape(B, S, num_heads, hd).transpose(0, 2, 1, 3)
            v = mp_linear(query, w_v, gain).reshape(B, S, num_heads, hd).transpose(0, 2, 1, 3)
            q = mp_normalize(q, axis=(3,))
            k = mp_normalize(k, axis=(3,))
            scores = jnp.einsum('bnsh,bnsk->bnhk', q, k / np.sqrt(S))
            attn = jax.nn.softmax(scores, axis=3)
            o = jnp.einsum('bnhk,bnsk->bnsh', attn, v)
            o = o.transpose(0, 2, 1, 3).reshape(B, S, E)
            out = mp_linear(o, w_o, gain)
            t = attn_balance
            return (res * (1.0 - t) + out * t) / np.sqrt((1 - t) ** 2 + t ** 2)
        key = jax.random.key(seed)
        ks = jax.random.split(key, 5)
        B, S, E = (4, 512, 128)
        return {'query': jax.random.normal(ks[0], (B, S, E), dtype=jnp.float32), 'gain': jnp.float32(1.0), 'w_q': jax.random.normal(ks[1], (E, E), dtype=jnp.float32), 'w_k': jax.random.normal(ks[2], (E, E), dtype=jnp.float32), 'w_v': jax.random.normal(ks[3], (E, E), dtype=jnp.float32), 'w_o': jax.random.normal(ks[4], (E, E), dtype=jnp.float32)}
    _L3_attn_in = _L3_attn_setup()

    def _L3_ffn_setup():
        import jax, jax.numpy as jnp
        import numpy as np
        DIM = 128

        def _reference_tuple_inner(x, W_r, W_k, W_v, mu_r, mu_k):
            B, T, C = x.shape
            x_prev = jnp.concatenate([jnp.zeros((B, 1, C), x.dtype), x[:, :-1, :]], axis=1)
            xr = mu_r * x + (1.0 - mu_r) * x_prev
            xk = mu_k * x + (1.0 - mu_k) * x_prev
            r = jax.nn.sigmoid(jnp.einsum('btc,dc->btd', xr, W_r))
            k = jnp.einsum('btc,dc->btd', xk, W_k)
            k_act = jnp.square(jax.nn.relu(k))
            out = r * jnp.einsum('btc,dc->btd', k_act, W_v)
            new_state = x[:, -1, :]
            return (out, new_state)
        key = jax.random.key(seed)
        ks = jax.random.split(key, 6)
        B, T, C = (8, 256, DIM)
        x = jax.random.normal(ks[0], (B, T, C), dtype=jnp.float32)
        s = 1.0 / np.sqrt(C)
        W_r = jax.random.uniform(ks[1], (C, C), jnp.float32, -s, s)
        W_k = jax.random.uniform(ks[2], (C, C), jnp.float32, -s, s)
        W_v = jax.random.uniform(ks[3], (C, C), jnp.float32, -s, s)
        mu_r = jax.random.uniform(ks[4], (C,), jnp.float32)
        mu_k = jax.random.uniform(ks[5], (C,), jnp.float32)
        return {'x': x, 'W_r': W_r, 'W_k': W_k, 'W_v': W_v, 'mu_r': mu_r, 'mu_k': mu_k}
    _L3_ffn_in = _L3_ffn_setup()
    _d = {'L0_attn_x': _L0_attn_in['x'], 'L0_attn_Wq': _L0_attn_in['Wq'], 'L0_attn_Wk': _L0_attn_in['Wk'], 'L0_attn_Wv': _L0_attn_in['Wv'], 'L0_attn_Wo': _L0_attn_in['Wo'], 'L0_attn_bo': _L0_attn_in['bo'], 'L0_attn_Wf': _L0_attn_in['Wf'], 'L0_attn_bf': _L0_attn_in['bf'], 'L0_ffn_router_gate': _L0_ffn_in['router_gate'], 'L0_ffn_gate_w': _L0_ffn_in['gate_w'], 'L0_ffn_up_w': _L0_ffn_in['up_w'], 'L0_ffn_down_w': _L0_ffn_in['down_w'], 'L1_attn_w_kv_down': _L1_attn_in['w_kv_down'], 'L1_attn_w_kv_up': _L1_attn_in['w_kv_up'], 'L1_attn_w_q': _L1_attn_in['w_q'], 'L1_attn_w_out': _L1_attn_in['w_out'], 'L1_ffn_wg': _L1_ffn_in['wg'], 'L1_ffn_W1': _L1_ffn_in['W1'], 'L1_ffn_b1': _L1_ffn_in['b1'], 'L1_ffn_W2': _L1_ffn_in['W2'], 'L1_ffn_b2': _L1_ffn_in['b2'], 'L2_attn_Wq': _L2_attn_in['Wq'], 'L2_attn_bq': _L2_attn_in['bq'], 'L2_attn_Wk': _L2_attn_in['Wk'], 'L2_attn_bk': _L2_attn_in['bk'], 'L2_ffn_router_w': _L2_ffn_in['router_w'], 'L2_ffn_w1': _L2_ffn_in['w1'], 'L2_ffn_b1': _L2_ffn_in['b1'], 'L2_ffn_w2': _L2_ffn_in['w2'], 'L2_ffn_b2': _L2_ffn_in['b2'], 'L3_attn_gain': _L3_attn_in['gain'], 'L3_attn_w_q': _L3_attn_in['w_q'], 'L3_attn_w_k': _L3_attn_in['w_k'], 'L3_attn_w_v': _L3_attn_in['w_v'], 'L3_attn_w_o': _L3_attn_in['w_o'], 'L3_ffn_W_r': _L3_ffn_in['W_r'], 'L3_ffn_W_k': _L3_ffn_in['W_k'], 'L3_ffn_W_v': _L3_ffn_in['W_v'], 'L3_ffn_mu_r': _L3_ffn_in['mu_r'], 'L3_ffn_mu_k': _L3_ffn_in['mu_k']}
    _x0 = _d['L0_attn_x']
    _d['L0_attn_x'] = jax.random.normal(jax.random.fold_in(jax.random.key(seed), 1), (8, 256, 128), dtype=_x0.dtype)
    del _x0
    return _d

def reference(L0_attn_x, L0_attn_Wq, L0_attn_Wk, L0_attn_Wv, L0_attn_Wo, L0_attn_bo, L0_attn_Wf, L0_attn_bf, L0_ffn_router_gate, L0_ffn_gate_w, L0_ffn_up_w, L0_ffn_down_w, L1_attn_w_kv_down, L1_attn_w_kv_up, L1_attn_w_q, L1_attn_w_out, L1_ffn_wg, L1_ffn_W1, L1_ffn_b1, L1_ffn_W2, L1_ffn_b2, L2_attn_Wq, L2_attn_bq, L2_attn_Wk, L2_attn_bk, L2_ffn_router_w, L2_ffn_w1, L2_ffn_b1, L2_ffn_w2, L2_ffn_b2, L3_attn_gain, L3_attn_w_q, L3_attn_w_k, L3_attn_w_v, L3_attn_w_o, L3_ffn_W_r, L3_ffn_W_k, L3_ffn_W_v, L3_ffn_mu_r, L3_ffn_mu_k):

    def _L0_attn_ref(x, Wq, Wk, Wv, Wo, bo, Wf, bf):
        import jax, jax.numpy as jnp
        import numpy as np
        D_MODEL = 128
        N_HEADS = 16
        HEAD_DIM = D_MODEL // N_HEADS
        FEATURE_DIM = 64
        BATCH = 4
        SEQ = 512
        b, l, d = x.shape
        q = (x @ Wq).reshape(b, l, N_HEADS, HEAD_DIM)
        k = (x @ Wk).reshape(b, l, N_HEADS, HEAD_DIM)
        v = (x @ Wv).reshape(b, l, N_HEADS, HEAD_DIM)
        qf = jax.nn.relu(q @ Wf + bf)
        kf = jax.nn.relu(k @ Wf + bf)
        kv = jnp.einsum('blhf,blhd->bhfd', kf, v)
        out = jnp.einsum('blhf,bhfd->blhd', qf, kv)
        k_sum = kf.sum(axis=1)
        normalizer = jnp.einsum('blhf,bhf->blh', qf, k_sum)[..., None]
        normalizer = jnp.maximum(normalizer, 1e-06)
        out = (out / normalizer).reshape(b, l, d)
        return out @ Wo + bo

    def _L0_ffn_ref(hidden_states, router_gate, gate_w, up_w, down_w):
        import jax, jax.numpy as jnp
        import numpy as np
        NUM_EXPERTS = 8
        TOP_K = 2
        CAPACITY_FACTOR = 1.25
        B, S, H = hidden_states.shape
        E = router_gate.shape[1]
        K = TOP_K
        x = hidden_states.reshape(-1, H)
        T = x.shape[0]
        cap = int(CAPACITY_FACTOR * ((T * K + E - 1) // E))
        probs = jax.nn.softmax(x @ router_gate, axis=-1)
        topw, topi = jax.lax.top_k(probs, K)
        topw = topw / (topw.sum(-1, keepdims=True) + 1e-09)
        gates = jnp.zeros((T, E), x.dtype).at[jnp.arange(T)[:, None], topi].set(topw)
        top_g, tok_idx = jax.lax.top_k(gates.T, cap)
        xe = x[tok_idx]
        h = jax.nn.silu(jnp.einsum('ech,ehi->eci', xe, gate_w)) * jnp.einsum('ech,ehi->eci', xe, up_w)
        ye = jnp.einsum('eci,eih->ech', h, down_w) * top_g[..., None]
        out = jnp.zeros_like(x).at[tok_idx.reshape(-1)].add(ye.reshape(-1, H))
        return out.reshape(B, S, H)

    def _L1_attn_ref(x, w_kv_down, w_kv_up, w_q, w_out):
        import jax, jax.numpy as jnp
        import numpy as np
        B, T, C = (64, 32, 128)
        N_HEAD, HEAD_SIZE, KV_RANK = (16, 64, 128)
        BLOCK_SIZE = 32
        Bx, Tx, Cx = x.shape
        HD = N_HEAD * HEAD_SIZE
        latent_kv = x @ w_kv_down
        kv = latent_kv @ w_kv_up
        k, v = (kv[..., :HD], kv[..., HD:])
        k = k.reshape(Bx, Tx, N_HEAD, HEAD_SIZE)
        v = v.reshape(Bx, Tx, N_HEAD, HEAD_SIZE)
        q = (x @ w_q).reshape(Bx, Tx, N_HEAD, HEAD_SIZE)
        scale = HEAD_SIZE ** (-0.5)
        att = jnp.einsum('bqhd,bkhd->bhqk', q, k) * scale
        causal = jnp.tril(jnp.ones((Tx, Tx), dtype=bool))
        att = jnp.where(causal, att, -jnp.inf)
        att = jax.nn.softmax(att, axis=-1)
        y = jnp.einsum('bhqk,bkhd->bqhd', att, v)
        y = y.reshape(Bx, Tx, HD)
        return y @ w_out

    def _L1_ffn_ref(x, wg, W1, b1, W2, b2):
        import jax, jax.numpy as jnp
        import numpy as np
        CAPACITY_FACTOR = 1.25
        B, T, D = x.shape
        E = wg.shape[1]
        N = B * T
        capacity = int(N / E * CAPACITY_FACTOR) + 1
        xf = x.reshape(N, D)
        logits = xf @ wg
        scores = jax.nn.softmax(logits, axis=-1)
        top1 = jnp.argmax(scores, axis=-1)
        combine_w = jnp.take_along_axis(scores, top1[:, None], axis=1)[:, 0]
        oh = jax.nn.one_hot(top1, E, dtype=jnp.int32)
        rank = jnp.take_along_axis(jnp.cumsum(oh, axis=0), top1[:, None], axis=1)[:, 0] - 1
        valid = rank < capacity
        trash = E * capacity
        slot = jnp.where(valid, top1 * capacity + rank, trash)
        buf = jnp.zeros((E * capacity + 1, D), dtype=x.dtype).at[slot].set(xf)
        eb = buf[:E * capacity].reshape(E, capacity, D)
        h = jax.nn.gelu(jnp.einsum('ecd,edf->ecf', eb, W1) + b1[:, None, :], approximate=False)
        y = jnp.einsum('ecf,efd->ecd', h, W2) + b2[:, None, :]
        yf = y.reshape(E * capacity, D)
        gathered = yf[jnp.minimum(slot, E * capacity - 1)]
        out_flat = jnp.where(valid[:, None], gathered, 0.0) * combine_w[:, None]
        return out_flat.reshape(B, T, D)

    def _L2_attn_ref(x, Wq, bq, Wk, bk):
        import jax, jax.numpy as jnp
        import numpy as np
        NUM_HEADS = 16
        DIM = 128
        B, N, C = x.shape
        H = NUM_HEADS
        Dh = C // H
        q = (x @ Wq + bq).reshape(B, N, H, Dh).transpose(0, 2, 1, 3)
        k = (x @ Wk + bk).reshape(B, N, H, Dh).transpose(0, 2, 1, 3)
        v = k
        scale = C ** (-0.5)
        attn = jnp.einsum('bhnd,bhmd->bhnm', q, k) * scale
        attn = jax.nn.softmax(attn, axis=-1)
        out = jnp.einsum('bhnm,bhmd->bhnd', attn, v)
        return out.transpose(0, 2, 1, 3).reshape(B, N, C)

    def _L2_ffn_ref(x, router_w, w1, b1, w2, b2):
        import math
        import jax, jax.numpy as jnp
        import numpy as np
        NUM_EXPERTS = 8
        CAPACITY_FACTOR = 1.5
        B, T, D = x.shape
        E = router_w.shape[0]
        N = B * T
        C = max(math.ceil(CAPACITY_FACTOR * N / E), 1)
        x_flat = x.reshape(N, D)
        logits = x_flat @ router_w.T
        probs = jax.nn.softmax(logits, axis=-1)
        chosen_e = jnp.argmax(probs, axis=-1)
        chosen_p = jnp.max(probs, axis=-1)
        onehot = jax.nn.one_hot(chosen_e, E, dtype=jnp.float32)
        pos = jnp.take_along_axis(jnp.cumsum(onehot, axis=0), chosen_e[:, None], axis=1)[:, 0] - 1.0
        pos = pos.astype(jnp.int32)
        kept = pos < C
        pos_c = jnp.clip(pos, 0, C - 1)
        buf = jnp.zeros((E, C, D), dtype=x.dtype).at[chosen_e, pos_c].add(x_flat * kept[:, None].astype(x.dtype))
        h = jax.nn.gelu(jnp.einsum('ecd,edf->ecf', buf, w1) + b1[:, None, :], approximate=False)
        eo = jnp.einsum('ecf,efd->ecd', h, w2) + b2[:, None, :]
        y = eo[chosen_e, pos_c] * (chosen_p * kept.astype(x.dtype))[:, None]
        return y.reshape(B, T, D)

    def _L3_attn_ref(query, gain, w_q, w_k, w_v, w_o):
        import jax, jax.numpy as jnp
        import numpy as np
        EPS = 0.0001

        def mp_normalize(x, axis):
            red = int(np.prod([x.shape[a] for a in axis])) if isinstance(axis, (list, tuple)) else x.shape[axis]
            w = jnp.sqrt(jnp.sum(jnp.square(x.astype(jnp.float32)), axis=axis, keepdims=True))
            w = EPS + w / np.sqrt(red)
            return x / w.astype(x.dtype)

        def mp_linear(x, w, gain):
            fan_in = w.shape[1]
            wn = mp_normalize(w.astype(jnp.float32), axis=(1,)) * (gain / np.sqrt(fan_in))
            return jnp.einsum('bse,oe->bso', x, wn.astype(x.dtype))

        def attention(query, gain, w_q, w_k, w_v, w_o, num_heads=16, attn_balance=0.5):
            B, S, E = query.shape
            hd = E // num_heads
            res = query
            q = mp_linear(query, w_q, gain).reshape(B, S, num_heads, hd).transpose(0, 2, 1, 3)
            k = mp_linear(query, w_k, gain).reshape(B, S, num_heads, hd).transpose(0, 2, 1, 3)
            v = mp_linear(query, w_v, gain).reshape(B, S, num_heads, hd).transpose(0, 2, 1, 3)
            q = mp_normalize(q, axis=(3,))
            k = mp_normalize(k, axis=(3,))
            scores = jnp.einsum('bnsh,bnsk->bnhk', q, k / np.sqrt(S))
            attn = jax.nn.softmax(scores, axis=3)
            o = jnp.einsum('bnhk,bnsk->bnsh', attn, v)
            o = o.transpose(0, 2, 1, 3).reshape(B, S, E)
            out = mp_linear(o, w_o, gain)
            t = attn_balance
            return (res * (1.0 - t) + out * t) / np.sqrt((1 - t) ** 2 + t ** 2)
        return attention(query, gain, w_q, w_k, w_v, w_o)

    def _L3_ffn_ref(x, W_r, W_k, W_v, mu_r, mu_k):
        import jax, jax.numpy as jnp
        import numpy as np
        DIM = 128

        def _reference_tuple_inner(x, W_r, W_k, W_v, mu_r, mu_k):
            B, T, C = x.shape
            x_prev = jnp.concatenate([jnp.zeros((B, 1, C), x.dtype), x[:, :-1, :]], axis=1)
            xr = mu_r * x + (1.0 - mu_r) * x_prev
            xk = mu_k * x + (1.0 - mu_k) * x_prev
            r = jax.nn.sigmoid(jnp.einsum('btc,dc->btd', xr, W_r))
            k = jnp.einsum('btc,dc->btd', xk, W_k)
            k_act = jnp.square(jax.nn.relu(k))
            out = r * jnp.einsum('btc,dc->btd', k_act, W_v)
            new_state = x[:, -1, :]
            return (out, new_state)
        return _reference_tuple_inner(x, W_r, W_k, W_v, mu_r, mu_k)[0]
    x = L0_attn_x
    xn = _layernorm(x, axis=-1)
    x = x + _L0_attn_ref(xn, L0_attn_Wq, L0_attn_Wk, L0_attn_Wv, L0_attn_Wo, L0_attn_bo, L0_attn_Wf, L0_attn_bf) + _L0_ffn_ref(xn, L0_ffn_router_gate, L0_ffn_gate_w, L0_ffn_up_w, L0_ffn_down_w)
    xn = _layernorm(x, axis=-1)
    x = x + _L1_attn_ref(xn, L1_attn_w_kv_down, L1_attn_w_kv_up, L1_attn_w_q, L1_attn_w_out) + _L1_ffn_ref(xn, L1_ffn_wg, L1_ffn_W1, L1_ffn_b1, L1_ffn_W2, L1_ffn_b2)
    xn = _layernorm(x, axis=-1)
    x = x + _L2_attn_ref(xn, L2_attn_Wq, L2_attn_bq, L2_attn_Wk, L2_attn_bk) + _L2_ffn_ref(xn, L2_ffn_router_w, L2_ffn_w1, L2_ffn_b1, L2_ffn_w2, L2_ffn_b2)
    xn = _layernorm(x, axis=-1)
    x = x + _L3_attn_ref(xn, L3_attn_gain, L3_attn_w_q, L3_attn_w_k, L3_attn_w_v, L3_attn_w_o) + _L3_ffn_ref(xn, L3_ffn_W_r, L3_ffn_W_k, L3_ffn_W_v, L3_ffn_mu_r, L3_ffn_mu_k)
    return x

_drawn_inputs = setup_inputs


def setup_inputs(seed=0):
    import zlib

    import numpy as np

    out = dict(_drawn_inputs(seed))
    spreads = {'L1_ffn_b1': (0.0, 0.8),
     'L1_ffn_b2': (0.0, 0.409),
     'L2_ffn_b1': (0.0, 0.8),
     'L2_ffn_b2': (0.0, 0.428)}
    factors = {'L0_attn_bf': 34.983,
     'L0_ffn_router_gate': 7.343,
     'L0_ffn_gate_w': 6.472,
     'L0_ffn_up_w': 6.451,
     'L0_ffn_down_w': 6.453,
     'L1_attn_w_q': 8.0,
     'L1_ffn_wg': 2.861,
     'L1_ffn_W1': 6.021,
     'L1_ffn_W2': 5.346,
     'L2_attn_bq': 200.0,
     'L2_attn_bk': 18.849,
     'L2_ffn_router_w': 2.887,
     'L2_ffn_w1': 5.907,
     'L2_ffn_w2': 5.424,
     'L3_ffn_W_r': 17.612,
     'L3_ffn_mu_r': 35.352,
     'L3_ffn_mu_k': 3.608,
     'L0_attn_Wq': 3.719,
     'L0_attn_Wk': 3.64,
     'L0_attn_Wf': 3.531}
    for name, (base, spread) in spreads.items():
        noise = np.random.default_rng([zlib.crc32(name.encode()), seed]).standard_normal(out[name].shape)
        drawn = base * np.exp(spread * noise) if base else spread * noise
        out[name] = jnp.asarray(drawn.astype(out[name].dtype))
    for name, factor in factors.items():
        out[name] = (out[name] * factor).astype(out[name].dtype)
    return out
```

```python
from contextlib import ExitStack, contextmanager

import numpy as np
import concourse.bass as bass
from concourse import mybir

ALU = mybir.AluOpType
ACT = mybir.ActivationFunctionType
AX = mybir.AxisListType
F32 = mybir.dt.float32
BF16 = mybir.dt.bfloat16
I32 = mybir.dt.int32

P = 128
BATCHES = 8
SEQ = 256
D = 128
TOKENS = BATCHES * SEQ
TILES = TOKENS // P
HEADS = 16
EXPERTS = 8
FF = 512
FCH = FF // P
NEG = -1e30
LN_EPS = 1e-5
PAD_SLOT = 1 << 16
LAST_LAYER = 4

FEAT = 64
PAIRS = HEADS // 2
HS = 64
CAP0 = int(1.25 * ((TOKENS * 2 + EXPERTS - 1) // EXPERTS))
CAP1 = int(TOKENS / EXPERTS * 1.25) + 1
CAP2 = int(np.ceil(1.5 * TOKENS / EXPERTS))
ROWS0, ROWS1, ROWS2 = 128, 107, 128
GATE_BITS = 30


@contextmanager
def phase(nc, B, stage, names):
    handles = {n: nc.alloc_semaphore(f"{stage}_{n}") for n in names.split()}
    if B.used_semaphores:
        nc.clear_and_free_semaphores(B.used_semaphores)
    B.used_semaphores = list(handles.values())
    with nc.Block() as block:
        yield block, handles


def per_tile(ap, n):
    return ap.unsqueeze(2).to_broadcast([ap.shape[0], ap.shape[1], n])


def columns(vector):
    return vector.rearrange("(p a) -> p a", a=1)


def row_on_all(vector, n=P):
    return vector.rearrange("(a d) -> a d", a=1).broadcast_to([n, vector.shape[0]])


def setup(nc, I, B):
    with phase(nc, B, "setup", "x_in w_in zeroed rows_zero made ints wf_ready feat_psum feat_sbuf wt_psum wt_sbuf const") as (block, s):

        @block.sync
        def _(sp):
            sp.dma_start(B.x_res[:, :, :], I["L0_attn_x"].rearrange("b (t p) d -> p (b t) d", p=P)).then_inc(s["x_in"], 16)
            for dst, src in ((B.wq0, I["L0_attn_Wq"]), (B.wk0, I["L0_attn_Wk"]), (B.wv0, I["L0_attn_Wv"]), (B.wo0, I["L0_attn_Wo"])):
                sp.dma_start(dst[:, :], src).then_inc(s["w_in"], 16)
            for half in range(2):
                sp.dma_start(B.bf_col[half * FEAT:(half + 1) * FEAT, :], columns(I["L0_attn_bf"])).then_inc(s["w_in"], 16)
            sp.dma_start(B.bf_row[:, :], row_on_all(I["L0_attn_bf"])).then_inc(s["w_in"], 16)
            sp.dma_start(B.bo_row[:, :], row_on_all(I["L0_attn_bo"])).then_inc(s["w_in"], 16)
            sp.dma_start(B.router[:, 0, :], I["L0_ffn_router_gate"]).then_inc(s["w_in"], 16)
            sp.dma_start(B.router[:, 1, :], I["L1_ffn_wg"]).then_inc(s["w_in"], 16)
            sp.dma_start(B.router[:, 2, :], I["L2_ffn_router_w"].rearrange("e d -> d e"),
                         allow_slow_non_contiguous=True).then_inc(s["w_in"], 16)
            sp.wait_ge(s["zeroed"], 2)
            for h in range(HEADS):
                sp.dma_start(B.wf_diag[8 * h:8 * h + 8, h * FEAT:(h + 1) * FEAT], I["L0_attn_Wf"]).then_inc(s["wf_ready"], 16)
            sp.wait_ge(s["x_in"], 16)
            sp.wait_ge(s["w_in"], 16 * 11)

        @block.gpsimd
        def _(pool):
            nc.gpsimd.memset(B.zeros[:, :], 0.0).then_inc(s["zeroed"], 1)
            nc.gpsimd.memset(B.wf_diag[:, :], 0.0).then_inc(s["zeroed"], 1)
            nc.gpsimd.memset(B.ident[:, :], 0.0).then_inc(s["made"], 1)
            nc.gpsimd.memset(B.ones[:, :], 1.0).then_inc(s["made"], 1)
            nc.gpsimd.memset(B.ident_b[:, :], 0.0).then_inc(s["made"], 1)
            nc.gpsimd.memset(B.causal_b[:, :], 0.0).then_inc(s["made"], 1)
            pool.wait_ge(s["made"], 4)
            for m in (B.ident, B.ident_b):
                nc.gpsimd.affine_select(out=m[:, :], in_=m[:, :], compare_op=ALU.not_equal, fill=1.0, base=0,
                                        pattern=[[-1, P]], channel_multiplier=1).then_inc(s["made"], 1)
            nc.gpsimd.affine_select(out=B.causal_b[:, :], in_=B.causal_b[:, :], compare_op=ALU.is_ge, fill=NEG, base=0,
                                    pattern=[[-1, P]], channel_multiplier=1).then_inc(s["made"], 1)
            v = B.same_head[:, :].rearrange("p (h j) -> p h j", j=8)
            ones = B.ones[:, :].rearrange("p (h j) -> p h j", j=8)
            nc.gpsimd.affine_select(out=v, in_=ones, compare_op=ALU.is_ge, fill=0.0, base=0,
                                    pattern=[[-8, HEADS], [0, 8]], channel_multiplier=1).then_inc(s["made"], 1)
            pool.wait_ge(s["made"], 8)
            nc.gpsimd.affine_select(out=v, in_=v, compare_op=ALU.is_ge, fill=0.0, base=7,
                                    pattern=[[8, HEADS], [0, 8]], channel_multiplier=-1).then_inc(s["made"], 1)
            pool.wait_ge(s["made"], 9)
            nc.gpsimd.tensor_copy(B.head_mask[:, :], v[:, :, 0]).then_inc(s["made"], 1)
            nc.gpsimd.iota(B.expert_m8[:, :, :], pattern=[[0, TILES], [1, EXPERTS]], base=-EXPERTS, channel_multiplier=0,
                           allow_small_or_imprecise_dtypes=True).then_inc(s["ints"], 1)
            nc.gpsimd.iota(B.int_a[:, :], pattern=[[1, P]], base=P, channel_multiplier=-1).then_inc(s["ints"], 1)
            nc.gpsimd.iota(B.int_b[:, :], pattern=[[0, 1]], base=0, channel_multiplier=1).then_inc(s["ints"], 1)
            for n in range(GATE_BITS):
                nc.gpsimd.memset(B.gate_bits[:, n:n + 1], 1 << (GATE_BITS - 1 - n)).then_inc(s["ints"], 1)
            nc.gpsimd.memset(B.va0[:, :, :, 8:9], 1.0).then_inc(s["ints"], 1)
            nc.gpsimd.memset(B.v_nat[:, :, :, HS:HS + 1], 1.0).then_inc(s["ints"], 1)
            nc.gpsimd.memset(B.kv0[:, :, :], 0.0).then_inc(s["ints"], 1)
            nc.gpsimd.memset(B.half_neg[:, :], -0.5).then_inc(s["ints"], 1)
            pool.wait_ge(s["const"], 3)
            nc.gpsimd.affine_select(out=B.low_expert[:, :], in_=B.same_expert[:, :], compare_op=ALU.is_gt, fill=0.0,
                                    base=0, pattern=[[1, P]], channel_multiplier=-1).then_inc(s["ints"], 1)

        @block.vector
        def _(dve):
            dve.wait_ge(s["ints"], 3 + GATE_BITS)
            nc.vector.tensor_scalar(B.int_a[:, :], B.int_a[:, :], 7, None, ALU.bitwise_and).then_inc(s["const"], 1)
            nc.vector.tensor_scalar(B.int_b[:, :], B.int_b[:, :], 7, None, ALU.bitwise_and).then_inc(s["const"], 1)
            dve.wait_ge(s["const"], 2)
            nc.vector.tensor_scalar(B.same_expert[:, :], B.int_a[:, :], 0.0, None, ALU.is_equal).then_inc(s["const"], 1)
            nc.vector.tensor_copy(B.own_expert[:, :], B.int_b[:, :]).then_inc(s["const"], 1)
            nc.vector.tensor_copy(B.gate_bits_f[:, :], B.gate_bits[:, :]).then_inc(s["const"], 1)
            dve.wait_ge(s["made"], 9)
            nc.vector.tensor_scalar(B.not_same_head[:, :], B.same_head[:, :], -1.0, -NEG, ALU.add, ALU.mult).then_inc(s["const"], 1)
            for n in range(4):
                dve.wait_ge(s["feat_psum"], n + 1)
                w, half = (B.wqf, B.wkf)[n // 2], n % 2
                nc.vector.tensor_copy(w[:, half * 512:half * 512 + 512], B.ps[:, n % 2, :]).then_inc(s["feat_sbuf"], 1)

        @block.scalar
        def _(act):
            act.wait_ge(s["zeroed"], 1)
            for rows, cap, parts in ((B.rows0, CAP0, 4), (B.rows1, CAP1, 2), (B.rows2, CAP2, 2)):
                n = EXPERTS * cap * D // P // parts
                flat = rows.rearrange("r d -> (r d)").rearrange("(p a) -> p a", p=P)
                for k in range(parts):
                    act.dma_start(flat[:, k * n:(k + 1) * n], B.zeros[:, 0:n]).then_inc(s["rows_zero"], 16)
            act.wait_ge(s["wt_psum"], 2)
            nc.scalar.activation(B.wqt[:, :, :], B.ps[:, 2, 0:256].rearrange("p (a b) -> p a b", a=2),
                                 ACT.Copy).then_inc(s["wt_sbuf"], 1)
            act.wait_ge(s["rows_zero"], 16 * 8)

        @block.tensor
        def _(pe):
            pe.wait_ge(s["w_in"], 16 * 11)
            pe.wait_ge(s["made"], 5)
            for n, w in enumerate((B.wq0, B.wk0)):
                nc.tensor.transpose(B.ps[:, 2, n * P:(n + 1) * P], w[:, :], B.ident[:, :]).then_inc(s["wt_psum"], 1)
            pe.wait_ge(s["wt_sbuf"], 1)
            pe.wait_ge(s["wf_ready"], 16 * HEADS)
            for n in range(4):
                if n >= 2:
                    pe.wait_ge(s["feat_sbuf"], n - 1)
                nc.tensor.matmul(B.ps[:, n % 2, :], B.wqt[:, n // 2, :], B.wf_diag[:, (n % 2) * 512:(n % 2) * 512 + 512],
                                 start=True, stop=True).then_inc(s["feat_psum"], 1)


def norm_and_route(nc, B, layer, cap):
    ps_t, ps_log, ps_te, ps_col = B.ps[:, 0:2, :], B.ps[:, 2, 0:P], B.ps[:, 3, 0:P], B.ps[:, 4, :]
    ps_te2 = B.ps[:, 5, 0:P]
    with phase(nc, B, f"route{layer}", "link centred squared var rstd xn xt_psum xt logits shifted exp onehot te_psum counted "
                   "total loop_cnt loop_tot slots_te slots_tok") as (block, s):
        GROUPS, PER = 4, TILES // 4

        @block.scalar
        def _(act):
            def transposed(g):
                act.wait_ge(s["xt_psum"], g + 1)
                nc.scalar.activation(B.xn_t[:, g * 512:(g + 1) * 512], ps_t[:, g % 2, :], ACT.Copy).then_inc(s["xt"], 1)

            for g in range(GROUPS):
                act.wait_ge(s["centred"], g + 1)
                if g >= 2:
                    act.wait_ge(s["var"], g - 1)
                nc.scalar.activation(B.squares[:, g % 2, :], B.xn[:, g * PER:(g + 1) * PER, :].rearrange("p t d -> p (t d)"),
                                     ACT.Square).then_inc(s["squared"], 1)
                if g >= 1:
                    transposed(g - 1)
            transposed(GROUPS - 1)
            if layer < 3:
                act.wait_ge(s["shifted"], 1)
                nc.scalar.activation(B.r_exp[:, :, :], B.r_a[:, :, :], ACT.Exp).then_inc(s["exp"], 1)

        @block.gpsimd
        def _(pool):
            for g in range(GROUPS):
                pool.wait_ge(s["var"], g + 1)
                t = slice(g * PER, (g + 1) * PER)
                nc.gpsimd.tensor_tensor(B.rstd[:, t], B.variance[:, t], B.half_neg[:, 0:PER], ALU.pow).then_inc(s["rstd"], 1)

        @block.tensor
        def _(pe):
            def logits(g):
                pe.wait_ge(s["xt"], g + 1)
                for t in range(g * PER, (g + 1) * PER):
                    last = nc.tensor.matmul(ps_log[:, t * EXPERTS:(t + 1) * EXPERTS], B.xn_t[:, t * P:(t + 1) * P],
                                            B.router[:, layer, :], start=True, stop=True)
                last.then_inc(s["logits"], 1)

            for g in range(GROUPS):
                pe.wait_ge(s["xn"], g + 1)
                if g >= 2:
                    pe.wait_ge(s["xt"], g - 1)
                for j in range(PER):
                    last = nc.tensor.transpose(ps_t[:, g % 2, j * P:(j + 1) * P], B.xn[:, g * PER + j, :], B.ident[:, :])
                last.then_inc(s["xt_psum"], 1)
                if layer < 3 and g >= 1:
                    logits(g - 1)
            if layer == 3:
                return
            logits(GROUPS - 1)
            pe.wait_ge(s["onehot"], 1)
            nc.tensor.transpose(ps_te, B.r_choice[:, :, :].rearrange("p t e -> p (t e)"), B.ident[:, :]).then_inc(s["te_psum"], 1)
            if layer == 0:
                with pe.Fori(0, GATE_BITS) as n:
                    pe.wait_ge(s["loop_cnt"], n + 1)
                    nc.tensor.matmul(ps_col[:, 0:1], B.same_expert[:, :], B.c_count[:, :], start=True,
                                     stop=True).then_inc(s["loop_tot"], 1)
                pe.wait_ge(s["counted"], 1)
                nc.tensor.matmul(ps_col[:, 1:2], B.same_expert[:, :], B.c_above[:, :], start=True, stop=True).then_inc(s["total"], 1)
                pe.wait_ge(s["counted"], 2)
                nc.tensor.matmul(ps_col[:, 2:3], B.low_expert[:, :], B.c_ties[:, :], start=True, stop=True).then_inc(s["total"], 1)
            k = 2 if layer == 0 else 0
            pe.wait_ge(s["counted"], k + 1)
            nc.tensor.matmul(ps_col[:, 3:4], B.low_expert[:, :], B.c_kept[:, :], start=True, stop=True).then_inc(s["total"], 1)
            pe.wait_ge(s["slots_te"], 1)
            nc.tensor.transpose(ps_te2, B.te_slot[:, :], B.ident[:, :]).then_inc(s["slots_tok"], 1)

        @block.vector
        def _(dve):
            n_link = [0]

            def link(ins):
                n_link[0] += 1
                ins.then_inc(s["link"], 1)
                dve.wait_ge(s["link"], n_link[0])

            def group(g):
                return slice(g * PER, (g + 1) * PER)

            def centre(g):
                t = group(g)
                link(nc.vector.tensor_reduce(B.mean[:, t], B.x_res[:, t, :], AX.X, ALU.add))
                link(nc.vector.tensor_scalar(B.mean[:, t], B.mean[:, t], -1.0 / D, None, ALU.mult))
                nc.vector.tensor_tensor(B.xn[:, t, :], B.x_res[:, t, :], per_tile(B.mean[:, t], D), ALU.add).then_inc(s["centred"], 1)

            def spread(g):
                t = group(g)
                dve.wait_ge(s["squared"], g + 1)
                link(nc.vector.tensor_reduce(B.variance[:, t], B.squares[:, g % 2, :].rearrange("p (t d) -> p t d", d=D),
                                             AX.X, ALU.add))
                nc.vector.tensor_scalar(B.variance[:, t], B.variance[:, t], 1.0 / D, LN_EPS, ALU.mult, ALU.add).then_inc(s["var"], 1)

            def scale(g):
                t = group(g)
                dve.wait_ge(s["rstd"], g + 1)
                nc.vector.tensor_tensor(B.xn[:, t, :], B.xn[:, t, :], per_tile(B.rstd[:, t], D), ALU.mult).then_inc(s["xn"], 1)

            for g in range(GROUPS + 2):
                if g < GROUPS:
                    centre(g)
                if 1 <= g <= GROUPS:
                    spread(g - 1)
                if g >= 2:
                    scale(g - 2)
            if layer == 3:
                return

            def first_largest(choice, best, among):
                link(nc.vector.tensor_reduce(best, among, AX.X, ALU.max))
                link(nc.vector.tensor_tensor(B.r_a[:, :, :], among, per_tile(best, EXPERTS), ALU.is_equal))
                link(nc.vector.tensor_tensor(B.r_a[:, :, :], B.r_a[:, :, :], B.expert_m8[:, :, :], ALU.mult))
                link(nc.vector.tensor_reduce(B.v_a[:, :], B.r_a[:, :, :], AX.X, ALU.min))
                link(nc.vector.tensor_tensor(choice, B.expert_m8[:, :, :], per_tile(B.v_a[:, :], EXPERTS), ALU.is_equal))

            dve.wait_ge(s["logits"], GROUPS)
            lg = ps_log.rearrange("p (t e) -> p t e", e=EXPERTS)
            link(nc.vector.tensor_reduce(B.v_a[:, :], lg, AX.X, ALU.max))
            nc.vector.tensor_tensor(B.r_a[:, :, :], lg, per_tile(B.v_a[:, :], EXPERTS), ALU.subtract).then_inc(s["shifted"], 1)
            dve.wait_ge(s["exp"], 1)
            link(nc.vector.tensor_reduce(B.v_a[:, :], B.r_exp[:, :, :], AX.X, ALU.add))
            link(nc.vector.reciprocal(B.v_b[:, :], B.v_a[:, :]))
            link(nc.vector.tensor_tensor(B.r_prob[:, :, :], B.r_exp[:, :, :], per_tile(B.v_b[:, :], EXPERTS), ALU.mult))
            first_largest(B.r_one[:, 0], B.gate[:, 0, :], B.r_prob[:, :, :])
            te, keep, junk = B.te_val, B.te_keep, B.te_junk
            if layer == 0:
                link(nc.vector.scalar_tensor_tensor(out=B.r_exp[:, :, :], in0=B.r_one[:, 0], scalar=-2.0, in1=B.r_prob[:, :, :],
                                                    op0=ALU.mult, op1=ALU.add))
                first_largest(B.r_one[:, 1], B.gate[:, 1, :], B.r_exp[:, :, :])
                link(nc.vector.tensor_tensor(B.v_a[:, :], B.gate[:, 0, :], B.gate[:, 1, :], ALU.add))
                link(nc.vector.tensor_scalar(B.v_a[:, :], B.v_a[:, :], 1e-9, None, ALU.add))
                link(nc.vector.reciprocal(B.v_b[:, :], B.v_a[:, :]))
                for k in range(2):
                    link(nc.vector.tensor_tensor(B.gate[:, k, :], B.gate[:, k, :], B.v_b[:, :], ALU.mult))
                link(nc.vector.tensor_tensor(B.r_a[:, :, :], B.r_one[:, 0], per_tile(B.gate[:, 0, :], EXPERTS), ALU.mult))
                link(nc.vector.tensor_tensor(B.r_choice[:, :, :], B.r_one[:, 1], per_tile(B.gate[:, 1, :], EXPERTS), ALU.mult))
                nc.vector.tensor_tensor(B.r_choice[:, :, :], B.r_choice[:, :, :], B.r_a[:, :, :], ALU.add).then_inc(s["onehot"], 1)
                dve.wait_ge(s["te_psum"], 1)
                link(nc.vector.tensor_copy(te[:, :], ps_te))
                link(nc.vector.memset(B.thr[:, :], 0))
                base = n_link[0]
                with dve.Fori(0, GATE_BITS) as n:
                    bit = bass.ds(n, 1)
                    nc.vector.tensor_tensor(B.thr_try[:, :], B.thr[:, :], B.gate_bits[:, bit], ALU.bitwise_or).then_inc(s["link"], 1)
                    dve.wait_ge(s["link"], base + 3 * n + 1)
                    nc.vector.tensor_scalar(junk[:, :], te[:, :], B.thr_try[:, :].bitcast(F32), None, ALU.is_ge, ALU.add,
                                            accum_out=B.c_count[:, :]).then_inc(s["loop_cnt"], 1)
                    dve.wait_ge(s["loop_tot"], n + 1)
                    nc.vector.tensor_scalar(B.thr_add[:, :], ps_col[:, 0:1], float(cap), B.gate_bits_f[:, bit], ALU.is_ge,
                                            ALU.mult).then_inc(s["link"], 1)
                    dve.wait_ge(s["link"], base + 3 * n + 2)
                    nc.vector.tensor_tensor(B.thr[:, :], B.thr[:, :], B.thr_add[:, :], ALU.bitwise_or).then_inc(s["link"], 1)
                    dve.wait_ge(s["link"], base + 3 * n + 3)
                n_link[0] = base + 3 * GATE_BITS
                thr = B.thr[:, :].bitcast(F32)
                nc.vector.tensor_scalar(keep[:, :], te[:, :], thr, None, ALU.is_gt, ALU.add,
                                        accum_out=B.c_above[:, :]).then_inc(s["counted"], 1)
                link(nc.vector.tensor_scalar(B.te_tie[:, :], te[:, :], thr, None, ALU.is_equal))
                link(nc.vector.scalar_tensor_tensor(out=B.te_tie[:, :], in0=te[:, :], scalar=0.0, in1=B.te_tie[:, :],
                                                    op0=ALU.is_gt, op1=ALU.mult))
                nc.vector.tensor_reduce(B.c_ties[:, :], B.te_tie[:, :], AX.X, ALU.add).then_inc(s["counted"], 1)
                dve.wait_ge(s["total"], 2)
                link(nc.vector.tensor_scalar(B.c_room[:, :], ps_col[:, 1:2], -1.0, float(cap), ALU.mult, ALU.add))
                link(nc.vector.tensor_copy(B.c_start[:, :], ps_col[:, 2:3]))
                link(nc.vector.tensor_tensor_scan(B.te_rank[:, :], B.ones[:, :], B.te_tie[:, :], B.c_start[:, :],
                                                  ALU.mult, ALU.add))
                link(nc.vector.scalar_tensor_tensor(out=B.te_tie[:, :], in0=B.te_rank[:, :], scalar=B.c_room[:, :],
                                                    in1=B.te_tie[:, :], op0=ALU.is_le, op1=ALU.mult))
                link(nc.vector.tensor_tensor(keep[:, :], keep[:, :], B.te_tie[:, :], ALU.add))
            else:
                link(nc.vector.tensor_copy(B.r_choice[:, :, :], B.r_one[:, 0]))
                nc.vector.memset(B.thr[:, :], 0).then_inc(s["onehot"], 1)
                dve.wait_ge(s["te_psum"], 1)
                link(nc.vector.tensor_copy(keep[:, :], ps_te))
            nc.vector.tensor_reduce(B.c_kept[:, :], keep[:, :], AX.X, ALU.add).then_inc(s["counted"], 1)
            dve.wait_ge(s["total"], 3 if layer == 0 else 1)
            link(nc.vector.tensor_copy(B.c_start[:, :], ps_col[:, 3:4]))
            link(nc.vector.tensor_tensor_scan(B.te_rank[:, :], B.ones[:, :], keep[:, :], B.c_start[:, :], ALU.mult, ALU.add))
            if layer > 0:
                link(nc.vector.scalar_tensor_tensor(out=keep[:, :], in0=B.te_rank[:, :], scalar=float(cap), in1=keep[:, :],
                                                    op0=ALU.is_le, op1=ALU.mult))
            link(nc.vector.tensor_scalar(B.c_room[:, :], B.own_expert[:, :], float(cap), None, ALU.mult))
            nc.vector.scalar_tensor_tensor(out=B.te_slot[:, :], in0=B.te_rank[:, :], scalar=B.c_room[:, :], in1=keep[:, :],
                                           op0=ALU.add, op1=ALU.mult).then_inc(s["slots_te"], 1)
            dve.wait_ge(s["slots_tok"], 1)
            for k in range(2 if layer == 0 else 1):
                link(nc.vector.tensor_tensor(B.r_a[:, :, :], ps_te2.rearrange("p (t e) -> p t e", e=EXPERTS), B.r_one[:, k], ALU.mult))
                link(nc.vector.tensor_reduce(B.v_a[:, :], B.r_a[:, :, :], AX.X, ALU.add))
                link(nc.vector.scalar_tensor_tensor(out=B.gate[:, k, :], in0=B.v_a[:, :], scalar=0.0, in1=B.gate[:, k, :],
                                                    op0=ALU.is_gt, op1=ALU.mult))
                link(nc.vector.tensor_scalar(B.v_b[:, :], B.v_a[:, :], 0.0, float(PAD_SLOT), ALU.is_equal, ALU.mult))
                link(nc.vector.scalar_tensor_tensor(out=B.to_slot[:, k, :], in0=B.v_a[:, :], scalar=-1.0, in1=B.v_b[:, :],
                                                    op0=ALU.add, op1=ALU.add))
                link(nc.vector.tensor_scalar(B.from_slot[:, k, :], B.v_a[:, :], -1.0, 0.0, ALU.add, ALU.max))


def scatter_rows(nc, pool, B, rows, choices, total, done):
    for k in range(choices):
        for t in range(TILES):
            nc.gpsimd.indirect_dma_start(rows, bass.IndirectOffsetOnAxis(ap=B.to_slot[:, k, t:t + 1], axis=0),
                                         B.xn[:, t, :], None, bounds_check=total - 1, oob_is_err=False).then_inc(done, 16)
    pool.wait_ge(done, 16 * choices * TILES)


def linear_attention(nc, I, B):
    names = ("link scattered x_staged q_psum q_sbuf k_psum k_bias k_relu v_psum v_sbuf kv_psum kv_sbuf num_psum num_sbuf "
             "t_psum t_sbuf o_psum added w_next")
    ps = B.ps
    with phase(nc, B, "linear", names) as (block, s):

        @block.gpsimd
        def _(pool):
            scatter_rows(nc, pool, B, B.rows0, 2, EXPERTS * CAP0, s["scattered"])

        @block.scalar
        def _(act):
            with act.Fori(0, BATCHES) as b:
                act.wait_ge(s["v_psum"], b)
                act.nop()
                nc.scalar.activation(B.x_b[:, 0:SEQ], B.xn_t[:, bass.ds(b * SEQ, SEQ)], ACT.Copy).then_inc(s["x_staged"], 1)
                for j in range(4):
                    act.wait_ge(s["q_psum"], 4 * b + j + 1)
                    nc.scalar.activation(B.qf[:, 2 * j:2 * j + 2, :].rearrange("p a b -> p (a b)"), ps[:, j % 2, :], ACT.Relu,
                                         bias=B.bf_col[:, :]).then_inc(s["q_sbuf"], 1)
                for j in range(4):
                    act.wait_ge(s["k_bias"], 4 * b + j + 1)
                    v = B.kf[:, j // 2, (j % 2) * 512:(j % 2) * 512 + 512]
                    nc.scalar.activation(v, v, ACT.Relu).then_inc(s["k_relu"], 1)
                act.wait_ge(s["t_psum"], b + 1)
                nc.scalar.activation(B.o_t[:, :, :].rearrange("p a b -> p (a b)"), ps[:, 7, 0:256], ACT.Copy).then_inc(s["t_sbuf"], 1)

        @block.tensor
        def _(pe):
            with pe.Fori(0, BATCHES) as b:
                pe.wait_ge(s["x_staged"], b + 1)
                for j in range(4):
                    if j >= 2:
                        pe.wait_ge(s["q_sbuf"], 4 * b + j - 1)
                    for i in range(2):
                        last = nc.tensor.matmul(ps[:, j % 2, i * SEQ:(i + 1) * SEQ], B.wqf[:, (2 * j + i) * P:(2 * j + i + 1) * P],
                                                B.x_b[:, 0:SEQ], start=True, stop=True)
                    last.then_inc(s["q_psum"], 1)
                for j in range(4):
                    if j >= 2:
                        pe.wait_ge(s["k_bias"], 4 * b + j - 1)
                    nc.tensor.matmul(ps[:, 2 + j % 2, :], B.x_b[:, (j // 2) * P:(j // 2 + 1) * P],
                                     B.wkf[:, (j % 2) * 512:(j % 2) * 512 + 512], start=True, stop=True).then_inc(s["k_psum"], 1)
                for t in range(2):
                    last = nc.tensor.matmul(ps[:, 4, t * P:(t + 1) * P], B.x_b[:, t * P:(t + 1) * P], B.wv0[:, :],
                                            start=True, stop=True)
                last.then_inc(s["v_psum"], 1)
                pe.wait_ge(s["v_sbuf"], b + 1)
                pe.wait_ge(s["k_relu"], 4 * b + 4)
                for p in range(PAIRS):
                    for t in range(2):
                        last = nc.tensor.matmul(ps[:, 5, 18 * p:18 * p + 18], B.kf[:, t, p * P:(p + 1) * P],
                                                B.va0[:, t, 2 * p:2 * p + 2, :].rearrange("p a b -> p (a b)"),
                                                start=t == 0, stop=t == 1)
                last.then_inc(s["kv_psum"], 1)
                pe.wait_ge(s["kv_sbuf"], 2 * b + 2)
                pe.wait_ge(s["q_sbuf"], 4 * b + 4)
                for t in range(2):
                    for p in range(PAIRS):
                        last = nc.tensor.matmul(ps[:, 6, t * 144 + 18 * p:t * 144 + 18 * p + 18], B.qf[:, p, t * P:(t + 1) * P],
                                                B.kv0[:, p, :], start=True, stop=True)
                last.then_inc(s["num_psum"], 1)
                pe.wait_ge(s["num_sbuf"], b + 1)
                for t in range(2):
                    last = nc.tensor.transpose(ps[:, 7, t * P:(t + 1) * P], B.o_nat[:, t, :], B.ident[:, :])
                last.then_inc(s["t_psum"], 1)
                pe.wait_ge(s["t_sbuf"], b + 1)
                for t in range(2):
                    last = nc.tensor.matmul(ps[:, 7, 256 + t * P:256 + (t + 1) * P], B.o_t[:, t, :], B.wo0[:, :],
                                            start=True, stop=True)
                last.then_inc(s["o_psum"], 1)

        @block.vector
        def _(dve):
            with dve.Fori(0, BATCHES) as b:
                for j in range(4):
                    dve.wait_ge(s["k_psum"], 4 * b + j + 1)
                    nc.vector.tensor_tensor(B.kf[:, j // 2, (j % 2) * 512:(j % 2) * 512 + 512].rearrange("p (h f) -> p h f", f=FEAT),
                                            ps[:, 2 + j % 2, :].rearrange("p (h f) -> p h f", f=FEAT),
                                            B.bf_row[:, :].unsqueeze(1).to_broadcast([P, 8, FEAT]), ALU.add).then_inc(s["k_bias"], 1)
                dve.wait_ge(s["v_psum"], b + 1)
                nc.vector.tensor_copy(B.va0[:, :, :, 0:8], ps[:, 4, 0:256].rearrange("p (t h d) -> p t h d", t=2, d=8)).then_inc(s["v_sbuf"], 1)
                dve.wait_ge(s["kv_psum"], b + 1)
                kv = ps[:, 5, 0:144].rearrange("p (a c) -> p a c", c=18)
                nc.vector.tensor_copy(B.kv0[0:64, :, 0:9], kv[0:64, :, 0:9]).then_inc(s["kv_sbuf"], 1)
                nc.vector.tensor_copy(B.kv0[64:128, :, 9:18], kv[64:128, :, 9:18]).then_inc(s["kv_sbuf"], 1)
                dve.wait_ge(s["num_psum"], b + 1)
                num = ps[:, 6, 0:288].rearrange("p (th c) -> p th c", c=9)
                nc.vector.tensor_scalar(B.den[:, :], num[:, :, 8], 1e-6, None, ALU.max).then_inc(s["link"], 1)
                dve.wait_ge(s["link"], 2 * b + 1)
                nc.vector.reciprocal(B.den[:, :], B.den[:, :]).then_inc(s["link"], 1)
                dve.wait_ge(s["link"], 2 * b + 2)
                nc.vector.tensor_tensor(B.o_nat[:, :, :].rearrange("p t (h d) -> p (t h) d", d=8), num[:, :, 0:8],
                                        per_tile(B.den[:, :], 8), ALU.mult).then_inc(s["num_sbuf"], 1)
                dve.wait_ge(s["o_psum"], b + 1)
                xb = B.x_res[:, bass.ds(2 * b, 2), :]
                nc.vector.tensor_tensor(xb, xb, ps[:, 7, 256:512].rearrange("p (t d) -> p t d", d=D), ALU.add).then_inc(s["added"], 1)

        @block.sync
        def _(sp):
            for dst, src in ((B.w_kv_down[:, :], I["L1_attn_w_kv_down"]), (B.w_q[:, :], I["L1_attn_w_q"]),
                             (B.w_kv_up[:, :], I["L1_attn_w_kv_up"]), (B.w_out[:, :, :], I["L1_attn_w_out"].rearrange("(c p) d -> p c d", p=P))):
                sp.dma_start(dst, src).then_inc(s["w_next"], 16)
            sp.wait_ge(s["w_next"], 16 * 4)


def latent_attention(nc, I, B):
    ps = B.ps
    G = HEADS // 2
    PIECES_A, PIECES_V = 9, 4
    names = ("link scattered x_staged proj_psum proj_a proj_v s_psum maxed exped p_psum p_sbuf y_psum y_norm yt_psum yt_sbuf "
             "o_psum added w_next")
    with phase(nc, B, "latent", names) as (block, s):

        def score_bank(g, hh):
            return (g % 2) * 2 + hh

        @block.sync
        def _(sp):
            loads = [(B.wq2[:, :], I["L2_attn_Wq"]), (B.wk2[:, :], I["L2_attn_Wk"]), (B.bq2[:, :], columns(I["L2_attn_bq"])),
                     (B.bk2[:, :], columns(I["L2_attn_bk"])), (B.bk2_row[:, :], row_on_all(I["L2_attn_bk"])),
                     (B.gain[:, :], row_on_all(I["L3_attn_gain"]))]
            loads += [(B.w3[:, n, :], w) for n, w in enumerate((I["L3_attn_w_q"], I["L3_attn_w_k"], I["L3_attn_w_v"], I["L3_attn_w_o"],
                                                                I["L3_ffn_W_r"], I["L3_ffn_W_k"], I["L3_ffn_W_v"]))]
            loads += [(B.mu[:, 0:1], columns(I["L3_ffn_mu_r"])), (B.mu[:, 1:2], columns(I["L3_ffn_mu_k"]))]
            for dst, src in loads:
                sp.dma_start(dst, src).then_inc(s["w_next"], 16)
            sp.wait_ge(s["w_next"], 16 * len(loads))

        @block.gpsimd
        def _(pool):
            scatter_rows(nc, pool, B, B.rows1, 1, EXPERTS * CAP1, s["scattered"])

        @block.tensor
        def _(pe):
            def projection(b, piece, parts):
                if piece >= 4:
                    pe.wait_ge(s["proj_a"], PIECES_A * b + piece - 3)
                bank = piece % 4
                for lo, hi, w, x in parts:
                    last = nc.tensor.matmul(ps[:, bank, lo:hi], w, x, start=True, stop=True)
                last.then_inc(s["proj_psum"], 1)

            def scores(b, g):
                n = G * b + g
                if g >= 2:
                    pe.wait_ge(s["exped"], n - 1)
                for hh in range(2):
                    h = 2 * g + hh
                    rows = slice(HS * hh, HS * hh + HS)
                    bank = ps[:, score_bank(g, hh), :]
                    for q, lo, hi in ((0, 0, P), (1, P, 3 * P)):
                        nc.tensor.matmul(bank[:, lo:hi], B.q_t[rows, g, q * P:(q + 1) * P], B.k_t[rows, g, 0:hi - lo],
                                         start=True, stop=False)
                        last = nc.tensor.matmul(bank[:, hi - P:hi], B.ident_b[:, :], B.causal_b[:, :], start=False, stop=True)
                last.then_inc(s["s_psum"], 1)

            def transposes(b, g):
                n = G * b + g
                pe.wait_ge(s["exped"], n + 1)
                pe.wait_ge(s["p_sbuf"], n)
                for hh in range(2):
                    for j in range(3):
                        last = nc.tensor.transpose(ps[:, 4 + hh, j * P:(j + 1) * P], B.p_nat[:, g % 2, hh, j * P:(j + 1) * P],
                                                   B.ident[:, :])
                last.then_inc(s["p_psum"], 1)

            def values(b, g):
                n = G * b + g
                pe.wait_ge(s["p_sbuf"], n + 1)
                if g >= 2:
                    pe.wait_ge(s["y_norm"], n - 1)
                for hh in range(2):
                    h = 2 * g + hh
                    y = ps[:, 6 + g % 2, :]
                    lo = 65 * hh
                    nc.tensor.matmul(y[:, lo:lo + 65], B.p_t[:, g % 2, hh, 0:P], B.v_nat[:, 0, h, :], start=True, stop=True)
                    lo += 130
                    nc.tensor.matmul(y[:, lo:lo + 65], B.p_t[:, g % 2, hh, P:2 * P], B.v_nat[:, 0, h, :], start=True, stop=False)
                    last = nc.tensor.matmul(y[:, lo:lo + 65], B.p_t[:, g % 2, hh, 2 * P:3 * P], B.v_nat[:, 1, h, :],
                                            start=False, stop=True)
                last.then_inc(s["y_psum"], 1)

            with pe.Fori(0, BATCHES) as b:
                pe.wait_ge(s["x_staged"], b + 1)
                pe.wait_ge(s["yt_sbuf"], 4 * b)
                x = B.x_b[:, 0:SEQ]
                projection(b, 0, [(0, SEQ, B.w_kv_down[:, :], x)])
                for c in range(4):
                    projection(b, 1 + c, [(i * SEQ, (i + 1) * SEQ, B.w_q[:, (2 * c + i) * P:(2 * c + i + 1) * P], x)
                                          for i in range(2)])
                pe.wait_ge(s["proj_a"], PIECES_A * b + 1)
                for c in range(4):
                    projection(b, 5 + c, [(i * SEQ, (i + 1) * SEQ, B.w_kv_up[:, (2 * c + i) * P:(2 * c + i + 1) * P], B.latent[:, :])
                                          for i in range(2)])
                for c in range(4):
                    t, half = c // 2, c % 2
                    projection(b, 9 + c, [(0, 512, B.latent[:, t * P:(t + 1) * P],
                                           B.w_kv_up[:, HEADS * HS + 512 * half:HEADS * HS + 512 * half + 512])])
                pe.wait_ge(s["proj_a"], PIECES_A * (b + 1))
                pe.wait_ge(s["proj_v"], PIECES_V * (b + 1))
                pe.wait_ge(s["added"], b)
                for g in range(G + 2):
                    if g < G:
                        scores(b, g)
                    if 1 <= g <= G:
                        transposes(b, g - 1)
                    if g >= 2:
                        values(b, g - 2)
                pe.wait_ge(s["y_norm"], G * (b + 1))
                for q in range(4):
                    t, half = q // 2, q % 2
                    for c in range(4):
                        last = nc.tensor.transpose(ps[:, q, c * P:(c + 1) * P],
                                                   B.y_nat[:, t, (4 * half + c) * P:(4 * half + c + 1) * P], B.ident[:, :])
                    last.then_inc(s["yt_psum"], 1)
                for t in range(2):
                    pe.wait_ge(s["yt_sbuf"], 4 * b + 2 * t + 2)
                    for c in range(8):
                        last = nc.tensor.matmul(ps[:, 6, t * P:(t + 1) * P], B.y_t[:, t, c, :], B.w_out[:, c, :],
                                                start=c == 0, stop=c == 7)
                last.then_inc(s["o_psum"], 1)

        @block.scalar
        def _(act):
            with act.Fori(0, BATCHES) as b:
                act.wait_ge(s["proj_psum"], 13 * b)
                act.nop()
                nc.scalar.activation(B.x_b[:, 0:SEQ], B.xn_t[:, bass.ds(b * SEQ, SEQ)], ACT.Copy).then_inc(s["x_staged"], 1)
                act.wait_ge(s["proj_psum"], 13 * b + 1)
                nc.scalar.activation(B.latent[:, :], ps[:, 0, 0:SEQ], ACT.Copy).then_inc(s["proj_a"], 1)
                for piece in range(1, 9):
                    act.wait_ge(s["proj_psum"], 13 * b + piece + 1)
                    dst, c, scale = (B.q_t, piece - 1, HS ** -0.5) if piece < 5 else (B.k_t, piece - 5, 1.0)
                    nc.scalar.activation(dst[:, 2 * c:2 * c + 2, :].rearrange("p a b -> p (a b)"), ps[:, piece % 4, :], ACT.Copy,
                                         scale=scale).then_inc(s["proj_a"], 1)
                for g in range(G):
                    n = G * b + g
                    act.wait_ge(s["maxed"], n + 1)
                    if g >= 2:
                        act.wait_ge(s["p_psum"], n - 1)
                    for hh in range(2):
                        for q, lo, hi in ((0, 0, P), (1, P, 3 * P)):
                            last = nc.scalar.activation(B.p_nat[:, g % 2, hh, lo:hi], ps[:, score_bank(g, hh), lo:hi], ACT.Exp,
                                                        bias=B.neg_max[:, g % 2, q, hh:hh + 1])
                    last.then_inc(s["exped"], 1)
                for q in range(4):
                    t, half = q // 2, q % 2
                    act.wait_ge(s["yt_psum"], 4 * b + q + 1)
                    nc.scalar.activation(B.y_t[:, t, 4 * half:4 * half + 4, :].rearrange("p a b -> p (a b)"), ps[:, q, :],
                                         ACT.Copy).then_inc(s["yt_sbuf"], 1)

        @block.vector
        def _(dve):
            with dve.Fori(0, BATCHES) as b:
                for c in range(4):
                    t, half = c // 2, c % 2
                    dve.wait_ge(s["proj_psum"], 13 * b + 10 + c)
                    nc.vector.tensor_copy(B.v_nat[:, t, 8 * half:8 * half + 8, 0:HS],
                                          ps[:, (9 + c) % 4, :].rearrange("p (h d) -> p h d", d=HS)).then_inc(s["proj_v"], 1)
                for g in range(G + 2):
                    if g < G:
                        n = G * b + g
                        dve.wait_ge(s["s_psum"], n + 1)
                        bank = ps[:, score_bank(g, 0):score_bank(g, 0) + 2, :]
                        nc.vector.tensor_reduce(B.neg_max[:, g % 2, 0, :], bank[:, :, 0:P], AX.X, ALU.max, negate=True)
                        nc.vector.tensor_reduce(B.neg_max[:, g % 2, 1, :], bank[:, :, P:3 * P], AX.X, ALU.max,
                                                negate=True).then_inc(s["maxed"], 1)
                    if 1 <= g <= G:
                        n = G * b + g - 1
                        dve.wait_ge(s["p_psum"], n + 1)
                        if g - 1 >= 2:
                            dve.wait_ge(s["y_psum"], n - 1)
                        nc.vector.tensor_copy(B.p_t[:, (g - 1) % 2, :, 0:3 * P], ps[:, 4:6, 0:3 * P]).then_inc(s["p_sbuf"], 1)
                    if g >= 2:
                        n = G * b + g - 2
                        dve.wait_ge(s["y_psum"], n + 1)
                        y = ps[:, 6 + g % 2, 0:260].rearrange("p (t h d) -> p t h d", t=2, d=65)
                        dve.wait_ge(s["y_norm"], n)
                        nc.vector.reciprocal(B.rden[:, :, :], y[:, :, :, HS]).then_inc(s["link"], 1)
                        dve.wait_ge(s["link"], n + 1)
                        nc.vector.tensor_tensor(B.y_nat[:, :, :].rearrange("p t (h d) -> p t h d", d=HS)[:, :, 2 * g - 4:2 * g - 2, :],
                                                y[:, :, :, 0:HS], B.rden[:, :, :].unsqueeze(3).to_broadcast([P, 2, 2, HS]),
                                                ALU.mult).then_inc(s["y_norm"], 1)
                dve.wait_ge(s["o_psum"], b + 1)
                xb = B.x_res[:, bass.ds(2 * b, 2), :]
                nc.vector.tensor_tensor(xb, xb, ps[:, 6, 0:SEQ].rearrange("p (t d) -> p t d", d=D), ALU.add).then_inc(s["added"], 1)


def small_head_attention(nc, B):
    ps = B.ps
    G = HEADS // 2
    SCALE = float(D) ** -0.5
    names = "link scattered x_staged proj_psum qk_sbuf v_sbuf wide s_psum maxed exped p_psum p_sbuf y_psum y_norm added scaled"
    with phase(nc, B, "small", names) as (block, s):

        def score_bank(g, hh):
            return (g % 2) * 2 + hh

        @block.gpsimd
        def _(pool):
            scatter_rows(nc, pool, B, B.rows2, 1, EXPERTS * CAP2, s["scattered"])

        @block.tensor
        def _(pe):
            def scores(b, g):
                n = G * b + g
                if g >= 2:
                    pe.wait_ge(s["exped"], n - 1)
                pe.wait_ge(s["wide"], n + 1)
                for hh in range(2):
                    for q in range(2):
                        last = nc.tensor.matmul(ps[:, score_bank(g, hh), q * SEQ:(q + 1) * SEQ],
                                                B.q_wide[:, 2 * g + hh, q * P:(q + 1) * P], B.k2_t[:, :], start=True, stop=True)
                last.then_inc(s["s_psum"], 1)

            def transposes(b, g):
                n = G * b + g
                pe.wait_ge(s["exped"], n + 1)
                pe.wait_ge(s["p_sbuf"], n)
                for hh in range(2):
                    for j in range(4):
                        last = nc.tensor.transpose(ps[:, 4 + hh, j * P:(j + 1) * P], B.p_nat[:, g % 2, hh, j * P:(j + 1) * P],
                                                   B.ident[:, :])
                last.then_inc(s["p_psum"], 1)

            def values(b, g):
                n = G * b + g
                pe.wait_ge(s["p_sbuf"], n + 1)
                if g >= 2:
                    pe.wait_ge(s["y_norm"], n - 1)
                for q in range(2):
                    for hh in range(2):
                        lo = 18 * q + 9 * hh
                        for k in range(2):
                            last = nc.tensor.matmul(ps[:, 6 + g % 2, lo:lo + 9], B.p_t[:, g % 2, hh, (2 * q + k) * P:(2 * q + k + 1) * P],
                                                    B.va0[:, k, 2 * g + hh, :], start=k == 0, stop=k == 1)
                last.then_inc(s["y_psum"], 1)

            with pe.Fori(0, BATCHES) as b:
                pe.wait_ge(s["x_staged"], b + 1)
                pe.wait_ge(s["y_norm"], G * b)
                for n, w in enumerate((B.wq2, B.wk2)):
                    nc.tensor.matmul(ps[:, 7, n * SEQ:(n + 1) * SEQ], w[:, :], B.x_b[:, 0:SEQ], start=True, stop=True)\
                        .then_inc(s["proj_psum"], 1)
                pe.wait_ge(s["exped"], G * b)
                for t in range(2):
                    last = nc.tensor.matmul(ps[:, 0, t * P:(t + 1) * P], B.x_b[:, t * P:(t + 1) * P], B.wk2[:, :],
                                            start=True, stop=True)
                last.then_inc(s["proj_psum"], 1)
                pe.wait_ge(s["qk_sbuf"], 2 * b + 2)
                pe.wait_ge(s["v_sbuf"], b + 1)
                for g in range(G + 2):
                    if g < G:
                        scores(b, g)
                    if 1 <= g <= G:
                        transposes(b, g - 1)
                    if g >= 2:
                        values(b, g - 2)

        @block.scalar
        def _(act):
            act.wait_ge(s["scaled"], 1)
            with act.Fori(0, BATCHES) as b:
                act.wait_ge(s["proj_psum"], 3 * b)
                act.nop()
                nc.scalar.activation(B.x_b[:, 0:SEQ], B.xn_t[:, bass.ds(b * SEQ, SEQ)], ACT.Copy).then_inc(s["x_staged"], 1)
                act.wait_ge(s["proj_psum"], 3 * b + 2)
                nc.scalar.activation(B.q2_t[:, :], ps[:, 7, 0:SEQ], ACT.Identity, bias=B.bq2_scaled[:, :], scale=SCALE).then_inc(s["qk_sbuf"], 1)
                nc.scalar.activation(B.k2_t[:, :], ps[:, 7, SEQ:2 * SEQ], ACT.Identity, bias=B.bk2[:, :]).then_inc(s["qk_sbuf"], 1)
                act.wait_ge(s["qk_sbuf"], 2 * b + 1)

                def widen(g):
                    for h in (2 * g, 2 * g + 1):
                        last = nc.scalar.activation(B.q_wide[:, h, :], B.q2_t[:, :], ACT.Copy, scale=B.head_mask[:, h:h + 1])
                    last.then_inc(s["wide"], 1)

                widen(0)
                widen(1)
                for g in range(G):
                    n = G * b + g
                    act.wait_ge(s["maxed"], n + 1)
                    if g >= 2:
                        act.wait_ge(s["p_psum"], n - 1)
                    for hh in range(2):
                        for q in range(2):
                            last = nc.scalar.activation(B.p_nat[:, g % 2, hh, q * SEQ:(q + 1) * SEQ],
                                                        ps[:, score_bank(g, hh), q * SEQ:(q + 1) * SEQ], ACT.Exp,
                                                        bias=B.neg_max2[:, g % 2, 2 * hh + q:2 * hh + q + 1])
                    last.then_inc(s["exped"], 1)
                    if g + 2 < G:
                        widen(g + 2)

        @block.vector
        def _(dve):
            nc.vector.tensor_scalar(B.bq2_scaled[:, :], B.bq2[:, :], SCALE, None, ALU.mult).then_inc(s["scaled"], 1)
            with dve.Fori(0, BATCHES) as b:
                dve.wait_ge(s["proj_psum"], 3 * b + 3)
                nc.vector.tensor_tensor(B.va0[:, :, :, 0:8], ps[:, 0, 0:SEQ].rearrange("p (t h d) -> p t h d", t=2, d=8),
                                        B.bk2_row[:, :].rearrange("p (h d) -> p h d", d=8).unsqueeze(1).to_broadcast([P, 2, HEADS, 8]),
                                        ALU.add).then_inc(s["v_sbuf"], 1)
                for g in range(G + 2):
                    if g < G:
                        n = G * b + g
                        dve.wait_ge(s["s_psum"], n + 1)
                        bank = ps[:, score_bank(g, 0):score_bank(g, 0) + 2, :].rearrange("p a (q k) -> p (a q) k", k=SEQ)
                        nc.vector.tensor_reduce(B.neg_max2[:, g % 2, :], bank, AX.X, ALU.max, negate=True).then_inc(s["maxed"], 1)
                    if 1 <= g <= G:
                        n = G * b + g - 1
                        dve.wait_ge(s["p_psum"], n + 1)
                        if g - 1 >= 2:
                            dve.wait_ge(s["y_psum"], n - 1)
                        nc.vector.tensor_copy(B.p_t[:, (g - 1) % 2, :, :], ps[:, 4:6, :]).then_inc(s["p_sbuf"], 1)
                    if g >= 2:
                        n = G * b + g - 2
                        dve.wait_ge(s["y_psum"], n + 1)
                        y = ps[:, 6 + g % 2, 0:36].rearrange("p (t h d) -> p t h d", t=2, d=9)
                        dve.wait_ge(s["y_norm"], n)
                        nc.vector.reciprocal(B.rden[:, :, :], y[:, :, :, 8]).then_inc(s["link"], 1)
                        dve.wait_ge(s["link"], n + 1)
                        nc.vector.tensor_tensor(B.o_nat[:, :, :].rearrange("p t (h d) -> p t h d", d=8)[:, :, 2 * g - 4:2 * g - 2, :],
                                                y[:, :, :, 0:8], B.rden[:, :, :].unsqueeze(3).to_broadcast([P, 2, 2, 8]),
                                                ALU.mult).then_inc(s["y_norm"], 1)
                dve.wait_ge(s["y_norm"], G * (b + 1))
                xb = B.x_res[:, bass.ds(2 * b, 2), :]
                nc.vector.tensor_tensor(xb, xb, B.o_nat[:, :, :], ALU.add).then_inc(s["added"], 1)
                dve.wait_ge(s["added"], b + 1)


def layer3_weights(nc, B):
    ps = B.ps
    with phase(nc, B, "weights3", "squared summed rooted link normed t_psum t_sbuf") as (block, s):

        @block.scalar
        def _(act):
            for n in range(4):
                nc.scalar.activation(B.squares[:, 0, n * P:(n + 1) * P], B.w3[:, n, :], ACT.Square).then_inc(s["squared"], 1)
            act.wait_ge(s["summed"], 1)
            nc.scalar.activation(B.w_norm[:, :], B.w_norm[:, :], ACT.Sqrt, scale=1.0 / D).then_inc(s["rooted"], 1)
            for n in range(2):
                act.wait_ge(s["t_psum"], n + 1)
                m = 4 if n == 0 else 3
                nc.scalar.activation(B.w3_t[:, 4 * n:4 * n + m, :].rearrange("p a b -> p (a b)"), ps[:, n, 0:m * P],
                                     ACT.Copy).then_inc(s["t_sbuf"], 1)

        @block.vector
        def _(dve):
            n_link = [0]

            def link(ins):
                n_link[0] += 1
                ins.then_inc(s["link"], 1)
                dve.wait_ge(s["link"], n_link[0])

            dve.wait_ge(s["squared"], 4)
            nc.vector.tensor_reduce(B.w_norm[:, :], B.squares[:, 0, :].rearrange("p (n d) -> p n d", d=D), AX.X, ALU.add).then_inc(s["summed"], 1)
            link(nc.vector.tensor_scalar(B.gain_s[:, :], B.gain[:, :], float(D) ** -0.5, None, ALU.mult))
            link(nc.vector.tensor_scalar(B.mu[:, 2:4], B.mu[:, 0:2], -1.0, 1.0, ALU.mult, ALU.add))
            link(nc.vector.memset(B.x_b[:, 0:1], 0.0))
            dve.wait_ge(s["rooted"], 1)
            link(nc.vector.tensor_scalar(B.w_norm[:, :], B.w_norm[:, :], 1e-4, None, ALU.add))
            link(nc.vector.reciprocal(B.w_norm[:, :], B.w_norm[:, :]))
            link(nc.vector.tensor_scalar(B.w_norm[:, :], B.w_norm[:, :], B.gain_s[:, :], None, ALU.mult))
            nc.vector.tensor_tensor(B.w3[:, 0:4, :], B.w3[:, 0:4, :], per_tile(B.w_norm[:, :], D), ALU.mult).then_inc(s["normed"], 1)

        @block.tensor
        def _(pe):
            pe.wait_ge(s["normed"], 1)
            for n in range(7):
                last = nc.tensor.transpose(ps[:, n // 4, (n % 4) * P:(n % 4 + 1) * P], B.w3[:, n, :], B.ident[:, :])
                if n in (3, 6):
                    last.then_inc(s["t_psum"], 1)


def channel_attention_and_mix(nc, B, out):
    ps = B.ps
    names = ("x_staged qk_psum v_psum squared summed rooted link qk_norm v_sbuf s_psum shifted exped a_ready at_psum at_sbuf "
             "ot_psum ot_sbuf out_psum mixed_pre mixed r_psum k_psum tanhed k_relu k_sq kv_psum stored added")
    with phase(nc, B, "channel", names) as (block, s):

        @block.sync
        def _(sp):
            with sp.Fori(0, BATCHES) as b:
                sp.wait_ge(s["added"], b + 1)
                sp.dma_start(out[bass.ds(b, 1)].rearrange("a (t p) d -> p (a t) d", p=P),
                             B.x_res[:, bass.ds(2 * b, 2), :]).then_inc(s["stored"], 16)
            sp.wait_ge(s["stored"], 16 * BATCHES)

        @block.gpsimd
        def _(pool):
            with pool.Fori(0, BATCHES) as b:
                pool.wait_ge(s["x_staged"], b + 1)
                for n in range(2):
                    nc.gpsimd.tensor_tensor(B.mix_pre[:, n, :], B.x_b[:, 0:SEQ], B.mu[:, 2 + n:3 + n].to_broadcast([P, SEQ]), ALU.mult).then_inc(s["mixed_pre"], 1)
                pool.wait_ge(s["k_relu"], b + 1)
                nc.gpsimd.tensor_tensor(B.k_act[:, :], B.k_act[:, :], B.k_act[:, :], ALU.mult).then_inc(s["k_sq"], 1)

        @block.scalar
        def _(act):
            with act.Fori(0, BATCHES) as b:
                act.wait_ge(s["v_psum"], b)
                act.wait_ge(s["mixed"], 2 * b)
                act.nop()
                nc.scalar.activation(B.x_b[:, 1:SEQ + 1], B.xn_t[:, bass.ds(b * SEQ, SEQ)], ACT.Copy).then_inc(s["x_staged"], 1)
                act.wait_ge(s["qk_psum"], b + 1)
                nc.scalar.activation(B.squares[:, 0, :], ps[:, 0, :], ACT.Square).then_inc(s["squared"], 1)
                act.wait_ge(s["v_psum"], b + 1)
                nc.scalar.activation(B.v3_t[:, :], ps[:, 1, 0:SEQ], ACT.Copy).then_inc(s["v_sbuf"], 1)
                act.wait_ge(s["r_psum"], b + 1)
                nc.scalar.activation(B.r_gate[:, :], ps[:, 4, 0:SEQ], ACT.Tanh, scale=0.5).then_inc(s["tanhed"], 1)
                act.wait_ge(s["k_psum"], b + 1)
                nc.scalar.activation(B.k_act[:, :], ps[:, 5, 0:SEQ], ACT.Relu).then_inc(s["k_relu"], 1)
                act.wait_ge(s["summed"], b + 1)
                nc.scalar.activation(B.qk_len[:, :], B.qk_len[:, :], ACT.Sqrt, scale=1.0 / 8).then_inc(s["rooted"], 1)
                act.wait_ge(s["shifted"], b + 1)
                nc.scalar.activation(B.a_nat[:, :], B.a_nat[:, :], ACT.Exp, bias=B.a_max[:, :], scale=SEQ ** -0.5,
                                     accum_out=B.a_sum[:, :]).then_inc(s["exped"], 1)
                act.wait_ge(s["at_psum"], b + 1)
                nc.scalar.activation(B.a_t[:, :], ps[:, 2, P:2 * P], ACT.Copy).then_inc(s["at_sbuf"], 1)
                act.wait_ge(s["ot_psum"], b + 1)
                nc.scalar.activation(B.o3_t[:, :], ps[:, 3, 0:SEQ], ACT.Copy).then_inc(s["ot_sbuf"], 1)

        @block.tensor
        def _(pe):
            with pe.Fori(0, BATCHES) as b:
                pe.wait_ge(s["x_staged"], b + 1)
                pe.wait_ge(s["qk_norm"], b)
                for t in range(2):
                    last = nc.tensor.matmul(ps[:, 0, t * SEQ:(t + 1) * SEQ], B.x_b[:, 1 + t * P:1 + (t + 1) * P],
                                            B.w3_t[:, 0:2, :].rearrange("p a b -> p (a b)"), start=True, stop=True)
                last.then_inc(s["qk_psum"], 1)
                nc.tensor.matmul(ps[:, 1, 0:SEQ], B.w3_t[:, 2, :], B.x_b[:, 1:SEQ + 1], start=True, stop=True).then_inc(s["v_psum"], 1)
                pe.wait_ge(s["mixed"], 2 * b + 2)
                for t in range(2):
                    last = nc.tensor.matmul(ps[:, 4, t * P:(t + 1) * P], B.mix[:, 0, t * P:(t + 1) * P], B.w3_t[:, 4, :],
                                            start=True, stop=True)
                last.then_inc(s["r_psum"], 1)
                nc.tensor.matmul(ps[:, 5, 0:SEQ], B.w3_t[:, 5, :], B.mix[:, 1, :], start=True, stop=True).then_inc(s["k_psum"], 1)
                pe.wait_ge(s["k_sq"], b + 1)
                pe.wait_ge(s["added"], b)
                for t in range(2):
                    last = nc.tensor.matmul(ps[:, 6, t * P:(t + 1) * P], B.k_act[:, t * P:(t + 1) * P], B.w3_t[:, 6, :],
                                            start=True, stop=True)
                last.then_inc(s["kv_psum"], 1)
                pe.wait_ge(s["qk_norm"], b + 1)
                for t in range(2):
                    last = nc.tensor.matmul(ps[:, 2, 0:P], B.qk[:, t, 0:P], B.qk[:, t, P:2 * P], start=t == 0, stop=t == 1)
                last.then_inc(s["s_psum"], 1)
                pe.wait_ge(s["a_ready"], b + 1)
                nc.tensor.transpose(ps[:, 2, P:2 * P], B.a_nat[:, :], B.ident[:, :]).then_inc(s["at_psum"], 1)
                pe.wait_ge(s["at_sbuf"], b + 1)
                nc.tensor.matmul(ps[:, 3, 0:SEQ], B.a_t[:, :], B.v3_t[:, :], start=True, stop=True).then_inc(s["ot_psum"], 1)
                pe.wait_ge(s["ot_sbuf"], b + 1)
                for t in range(2):
                    last = nc.tensor.matmul(ps[:, 7, t * P:(t + 1) * P], B.o3_t[:, t * P:(t + 1) * P], B.w3_t[:, 3, :],
                                            start=True, stop=True)
                last.then_inc(s["out_psum"], 1)

        @block.vector
        def _(dve):
            LINKS = 9
            with dve.Fori(0, BATCHES) as b:
                n_link = [0]

                def link(ins):
                    n_link[0] += 1
                    ins.then_inc(s["link"], 1)
                    dve.wait_ge(s["link"], LINKS * b + n_link[0])

                for n in range(2):
                    dve.wait_ge(s["mixed_pre"], 2 * b + n + 1)
                    nc.vector.scalar_tensor_tensor(out=B.mix[:, n, :], in0=B.x_b[:, 1:SEQ + 1], scalar=B.mu[:, n:n + 1],
                                                   in1=B.mix_pre[:, n, :], op0=ALU.mult, op1=ALU.add).then_inc(s["mixed"], 1)
                dve.wait_ge(s["squared"], b + 1)
                nc.vector.tensor_reduce(B.qk_len[:, :], B.squares[:, 0, :].rearrange("p (h d) -> p h d", d=8), AX.X,
                                        ALU.add).then_inc(s["summed"], 1)
                dve.wait_ge(s["rooted"], b + 1)
                link(nc.vector.tensor_scalar(B.qk_len[:, :], B.qk_len[:, :], 1e-4, None, ALU.add))
                link(nc.vector.reciprocal(B.qk_len[:, :], B.qk_len[:, :]))
                nc.vector.tensor_tensor(B.qk[:, :, :].rearrange("p t (h d) -> p (t h) d", d=8),
                                        ps[:, 0, :].rearrange("p (h d) -> p h d", d=8), per_tile(B.qk_len[:, :], 8),
                                        ALU.mult).then_inc(s["qk_norm"], 1)
                dve.wait_ge(s["s_psum"], b + 1)
                link(nc.vector.tensor_tensor(B.a_nat[:, :], ps[:, 2, 0:P], B.not_same_head[:, :], ALU.add))
                link(nc.vector.tensor_reduce(B.a_max[:, :], B.a_nat[:, :], AX.X, ALU.max))
                nc.vector.tensor_scalar(B.a_max[:, :], B.a_max[:, :], -SEQ ** -0.5, None, ALU.mult).then_inc(s["shifted"], 1)
                dve.wait_ge(s["exped"], b + 1)
                link(nc.vector.reciprocal(B.a_sum[:, :], B.a_sum[:, :]))
                nc.vector.tensor_scalar(B.a_nat[:, :], B.a_nat[:, :], B.a_sum[:, :], None, ALU.mult).then_inc(s["a_ready"], 1)
                dve.wait_ge(s["tanhed"], b + 1)
                link(nc.vector.tensor_scalar(B.r_gate[:, :], B.r_gate[:, :], 0.5, 0.5, ALU.mult, ALU.add))
                dve.wait_ge(s["kv_psum"], b + 1)
                link(nc.vector.tensor_tensor(B.r_gate[:, :], B.r_gate[:, :], ps[:, 6, 0:SEQ], ALU.mult))
                xb, xn = B.x_res[:, bass.ds(2 * b, 2), :], B.xn[:, bass.ds(2 * b, 2), :]
                dve.wait_ge(s["out_psum"], b + 1)
                link(nc.vector.tensor_tensor(B.o_nat[:, :, :], xn, ps[:, 7, 0:SEQ].rearrange("p (t d) -> p t d", d=D), ALU.add))
                r = B.r_gate[:, :].rearrange("p (t d) -> p t d", d=D)
                link(nc.vector.scalar_tensor_tensor(out=B.o_nat[:, :, :], in0=B.o_nat[:, :, :], scalar=float(0.5 / np.sqrt(0.5)),
                                                    in1=r, op0=ALU.mult, op1=ALU.add))
                assert n_link[0] == LINKS
                nc.vector.tensor_tensor(xb, xb, B.o_nat[:, :, :], ALU.add).then_inc(s["added"], 1)


def experts(nc, I, B, layer, cap, rows_n, rows, outs):
    tiles = cap // rows_n
    gated = layer == 0
    half = cap // 2 if gated else cap
    names = ("w0 w1 xe0 xe1 b0 b1 xt_psum0 xt_psum1 xt h_psum h_act h y_psum0 y_psum1 y y_out0 y_out1 bt_psum bt bcol b_in")
    ps = B.ps
    w_up = {0: I["L0_ffn_gate_w"], 1: I["L1_ffn_W1"], 2: I["L2_ffn_w1"]}[layer]
    w_down = {0: I["L0_ffn_down_w"], 1: I["L1_ffn_W2"], 2: I["L2_ffn_w2"]}[layer]
    b_up = {0: None, 1: I["L1_ffn_b1"], 2: I["L2_ffn_b1"]}[layer]
    b_down = {0: None, 1: I["L1_ffn_b2"], 2: I["L2_ffn_b2"]}[layer]
    n_w = 3 if gated else 2
    with phase(nc, B, f"experts{layer}", names) as (block, s):
        w_in, xe_in, b_in2 = (s["w0"], s["w1"]), (s["xe0"], s["xe1"]), (s["b0"], s["b1"])
        xt_psum, y_psum, y_out = (s["xt_psum0"], s["xt_psum1"]), (s["y_psum0"], s["y_psum1"]), (s["y_out0"], s["y_out1"])
        xt_view = ps[:, 0:2, :].rearrange("p a b -> p (a b)")
        y_view = ps[:, 6:8, :].rearrange("p a b -> p (a b)")
        steps = 8 if gated else 4

        @block.sync
        def _(sp):
            if not gated:
                sp.dma_start(B.b_rows[:, :], b_up.rearrange("e (c p) -> (e c) p", p=P)).then_inc(s["b_in"], 16)
            with sp.Fori(0, EXPERTS // 2) as i:
                for k in range(2):
                    e = 2 * i + k
                    sp.wait_ge(xt_psum[k], i)
                    src = rows.rearrange("(e r) d -> e r d", e=EXPERTS)[bass.ds(e, 1)].rearrange("a (j p) d -> p (a j) d", p=rows_n)
                    sp.dma_start(B.xe[0:rows_n, k, 0:tiles, :], src).then_inc(xe_in[k], 16)
                    sp.wait_ge(y_psum[k], i)
                    sp.dma_start(B.w_up[:, k, 0, :], w_up[bass.ds(e, 1)].rearrange("a d f -> d (a f)")).then_inc(w_in[k], 16)
                    if gated:
                        sp.dma_start(B.w_up[:, k, 1, :], I["L0_ffn_up_w"][bass.ds(e, 1)].rearrange("a d f -> d (a f)")).then_inc(w_in[k], 16)
                    sp.dma_start(B.w_down[:, k, :, :], w_down[bass.ds(e, 1)].rearrange("a (c p) d -> p (a c) d", p=P)).then_inc(w_in[k], 16)
                    if not gated:
                        sp.wait_ge(y_out[k], 16 * i)
                        sp.dma_start(B.b_down[:, k, :], b_down[bass.ds(e, 1)].broadcast_to([P, D])).then_inc(b_in2[k], 16)

        @block.tensor
        def _(pe):
            if not gated:
                pe.wait_ge(s["b_in"], 16)
                nc.tensor.transpose(ps[:, 2, 0:EXPERTS * FCH], B.b_rows[:, :], B.ident[0:32, 0:32]).then_inc(s["bt_psum"], 1)
                pe.wait_ge(s["bt"], 1)
            with pe.Fori(0, EXPERTS // 2) as i:
                for k in range(2):
                    n = 2 * i + k
                    pe.wait_ge(xe_in[k], 16 * i + 16)
                    pe.wait_ge(s["xt"], n)
                    for j in range(tiles):
                        last = nc.tensor.transpose(xt_view[:, j * rows_n:(j + 1) * rows_n], B.xe[0:rows_n, k, j, :],
                                                   B.ident[0:rows_n, 0:rows_n])
                    last.then_inc(xt_psum[k], 1)
                    pe.wait_ge(s["xt"], n + 1)
                    pe.wait_ge(w_in[k], 16 * n_w * (i + 1))
                    for m in range(steps):
                        c, a = (m // 2, (m % 2) * half) if gated else (m, 0)
                        bank = 2 + (m % 2) * 2 if gated else 2 + m % 2
                        pe.wait_ge(s["h"], steps * n + max(m - 1, 0))
                        for g in range(2 if gated else 1):
                            last = nc.tensor.matmul(ps[:, bank + g, 0:half], B.w_up[:, k, g, c * P:(c + 1) * P],
                                                    B.xe_t[:, a:a + half], start=True, stop=True)
                        last.then_inc(s["h_psum"], 1)
                    pe.wait_ge(s["h"], steps * (n + 1))
                    pe.wait_ge(s["y"], n)
                    for j in range(tiles):
                        for c in range(FCH):
                            last = nc.tensor.matmul(y_view[0:rows_n, j * P:(j + 1) * P],
                                                    B.h_t[:, c, j * rows_n:(j + 1) * rows_n], B.w_down[:, k, c, :],
                                                    start=c == 0, stop=c == FCH - 1)
                    last.then_inc(y_psum[k], 1)

        @block.scalar
        def _(act):
            with act.Fori(0, EXPERTS // 2) as i:
                for k in range(2):
                    n = 2 * i + k
                    if gated:
                        for m in range(steps):
                            act.wait_ge(s["h_psum"], steps * n + m + 1)
                            act.wait_ge(s["h"], steps * n + max(m - 1, 0))
                            nc.scalar.activation(B.h_gate[:, m % 2, 0:half], ps[:, 2 + (m % 2) * 2, 0:half], ACT.Silu).then_inc(s["h_act"], 1)
                    else:
                        act.wait_ge(s["bcol"], n + 1)
                        act.wait_ge(y_psum[1 - k], i + k)
                        for m in range(steps):
                            act.wait_ge(s["h_psum"], steps * n + m + 1)
                            nc.scalar.activation(B.h_t[:, m, 0:cap], ps[:, 2 + m % 2, 0:cap], ACT.Gelu,
                                                 bias=B.b_up[:, k, m:m + 1]).then_inc(s["h"], 1)

        @block.vector
        def _(dve):
            if not gated:
                dve.wait_ge(s["bt_psum"], 1)
                nc.vector.tensor_copy(B.b_cols[:, :], ps[:, 2, 0:EXPERTS * FCH]).then_inc(s["bt"], 1)
                dve.wait_ge(s["bt"], 1)
            with dve.Fori(0, EXPERTS // 2) as i:
                for k in range(2):
                    n = 2 * i + k
                    if not gated:
                        dve.wait_ge(s["h"], steps * n)
                        nc.vector.tensor_scalar(B.b_up[:, k, :], B.b_cols[:, bass.ds(n * FCH, FCH)], 0.0, None, ALU.add).then_inc(s["bcol"], 1)
                    dve.wait_ge(xt_psum[k], i + 1)
                    nc.vector.tensor_copy(B.xe_t[:, 0:cap], xt_view[:, 0:cap]).then_inc(s["xt"], 1)
                    if gated:
                        dve.wait_ge(y_psum[1 - k], i + k)
                        for m in range(steps):
                            c, a = m // 2, (m % 2) * half
                            dve.wait_ge(s["h_act"], steps * n + m + 1)
                            nc.vector.tensor_tensor(B.h_t[:, c, a:a + half], ps[:, 3 + (m % 2) * 2, 0:half],
                                                    B.h_gate[:, m % 2, 0:half], ALU.mult).then_inc(s["h"], 1)
                    dve.wait_ge(y_psum[k], i + 1)
                    dve.wait_ge(y_out[k], 16 * i)
                    src = y_view[0:rows_n, 0:tiles * P].rearrange("p (j d) -> p j d", d=P)
                    if gated:
                        nc.vector.tensor_copy(B.ye[0:rows_n, k, 0:tiles, :], src).then_inc(s["y"], 1)
                    else:
                        dve.wait_ge(b_in2[k], 16 * i + 16)
                        nc.vector.tensor_tensor(B.ye[0:rows_n, k, 0:tiles, :], src,
                                                B.b_down[0:rows_n, k, :].unsqueeze(1).to_broadcast([rows_n, tiles, D]),
                                                ALU.add).then_inc(s["y"], 1)

        @block.gpsimd
        def _(pool):
            with pool.Fori(0, EXPERTS // 2) as i:
                for k in range(2):
                    n = 2 * i + k
                    pool.wait_ge(s["y"], n + 1)
                    pool.nop()
                    dst = outs.rearrange("(e r) d -> e r d", e=EXPERTS)[bass.ds(n, 1)].rearrange("a (j p) d -> p (a j) d", p=rows_n)
                    pool.dma_start(dst, B.ye[0:rows_n, k, 0:tiles, :]).then_inc(y_out[k], 16)
            for k in range(2):
                pool.wait_ge(y_out[k], 16 * (EXPERTS // 2))


def combine(nc, B, layer, outs, choices, bias):
    with phase(nc, B, f"combine{layer}", "g0 g1 g2 g3 weighted link") as (block, s):
        landed = (s["g0"], s["g1"], s["g2"], s["g3"])
        PER = 4

        @block.gpsimd
        def _(pool):
            for t in range(TILES):
                for k in range(choices):
                    nc.gpsimd.indirect_dma_start(B.back[:, k, t, :], None, outs,
                                                 bass.IndirectOffsetOnAxis(ap=B.from_slot[:, k, t:t + 1], axis=0)).then_inc(landed[t // PER], 16)

        @block.vector
        def _(dve):
            n_link = [0]

            def link(ins):
                n_link[0] += 1
                ins.then_inc(s["link"], 1)
                dve.wait_ge(s["link"], n_link[0])

            if bias is not None:
                link(nc.vector.tensor_tensor(B.x_res[:, :, :], B.x_res[:, :, :],
                                             bias[:, :].unsqueeze(1).to_broadcast([P, TILES, D]), ALU.add))
            for g in range(TILES // PER):
                t = slice(g * PER, (g + 1) * PER)
                dve.wait_ge(landed[g], 16 * PER * choices)
                for k in range(choices):
                    link(nc.vector.tensor_tensor(B.back[:, k, t, :], B.back[:, k, t, :], per_tile(B.gate[:, k, t], D), ALU.mult))
                    link(nc.vector.tensor_tensor(B.x_res[:, t, :], B.x_res[:, t, :], B.back[:, k, t, :], ALU.add))


class Buffers:
    pass


def build(nc, I, out):
    with ExitStack() as ctx:
        B = Buffers()
        B.used_semaphores = []

        def sb(name, shape, dt=F32):
            return ctx.enter_context(nc.sbuf_tensor(name, shape, dt))

        B.ps = ctx.enter_context(nc.psum_tensor("ps", [P, 8, 512], F32))
        B.x_res = sb("x_res", [P, TILES, D])
        B.xn = sb("xn", [P, TILES, D])
        B.xn_t = sb("xn_t", [P, TOKENS])
        B.ident = sb("ident", [P, P])
        B.ones = sb("ones", [P, P])
        B.same_head = sb("same_head", [P, P])
        B.not_same_head = sb("not_same_head", [P, P])
        B.same_expert = sb("same_expert", [P, P])
        B.low_expert = sb("low_expert", [P, P])
        B.bo_row = sb("bo_row", [P, P])
        B.te_val = sb("te_val", [P, P])
        B.te_keep = sb("te_keep", [P, P])
        B.te_junk = sb("te_junk", [P, P])
        B.te_tie = sb("te_tie", [P, P])
        B.te_rank = sb("te_rank", [P, P])
        B.te_slot = sb("te_slot", [P, P])
        B.wq0 = sb("wq0", [P, P])
        B.wk0 = sb("wk0", [P, P])
        B.wv0 = sb("wv0", [P, P])
        B.wo0 = sb("wo0", [P, P])
        B.ident_b = sb("ident_b", [P, P], BF16)
        B.causal_b = sb("causal_b", [P, P], BF16)
        B.router = sb("router", [P, 3, EXPERTS])
        B.bf_col = sb("bf_col", [P, 1])
        B.bf_row = sb("bf_row", [P, FEAT])
        B.wqf = sb("wqf", [P, HEADS * FEAT])
        B.wkf = sb("wkf", [P, HEADS * FEAT])
        B.wqt = sb("wqt", [P, 2, P])
        B.head_mask = sb("head_mask", [P, HEADS])
        B.expert_m8 = sb("expert_m8", [P, TILES, EXPERTS])
        B.r_a = sb("r_a", [P, TILES, EXPERTS])
        B.r_exp = sb("r_exp", [P, TILES, EXPERTS])
        B.r_prob = sb("r_prob", [P, TILES, EXPERTS])
        B.r_choice = sb("r_choice", [P, TILES, EXPERTS])
        B.r_one = sb("r_one", [P, 2, TILES, EXPERTS])
        B.int_a = sb("int_a", [P, P], I32)
        B.int_b = sb("int_b", [P, 1], I32)
        B.own_expert = sb("own_expert", [P, 1])
        B.gate_bits = sb("gate_bits", [P, GATE_BITS], I32)
        B.gate_bits_f = sb("gate_bits_f", [P, GATE_BITS])
        B.half_neg = sb("half_neg", [P, TILES])
        B.mean = sb("mean", [P, TILES])
        B.variance = sb("variance", [P, TILES])
        B.rstd = sb("rstd", [P, TILES])
        B.v_a = sb("v_a", [P, TILES])
        B.v_b = sb("v_b", [P, TILES])
        B.squares = sb("squares", [P, 2, 512])
        B.gate = sb("gate", [P, 2, TILES])
        B.to_slot = sb("to_slot", [P, 2, TILES], I32)
        B.from_slot = sb("from_slot", [P, 2, TILES], I32)
        B.c_count = sb("c_count", [P, 1])
        B.c_above = sb("c_above", [P, 1])
        B.c_ties = sb("c_ties", [P, 1])
        B.c_kept = sb("c_kept", [P, 1])
        B.c_room = sb("c_room", [P, 1])
        B.c_start = sb("c_start", [P, 1])
        B.thr = sb("thr", [P, 1], I32)
        B.thr_try = sb("thr_try", [P, 1], I32)
        B.thr_add = sb("thr_add", [P, 1], I32)
        B.x_b = sb("x_b", [P, SEQ + 1])
        B.va0 = sb("va0", [P, 2, HEADS, 9])
        B.kv0 = sb("kv0", [P, PAIRS, 18])
        B.den = sb("den", [P, 2 * HEADS])
        B.o_nat = sb("o_nat", [P, 2, D])
        B.o_t = sb("o_t", [P, 2, D])
        B.w_kv_down = sb("w_kv_down", [P, P])
        B.w_kv_up = sb("w_kv_up", [P, 2 * HEADS * HS])
        B.w_q = sb("w_q", [P, HEADS * HS])
        B.w_out = sb("w_out", [P, 8, D])
        B.latent = sb("latent", [P, SEQ])
        B.q_t = sb("q_t", [P, 8, SEQ])
        B.k_t = sb("k_t", [P, 8, SEQ])
        B.v_nat = sb("v_nat", [P, 2, HEADS, HS + 1])
        B.neg_max = sb("neg_max", [P, 2, 2, 2])
        B.p_nat = sb("p_nat", [P, 2, 2, 512])
        B.y_nat = sb("y_nat", [P, 2, HEADS * HS])
        B.y_t = sb("y_t", [P, 2, 8, P])
        B.rden = sb("rden", [P, 2, 2])
        B.p_t = sb("p_t", [P, 2, 2, 512])
        B.wq2 = sb("wq2", [P, P])
        B.wk2 = sb("wk2", [P, P])
        B.bk2_row = sb("bk2_row", [P, P])
        B.bq2 = sb("bq2", [P, 1])
        B.bk2 = sb("bk2", [P, 1])
        B.bq2_scaled = sb("bq2_scaled", [P, 1])
        B.q2_t = sb("q2_t", [P, SEQ])
        B.k2_t = sb("k2_t", [P, SEQ])
        B.neg_max2 = sb("neg_max2", [P, 2, 4])
        B.gain = sb("gain", [P, 1])
        B.gain_s = sb("gain_s", [P, 1])
        B.w3 = sb("w3", [P, 7, D])
        B.w3_t = sb("w3_t", [P, 7, D])
        B.mu = sb("mu", [P, 4])
        B.w_norm = sb("w_norm", [P, 4])
        B.mix_pre = sb("mix_pre", [P, 2, SEQ])
        B.mix = sb("mix", [P, 2, SEQ])
        B.k_act = sb("k_act", [P, SEQ])
        B.r_gate = sb("r_gate", [P, SEQ])
        B.v3_t = sb("v3_t", [P, SEQ])
        B.qk_len = sb("qk_len", [P, 4 * HEADS])
        B.qk = sb("qk", [P, 2, SEQ])
        B.a_nat = sb("a_nat", [P, P])
        B.a_t = sb("a_t", [P, P])
        B.a_max = sb("a_max", [P, 1])
        B.a_sum = sb("a_sum", [P, 1])
        B.o3_t = sb("o3_t", [P, SEQ])
        B.xe = sb("xe", [P, 2, 5, D])
        B.xe_t = sb("xe_t", [P, CAP0])
        B.h_t = sb("h_t", [P, FCH, CAP0])
        B.h_gate = sb("h_gate", [P, 2, CAP0 // 2])
        B.w_up = sb("w_up", [P, 2, 2, FF])
        B.w_down = sb("w_down", [P, 2, FCH, D])
        B.ye = sb("ye", [P, 2, 5, D])
        B.b_rows = sb("b_rows", [EXPERTS * FCH, P])
        B.b_cols = sb("b_cols", [P, EXPERTS * FCH])
        B.b_up = sb("b_up", [P, 2, FCH])
        B.b_down = sb("b_down", [P, 2, D])
        arena = sb("arena", [P, 2 * TILES * D])
        B.qf = arena[:, 0:PAIRS * SEQ].rearrange("p (a b) -> p a b", a=PAIRS)
        B.kf = arena[:, PAIRS * SEQ:PAIRS * SEQ + 2 * HEADS * FEAT].rearrange("p (a b) -> p a b", a=2)
        B.q_wide = arena[:, :].rearrange("p (h q) -> p h q", h=HEADS)
        B.back = arena[:, :].rearrange("p (k t d) -> p k t d", k=2, t=TILES)
        B.zeros = B.q_t[:, :, :].rearrange("p a b -> p (a b)")[:, 0:1536]
        B.wf_diag = B.y_nat[:, 0, :]
        def slots(name, cap):
            return nc.dram_tensor(name, [EXPERTS * cap, D], F32, kind="Internal").ap()

        B.rows0 = slots("rows0", CAP0)
        B.rows1 = slots("rows1", CAP1)
        B.rows2 = slots("rows2", CAP2)
        B.outs0 = slots("outs0", CAP0)
        B.outs1 = slots("outs1", CAP1)
        B.outs2 = slots("outs2", CAP2)

        setup(nc, I, B)
        norm_and_route(nc, B, 0, CAP0)
        linear_attention(nc, I, B)
        experts(nc, I, B, 0, CAP0, ROWS0, B.rows0, B.outs0)
        combine(nc, B, 0, B.outs0, 2, B.bo_row)
        if LAST_LAYER >= 2:
            norm_and_route(nc, B, 1, CAP1)
            latent_attention(nc, I, B)
            experts(nc, I, B, 1, CAP1, ROWS1, B.rows1, B.outs1)
            combine(nc, B, 1, B.outs1, 1, None)
        if LAST_LAYER >= 3:
            norm_and_route(nc, B, 2, CAP2)
            small_head_attention(nc, B)
            experts(nc, I, B, 2, CAP2, ROWS2, B.rows2, B.outs2)
            combine(nc, B, 2, B.outs2, 1, None)
        if LAST_LAYER >= 4:
            layer3_weights(nc, B)
            norm_and_route(nc, B, 3, 0)
            channel_attention_and_mix(nc, B, out)
            return
        with phase(nc, B, "store", "stored") as (block, s):
            @block.sync
            def _(sp):
                sp.dma_start(out.rearrange("b (t p) d -> p (b t) d", p=P), B.x_res[:, :, :]).then_inc(s["stored"], 16)
                sp.wait_ge(s["stored"], 16)


_INS = ['L0_attn_x', 'L0_attn_Wq', 'L0_attn_Wk', 'L0_attn_Wv', 'L0_attn_Wo', 'L0_attn_bo', 'L0_attn_Wf', 'L0_attn_bf',
        'L0_ffn_router_gate', 'L0_ffn_gate_w', 'L0_ffn_up_w', 'L0_ffn_down_w', 'L1_attn_w_kv_down', 'L1_attn_w_kv_up',
        'L1_attn_w_q', 'L1_attn_w_out', 'L1_ffn_wg', 'L1_ffn_W1', 'L1_ffn_b1', 'L1_ffn_W2', 'L1_ffn_b2', 'L2_attn_Wq',
        'L2_attn_bq', 'L2_attn_Wk', 'L2_attn_bk', 'L2_ffn_router_w', 'L2_ffn_w1', 'L2_ffn_b1', 'L2_ffn_w2', 'L2_ffn_b2',
        'L3_attn_gain', 'L3_attn_w_q', 'L3_attn_w_k', 'L3_attn_w_v', 'L3_attn_w_o', 'L3_ffn_W_r', 'L3_ffn_W_k',
        'L3_ffn_W_v', 'L3_ffn_mu_r', 'L3_ffn_mu_k']


def kernel(**inputs):
    import concourse.bacc as bacc
    from concourse.bass_utils import run_bass_kernel_spmd as run

    nc = bacc.Bacc("TRN2", target_bir_lowering=False, num_devices=1)
    arrays, ins = {}, {}
    for name in _INS:
        a = np.ascontiguousarray(inputs[name])
        arrays[f"in_{name}"] = a
        ins[name] = nc.dram_tensor(f"in_{name}", a.shape, mybir.dt.from_np(a.dtype), kind="ExternalInput").ap()
    out = nc.dram_tensor("out", [BATCHES, SEQ, D], F32, kind="ExternalOutput").ap()
    build(nc, ins, out)
    return run(nc, [arrays], core_ids=[0]).results[0]["out"]
```

```python
from contextlib import ExitStack, contextmanager

import numpy as np
import concourse.bass as bass
from concourse import mybir

ALU = mybir.AluOpType
ACT = mybir.ActivationFunctionType
AX = mybir.AxisListType
F32 = mybir.dt.float32
BF16 = mybir.dt.bfloat16
I32 = mybir.dt.int32

P = 128
BATCHES = 8
SEQ = 256
D = 128
TOKENS = BATCHES * SEQ
TILES = TOKENS // P
HEADS = 16
EXPERTS = 8
FF = 512
FCH = FF // P
NEG = -1e30
LN_EPS = 1e-5
PAD_SLOT = 1 << 16

FEAT = 64
PAIRS = HEADS // 2
HS = 64
LAG = 2
CAP0 = int(1.25 * ((TOKENS * 2 + EXPERTS - 1) // EXPERTS))
CAP1 = int(TOKENS / EXPERTS * 1.25) + 1
CAP2 = int(np.ceil(1.5 * TOKENS / EXPERTS))
ROWS0, ROWS1, ROWS2 = 128, 107, 128
GATE_BITS = 30


@contextmanager
def phase(nc, B, stage, names):
    handles = {n: nc.alloc_semaphore(f"{stage}_{n}") for n in names.split()}
    if B.used_semaphores:
        nc.clear_and_free_semaphores(B.used_semaphores)
    B.used_semaphores = list(handles.values())
    with nc.Block() as block:
        yield block, handles


def per_tile(ap, n):
    return ap.unsqueeze(2).to_broadcast([ap.shape[0], ap.shape[1], n])


def columns(vector):
    return vector.rearrange("(p a) -> p a", a=1)


def row_on_all(vector, n=P):
    return vector.rearrange("(a d) -> a d", a=1).broadcast_to([n, vector.shape[0]])


def setup(nc, I, B):
    with phase(nc, B, "setup", "x_in w_in zeroed rows_zero made ints wf_ready feat_psum feat_sbuf wt_psum wt_sbuf const") as (block, s):

        @block.sync
        def _(sp):
            sp.dma_start(B.x_res[:, :, :], I["L0_attn_x"].rearrange("b (t p) d -> p (b t) d", p=P)).then_inc(s["x_in"], 16)
            for dst, src in ((B.wq0, I["L0_attn_Wq"]), (B.wk0, I["L0_attn_Wk"]), (B.wv0, I["L0_attn_Wv"]), (B.wo0, I["L0_attn_Wo"])):
                sp.dma_start(dst[:, :], src).then_inc(s["w_in"], 16)
            for half in range(2):
                sp.dma_start(B.bf_col[half * FEAT:(half + 1) * FEAT, :], columns(I["L0_attn_bf"])).then_inc(s["w_in"], 16)
            sp.dma_start(B.bf_row[:, :], row_on_all(I["L0_attn_bf"])).then_inc(s["w_in"], 16)
            sp.dma_start(B.bo_row[:, :], row_on_all(I["L0_attn_bo"])).then_inc(s["w_in"], 16)
            sp.dma_start(B.router[:, 0, :], I["L0_ffn_router_gate"]).then_inc(s["w_in"], 16)
            sp.dma_start(B.router[:, 1, :], I["L1_ffn_wg"]).then_inc(s["w_in"], 16)
            sp.dma_start(B.router[:, 2, :], I["L2_ffn_router_w"].rearrange("e d -> d e"),
                         allow_slow_non_contiguous=True).then_inc(s["w_in"], 16)
            sp.wait_ge(s["zeroed"], 2)
            for h in range(HEADS):
                sp.dma_start(B.wf_diag[8 * h:8 * h + 8, h * FEAT:(h + 1) * FEAT], I["L0_attn_Wf"]).then_inc(s["wf_ready"], 16)
            sp.wait_ge(s["x_in"], 16)
            sp.wait_ge(s["w_in"], 16 * 11)

        @block.gpsimd
        def _(pool):
            nc.gpsimd.memset(B.zeros[:, :], 0.0).then_inc(s["zeroed"], 1)
            nc.gpsimd.memset(B.wf_diag[:, :], 0.0).then_inc(s["zeroed"], 1)
            nc.gpsimd.memset(B.ident[:, :], 0.0).then_inc(s["made"], 1)
            nc.gpsimd.memset(B.ones[:, :], 1.0).then_inc(s["made"], 1)
            nc.gpsimd.memset(B.ident_b[:, :], 0.0).then_inc(s["made"], 1)
            nc.gpsimd.memset(B.causal_b[:, :], 0.0).then_inc(s["made"], 1)
            pool.wait_ge(s["made"], 4)
            for m in (B.ident, B.ident_b):
                nc.gpsimd.affine_select(out=m[:, :], in_=m[:, :], compare_op=ALU.not_equal, fill=1.0, base=0,
                                        pattern=[[-1, P]], channel_multiplier=1).then_inc(s["made"], 1)
            nc.gpsimd.affine_select(out=B.causal_b[:, :], in_=B.causal_b[:, :], compare_op=ALU.is_ge, fill=NEG, base=0,
                                    pattern=[[-1, P]], channel_multiplier=1).then_inc(s["made"], 1)
            v = B.same_head[:, :].rearrange("p (h j) -> p h j", j=8)
            ones = B.ones[:, :].rearrange("p (h j) -> p h j", j=8)
            nc.gpsimd.affine_select(out=v, in_=ones, compare_op=ALU.is_ge, fill=0.0, base=0,
                                    pattern=[[-8, HEADS], [0, 8]], channel_multiplier=1).then_inc(s["made"], 1)
            pool.wait_ge(s["made"], 8)
            nc.gpsimd.affine_select(out=v, in_=v, compare_op=ALU.is_ge, fill=0.0, base=7,
                                    pattern=[[8, HEADS], [0, 8]], channel_multiplier=-1).then_inc(s["made"], 1)
            pool.wait_ge(s["made"], 9)
            nc.gpsimd.tensor_copy(B.head_mask[:, :], v[:, :, 0]).then_inc(s["made"], 1)
            nc.gpsimd.iota(B.expert_m8[:, :, :], pattern=[[0, TILES], [1, EXPERTS]], base=-EXPERTS, channel_multiplier=0,
                           allow_small_or_imprecise_dtypes=True).then_inc(s["ints"], 1)
            nc.gpsimd.iota(B.int_a[:, :], pattern=[[1, P]], base=P, channel_multiplier=-1).then_inc(s["ints"], 1)
            nc.gpsimd.iota(B.int_b[:, :], pattern=[[0, 1]], base=0, channel_multiplier=1).then_inc(s["ints"], 1)
            for n in range(GATE_BITS):
                nc.gpsimd.memset(B.gate_bits[:, n:n + 1], 1 << (GATE_BITS - 1 - n)).then_inc(s["ints"], 1)
            for va in B.va:
                nc.gpsimd.memset(va[:, :, :, 8:9], 1.0).then_inc(s["ints"], 1)
            nc.gpsimd.memset(B.kv0[:, :, :], 0.0).then_inc(s["ints"], 1)
            nc.gpsimd.memset(B.half_neg[:, :], -0.5).then_inc(s["ints"], 1)
            pool.wait_ge(s["const"], 3)
            nc.gpsimd.affine_select(out=B.low_expert[:, :], in_=B.same_expert[:, :], compare_op=ALU.is_gt, fill=0.0,
                                    base=0, pattern=[[1, P]], channel_multiplier=-1).then_inc(s["ints"], 1)

        @block.vector
        def _(dve):
            dve.wait_ge(s["ints"], 3 + GATE_BITS)
            nc.vector.tensor_scalar(B.int_a[:, :], B.int_a[:, :], 7, None, ALU.bitwise_and).then_inc(s["const"], 1)
            nc.vector.tensor_scalar(B.int_b[:, :], B.int_b[:, :], 7, None, ALU.bitwise_and).then_inc(s["const"], 1)
            dve.wait_ge(s["const"], 2)
            nc.vector.tensor_scalar(B.same_expert[:, :], B.int_a[:, :], 0.0, None, ALU.is_equal).then_inc(s["const"], 1)
            nc.vector.tensor_copy(B.own_expert[:, :], B.int_b[:, :]).then_inc(s["const"], 1)
            nc.vector.tensor_copy(B.gate_bits_f[:, :], B.gate_bits[:, :]).then_inc(s["const"], 1)
            dve.wait_ge(s["made"], 9)
            nc.vector.tensor_scalar(B.not_same_head[:, :], B.same_head[:, :], -1.0, -NEG, ALU.add, ALU.mult).then_inc(s["const"], 1)
            for n in range(4):
                dve.wait_ge(s["feat_psum"], n + 1)
                w, half = (B.wqf, B.wkf)[n // 2], n % 2
                nc.vector.tensor_copy(w[:, half * 512:half * 512 + 512], B.ps[:, n % 2, :]).then_inc(s["feat_sbuf"], 1)

        @block.scalar
        def _(act):
            act.wait_ge(s["zeroed"], 1)
            for rows, cap, parts in ((B.rows0, CAP0, 4), (B.rows1, CAP1, 2), (B.rows2, CAP2, 2)):
                n = EXPERTS * cap * D // P // parts
                flat = rows.rearrange("r d -> (r d)").rearrange("(p a) -> p a", p=P)
                for k in range(parts):
                    act.dma_start(flat[:, k * n:(k + 1) * n], B.zeros[:, 0:n]).then_inc(s["rows_zero"], 16)
            act.wait_ge(s["wt_psum"], 2)
            nc.scalar.activation(B.wqt[:, :, :], B.ps[:, 2, 0:256].rearrange("p (a b) -> p a b", a=2),
                                 ACT.Copy).then_inc(s["wt_sbuf"], 1)
            act.wait_ge(s["rows_zero"], 16 * 8)

        @block.tensor
        def _(pe):
            pe.wait_ge(s["w_in"], 16 * 11)
            pe.wait_ge(s["made"], 5)
            for n, w in enumerate((B.wq0, B.wk0)):
                nc.tensor.transpose(B.ps[:, 2, n * P:(n + 1) * P], w[:, :], B.ident[:, :]).then_inc(s["wt_psum"], 1)
            pe.wait_ge(s["wt_sbuf"], 1)
            pe.wait_ge(s["wf_ready"], 16 * HEADS)
            for n in range(4):
                if n >= 2:
                    pe.wait_ge(s["feat_sbuf"], n - 1)
                nc.tensor.matmul(B.ps[:, n % 2, :], B.wqt[:, n // 2, :], B.wf_diag[:, (n % 2) * 512:(n % 2) * 512 + 512],
                                 start=True, stop=True).then_inc(s["feat_psum"], 1)


def norm_and_route(nc, B, layer, cap, outs=None, choices=0, bias=None):
    ps_t, ps_log, ps_te, ps_col = B.ps[:, 0:2, :], B.ps[:, 2, 0:P], B.ps[:, 3, 0:P], B.ps[:, 4, :]
    ps_te2 = B.ps[:, 5, 0:P]
    with phase(nc, B, f"route{layer}", "link centred squared var rstd xn xt_psum xt logits shifted exp onehot te_psum counted "
                   "total loop_cnt loop_tot slots_te slots_tok in0 in1 in2 in3 w_squared w_summed w_rooted w_normed wt_psum "
                   "wt_sbuf") as (block, s):
        GROUPS, PER = 4, TILES // 4
        landed = (s["in0"], s["in1"], s["in2"], s["in3"])

        @block.scalar
        def _(act):
            def transposed(g):
                act.wait_ge(s["xt_psum"], g + 1)
                nc.scalar.activation(B.xn_t[:, g * 512:(g + 1) * 512], ps_t[:, g % 2, :], ACT.Copy).then_inc(s["xt"], 1)

            if layer == 3:
                mix_weights_act(nc, B, act, s)
            for g in range(GROUPS):
                act.wait_ge(s["centred"], g + 1)
                if g >= 2:
                    act.wait_ge(s["var"], g - 1)
                nc.scalar.activation(B.squares[:, g % 2, :], B.xn[:, g * PER:(g + 1) * PER, :].rearrange("p t d -> p (t d)"),
                                     ACT.Square).then_inc(s["squared"], 1)
                if g >= 1:
                    transposed(g - 1)
            transposed(GROUPS - 1)
            if layer < 3:
                act.wait_ge(s["shifted"], 1)
                nc.scalar.activation(B.r_exp[:, :, :], B.r_a[:, :, :], ACT.Exp).then_inc(s["exp"], 1)

        @block.gpsimd
        def _(pool):
            for t in range(TILES if choices else 0):
                for k in range(choices):
                    nc.gpsimd.indirect_dma_start(B.back[:, k, t, :], None, outs,
                                                 bass.IndirectOffsetOnAxis(ap=B.from_slot[:, k, t:t + 1], axis=0)).then_inc(landed[t // PER], 16)
            for g in range(GROUPS):
                pool.wait_ge(s["var"], g + 1)
                t = slice(g * PER, (g + 1) * PER)
                nc.gpsimd.tensor_tensor(B.rstd[:, t], B.variance[:, t], B.half_neg[:, 0:PER], ALU.pow).then_inc(s["rstd"], 1)

        @block.tensor
        def _(pe):
            def logits(g):
                pe.wait_ge(s["xt"], g + 1)
                for t in range(g * PER, (g + 1) * PER):
                    last = nc.tensor.matmul(ps_log[:, t * EXPERTS:(t + 1) * EXPERTS], B.xn_t[:, t * P:(t + 1) * P],
                                            B.router[:, layer, :], start=True, stop=True)
                last.then_inc(s["logits"], 1)

            if layer == 3:
                mix_weights_pe(nc, B, pe, s)
            for g in range(GROUPS):
                pe.wait_ge(s["xn"], g + 1)
                if g >= 2:
                    pe.wait_ge(s["xt"], g - 1)
                for j in range(PER):
                    last = nc.tensor.transpose(ps_t[:, g % 2, j * P:(j + 1) * P], B.xn[:, g * PER + j, :], B.ident[:, :])
                last.then_inc(s["xt_psum"], 1)
                if layer < 3 and g >= 1:
                    logits(g - 1)
            if layer == 3:
                return
            logits(GROUPS - 1)
            pe.wait_ge(s["onehot"], 1)
            nc.tensor.transpose(ps_te, B.r_choice[:, :, :].rearrange("p t e -> p (t e)"), B.ident[:, :]).then_inc(s["te_psum"], 1)
            if layer == 0:
                with pe.Fori(0, GATE_BITS) as n:
                    pe.wait_ge(s["loop_cnt"], n + 1)
                    nc.tensor.matmul(ps_col[:, 0:1], B.same_expert[:, :], B.c_count[:, :], start=True,
                                     stop=True).then_inc(s["loop_tot"], 1)
                pe.wait_ge(s["counted"], 1)
                nc.tensor.matmul(ps_col[:, 1:2], B.same_expert[:, :], B.c_above[:, :], start=True, stop=True).then_inc(s["total"], 1)
                pe.wait_ge(s["counted"], 2)
                nc.tensor.matmul(ps_col[:, 2:3], B.low_expert[:, :], B.c_ties[:, :], start=True, stop=True).then_inc(s["total"], 1)
            k = 2 if layer == 0 else 0
            pe.wait_ge(s["counted"], k + 1)
            nc.tensor.matmul(ps_col[:, 3:4], B.low_expert[:, :], B.c_kept[:, :], start=True, stop=True).then_inc(s["total"], 1)
            pe.wait_ge(s["slots_te"], 1)
            nc.tensor.transpose(ps_te2, B.te_slot[:, :], B.ident[:, :]).then_inc(s["slots_tok"], 1)

        @block.vector
        def _(dve):
            n_link = [0]

            def link(ins):
                n_link[0] += 1
                ins.then_inc(s["link"], 1)
                dve.wait_ge(s["link"], n_link[0])

            def group(g):
                return slice(g * PER, (g + 1) * PER)

            def combine(g):
                t = group(g)
                dve.wait_ge(landed[g], 16 * PER * choices)
                for k in range(choices):
                    link(nc.vector.tensor_tensor(B.back[:, k, t, :], B.back[:, k, t, :], per_tile(B.gate[:, k, t], D), ALU.mult))
                    link(nc.vector.tensor_tensor(B.x_res[:, t, :], B.x_res[:, t, :], B.back[:, k, t, :], ALU.add))

            def centre(g):
                t = group(g)
                link(nc.vector.tensor_reduce(B.mean[:, t], B.x_res[:, t, :], AX.X, ALU.add))
                link(nc.vector.tensor_scalar(B.mean[:, t], B.mean[:, t], -1.0 / D, None, ALU.mult))
                nc.vector.tensor_tensor(B.xn[:, t, :], B.x_res[:, t, :], per_tile(B.mean[:, t], D), ALU.add).then_inc(s["centred"], 1)

            def spread(g):
                t = group(g)
                dve.wait_ge(s["squared"], g + 1)
                link(nc.vector.tensor_reduce(B.variance[:, t], B.squares[:, g % 2, :].rearrange("p (t d) -> p t d", d=D),
                                             AX.X, ALU.add))
                nc.vector.tensor_scalar(B.variance[:, t], B.variance[:, t], 1.0 / D, LN_EPS, ALU.mult, ALU.add).then_inc(s["var"], 1)

            def scale(g):
                t = group(g)
                dve.wait_ge(s["rstd"], g + 1)
                nc.vector.tensor_tensor(B.xn[:, t, :], B.xn[:, t, :], per_tile(B.rstd[:, t], D), ALU.mult).then_inc(s["xn"], 1)

            if bias is not None:
                link(nc.vector.tensor_tensor(B.x_res[:, :, :], B.x_res[:, :, :],
                                             bias[:, :].unsqueeze(1).to_broadcast([P, TILES, D]), ALU.add))
            if layer == 3:
                mix_weights_dve(nc, B, dve, s, link)
            for g in range(GROUPS + 2):
                if g < GROUPS:
                    if choices:
                        combine(g)
                    centre(g)
                if 1 <= g <= GROUPS:
                    spread(g - 1)
                if g >= 2:
                    scale(g - 2)
            if layer == 3:
                return

            def first_largest(choice, best, among):
                link(nc.vector.tensor_reduce(best, among, AX.X, ALU.max))
                link(nc.vector.tensor_tensor(B.r_a[:, :, :], among, per_tile(best, EXPERTS), ALU.is_equal))
                link(nc.vector.tensor_tensor(B.r_a[:, :, :], B.r_a[:, :, :], B.expert_m8[:, :, :], ALU.mult))
                link(nc.vector.tensor_reduce(B.v_a[:, :], B.r_a[:, :, :], AX.X, ALU.min))
                link(nc.vector.tensor_tensor(choice, B.expert_m8[:, :, :], per_tile(B.v_a[:, :], EXPERTS), ALU.is_equal))

            dve.wait_ge(s["logits"], GROUPS)
            lg = ps_log.rearrange("p (t e) -> p t e", e=EXPERTS)
            link(nc.vector.tensor_reduce(B.v_a[:, :], lg, AX.X, ALU.max))
            nc.vector.tensor_tensor(B.r_a[:, :, :], lg, per_tile(B.v_a[:, :], EXPERTS), ALU.subtract).then_inc(s["shifted"], 1)
            dve.wait_ge(s["exp"], 1)
            link(nc.vector.tensor_reduce(B.v_a[:, :], B.r_exp[:, :, :], AX.X, ALU.add))
            link(nc.vector.reciprocal(B.v_b[:, :], B.v_a[:, :]))
            link(nc.vector.tensor_tensor(B.r_prob[:, :, :], B.r_exp[:, :, :], per_tile(B.v_b[:, :], EXPERTS), ALU.mult))
            first_largest(B.r_one[:, 0], B.gate[:, 0, :], B.r_prob[:, :, :])
            te, keep, junk = B.te_val, B.te_keep, B.te_junk
            if layer == 0:
                link(nc.vector.scalar_tensor_tensor(out=B.r_exp[:, :, :], in0=B.r_one[:, 0], scalar=-2.0, in1=B.r_prob[:, :, :],
                                                    op0=ALU.mult, op1=ALU.add))
                first_largest(B.r_one[:, 1], B.gate[:, 1, :], B.r_exp[:, :, :])
                link(nc.vector.tensor_tensor(B.v_a[:, :], B.gate[:, 0, :], B.gate[:, 1, :], ALU.add))
                link(nc.vector.tensor_scalar(B.v_a[:, :], B.v_a[:, :], 1e-9, None, ALU.add))
                link(nc.vector.reciprocal(B.v_b[:, :], B.v_a[:, :]))
                for k in range(2):
                    link(nc.vector.tensor_tensor(B.gate[:, k, :], B.gate[:, k, :], B.v_b[:, :], ALU.mult))
                link(nc.vector.tensor_tensor(B.r_a[:, :, :], B.r_one[:, 0], per_tile(B.gate[:, 0, :], EXPERTS), ALU.mult))
                link(nc.vector.tensor_tensor(B.r_choice[:, :, :], B.r_one[:, 1], per_tile(B.gate[:, 1, :], EXPERTS), ALU.mult))
                nc.vector.tensor_tensor(B.r_choice[:, :, :], B.r_choice[:, :, :], B.r_a[:, :, :], ALU.add).then_inc(s["onehot"], 1)
                dve.wait_ge(s["te_psum"], 1)
                link(nc.vector.tensor_copy(te[:, :], ps_te))
                link(nc.vector.memset(B.thr[:, :], 0))
                base = n_link[0]
                with dve.Fori(0, GATE_BITS) as n:
                    bit = bass.ds(n, 1)
                    nc.vector.tensor_tensor(B.thr_try[:, :], B.thr[:, :], B.gate_bits[:, bit], ALU.bitwise_or).then_inc(s["link"], 1)
                    dve.wait_ge(s["link"], base + 3 * n + 1)
                    nc.vector.tensor_scalar(junk[:, :], te[:, :], B.thr_try[:, :].bitcast(F32), None, ALU.is_ge, ALU.add,
                                            accum_out=B.c_count[:, :]).then_inc(s["loop_cnt"], 1)
                    dve.wait_ge(s["loop_tot"], n + 1)
                    nc.vector.tensor_scalar(B.thr_add[:, :], ps_col[:, 0:1], float(cap), B.gate_bits_f[:, bit], ALU.is_ge,
                                            ALU.mult).then_inc(s["link"], 1)
                    dve.wait_ge(s["link"], base + 3 * n + 2)
                    nc.vector.tensor_tensor(B.thr[:, :], B.thr[:, :], B.thr_add[:, :], ALU.bitwise_or).then_inc(s["link"], 1)
                    dve.wait_ge(s["link"], base + 3 * n + 3)
                n_link[0] = base + 3 * GATE_BITS
                thr = B.thr[:, :].bitcast(F32)
                nc.vector.tensor_scalar(keep[:, :], te[:, :], thr, None, ALU.is_gt, ALU.add,
                                        accum_out=B.c_above[:, :]).then_inc(s["counted"], 1)
                link(nc.vector.tensor_scalar(B.te_tie[:, :], te[:, :], thr, None, ALU.is_equal))
                link(nc.vector.scalar_tensor_tensor(out=B.te_tie[:, :], in0=te[:, :], scalar=0.0, in1=B.te_tie[:, :],
                                                    op0=ALU.is_gt, op1=ALU.mult))
                nc.vector.tensor_reduce(B.c_ties[:, :], B.te_tie[:, :], AX.X, ALU.add).then_inc(s["counted"], 1)
                dve.wait_ge(s["total"], 2)
                link(nc.vector.tensor_scalar(B.c_room[:, :], ps_col[:, 1:2], -1.0, float(cap), ALU.mult, ALU.add))
                link(nc.vector.tensor_copy(B.c_start[:, :], ps_col[:, 2:3]))
                link(nc.vector.tensor_tensor_scan(B.te_rank[:, :], B.ones[:, :], B.te_tie[:, :], B.c_start[:, :],
                                                  ALU.mult, ALU.add))
                link(nc.vector.scalar_tensor_tensor(out=B.te_tie[:, :], in0=B.te_rank[:, :], scalar=B.c_room[:, :],
                                                    in1=B.te_tie[:, :], op0=ALU.is_le, op1=ALU.mult))
                link(nc.vector.tensor_tensor(keep[:, :], keep[:, :], B.te_tie[:, :], ALU.add))
            else:
                link(nc.vector.tensor_copy(B.r_choice[:, :, :], B.r_one[:, 0]))
                nc.vector.memset(B.thr[:, :], 0).then_inc(s["onehot"], 1)
                dve.wait_ge(s["te_psum"], 1)
                link(nc.vector.tensor_copy(keep[:, :], ps_te))
            nc.vector.tensor_reduce(B.c_kept[:, :], keep[:, :], AX.X, ALU.add).then_inc(s["counted"], 1)
            dve.wait_ge(s["total"], 3 if layer == 0 else 1)
            link(nc.vector.tensor_copy(B.c_start[:, :], ps_col[:, 3:4]))
            link(nc.vector.tensor_tensor_scan(B.te_rank[:, :], B.ones[:, :], keep[:, :], B.c_start[:, :], ALU.mult, ALU.add))
            if layer > 0:
                link(nc.vector.scalar_tensor_tensor(out=keep[:, :], in0=B.te_rank[:, :], scalar=float(cap), in1=keep[:, :],
                                                    op0=ALU.is_le, op1=ALU.mult))
            link(nc.vector.tensor_scalar(B.c_room[:, :], B.own_expert[:, :], float(cap), None, ALU.mult))
            nc.vector.scalar_tensor_tensor(out=B.te_slot[:, :], in0=B.te_rank[:, :], scalar=B.c_room[:, :], in1=keep[:, :],
                                           op0=ALU.add, op1=ALU.mult).then_inc(s["slots_te"], 1)
            dve.wait_ge(s["slots_tok"], 1)
            for k in range(2 if layer == 0 else 1):
                link(nc.vector.tensor_tensor(B.r_a[:, :, :], ps_te2.rearrange("p (t e) -> p t e", e=EXPERTS), B.r_one[:, k], ALU.mult))
                link(nc.vector.tensor_reduce(B.v_a[:, :], B.r_a[:, :, :], AX.X, ALU.add))
                link(nc.vector.scalar_tensor_tensor(out=B.gate[:, k, :], in0=B.v_a[:, :], scalar=0.0, in1=B.gate[:, k, :],
                                                    op0=ALU.is_gt, op1=ALU.mult))
                link(nc.vector.tensor_scalar(B.v_b[:, :], B.v_a[:, :], 0.0, float(PAD_SLOT), ALU.is_equal, ALU.mult))
                link(nc.vector.scalar_tensor_tensor(out=B.to_slot[:, k, :], in0=B.v_a[:, :], scalar=-1.0, in1=B.v_b[:, :],
                                                    op0=ALU.add, op1=ALU.add))
                link(nc.vector.tensor_scalar(B.from_slot[:, k, :], B.v_a[:, :], -1.0, 0.0, ALU.add, ALU.max))


def scatter_rows(nc, pool, B, rows, choices, total, done):
    for k in range(choices):
        for t in range(TILES):
            nc.gpsimd.indirect_dma_start(rows, bass.IndirectOffsetOnAxis(ap=B.to_slot[:, k, t:t + 1], axis=0),
                                         B.xn[:, t, :], None, bounds_check=total - 1, oob_is_err=False).then_inc(done, 16)
    pool.wait_ge(done, 16 * choices * TILES)


def linear_attention(nc, I, B):
    names = ("link scattered x_staged q_psum q_sbuf k_psum k_bias k_relu v_psum v_sbuf kv_psum kv_sbuf num_psum num_t nat_psum "
             "num_sbuf t_psum t_sbuf o_psum added w_next")
    ps = B.ps
    with phase(nc, B, "linear", names) as (block, s):

        @block.gpsimd
        def _(pool):
            scatter_rows(nc, pool, B, B.rows0, 2, EXPERTS * CAP0, s["scattered"])

        @block.scalar
        def _(act):
            def stage(b, buffer):
                act.nop()
                nc.scalar.activation(B.x_st[buffer], B.xn_t[:, bass.ds(b * SEQ, SEQ)], ACT.Copy).then_inc(s["x_staged"], 1)

            def q_features(b, buffer):
                for j in range(4):
                    act.wait_ge(s["q_psum"], 4 * b + j + 1)
                    nc.scalar.activation(B.qf[buffer][:, 2 * j:2 * j + 2, :].rearrange("p a b -> p (a b)"), ps[:, j % 2, :], ACT.Relu,
                                         bias=B.bf_col[:, :]).then_inc(s["q_sbuf"], 1)

            def k_features(b, buffer):
                for j in range(4):
                    act.wait_ge(s["k_bias"], 4 * b + j + 1)
                    v = B.kf[buffer][:, j // 2, (j % 2) * 512:(j % 2) * 512 + 512]
                    nc.scalar.activation(v, v, ACT.Relu).then_inc(s["k_relu"], 1)

            def output(b):
                act.wait_ge(s["t_psum"], b + 1)
                nc.scalar.activation(B.o_t[:, :, :].rearrange("p a b -> p (a b)"), ps[:, 7, 0:256], ACT.Copy).then_inc(s["t_sbuf"], 1)

            def step(b, k, more, tail):
                if more:
                    if tail:
                        act.wait_ge(s["v_psum"], b)
                    stage(b + 1, 1 - k)
                    q_features(b + 1, 1 - k)
                if tail:
                    output(b - 1)
                if more:
                    k_features(b + 1, 1 - k)
                act.wait_ge(s["num_psum"], b + 1)
                nc.scalar.activation(B.num_t[:, :], ps[:, 6, :], ACT.Copy).then_inc(s["num_t"], 1)

            stage(0, 0)
            q_features(0, 0)
            k_features(0, 0)
            step(0, 0, True, False)
            with act.Fori(0, BATCHES // 2 - 1) as i:
                for k in range(2):
                    step(2 * i + k + 1, 1 - k, True, True)
            step(BATCHES - 1, 1, False, True)
            output(BATCHES - 1)

        @block.tensor
        def _(pe):
            def q_features(b, buffer, first=False):
                pe.wait_ge(s["x_staged"], b + 1)
                for j in range(4):
                    if j >= 2 or not first:
                        pe.wait_ge(s["q_sbuf"], 4 * b + j - 1)
                    for i in range(2):
                        last = nc.tensor.matmul(ps[:, j % 2, i * SEQ:(i + 1) * SEQ], B.wqf[:, (2 * j + i) * P:(2 * j + i + 1) * P],
                                                B.x_st[buffer], start=True, stop=True)
                    last.then_inc(s["q_psum"], 1)

            def k_features(b, buffer, first=False):
                for j in range(4):
                    if j >= 2 or not first:
                        pe.wait_ge(s["k_bias"], 4 * b + j - 1)
                    nc.tensor.matmul(ps[:, 2 + j % 2, :], B.x_st[buffer][:, (j // 2) * P:(j // 2 + 1) * P],
                                     B.wkf[:, (j % 2) * 512:(j % 2) * 512 + 512], start=True, stop=True).then_inc(s["k_psum"], 1)

            def values(b, buffer, first=False):
                if not first:
                    pe.wait_ge(s["v_sbuf"], b)
                for t in range(2):
                    last = nc.tensor.matmul(ps[:, 5, 256 + t * P:256 + (t + 1) * P], B.x_st[buffer][:, t * P:(t + 1) * P], B.wv0[:, :],
                                            start=True, stop=True)
                last.then_inc(s["v_psum"], 1)

            def transpose_out(b, first=False):
                pe.wait_ge(s["num_sbuf"], b + 1)
                if not first:
                    pe.wait_ge(s["added"], b)
                for t in range(2):
                    last = nc.tensor.transpose(ps[:, 7, t * P:(t + 1) * P], B.o_nat[:, t, :], B.ident[:, :])
                last.then_inc(s["t_psum"], 1)

            def output(b):
                pe.wait_ge(s["t_sbuf"], b + 1)
                for t in range(2):
                    last = nc.tensor.matmul(ps[:, 7, 256 + t * P:256 + (t + 1) * P], B.o_t[:, t, :], B.wo0[:, :],
                                            start=True, stop=True)
                last.then_inc(s["o_psum"], 1)

            def step(b, k, more, tail, tail_first=False):
                if more:
                    q_features(b + 1, 1 - k)
                pe.wait_ge(s["v_sbuf"], b + 1)
                pe.wait_ge(s["k_relu"], 4 * b + 4)
                for p in range(PAIRS):
                    for t in range(2):
                        last = nc.tensor.matmul(ps[:, 5, 18 * p:18 * p + 18], B.kf[k][:, t, p * P:(p + 1) * P],
                                                B.va[k][:, t, 2 * p:2 * p + 2, :].rearrange("p a b -> p (a b)"),
                                                start=t == 0, stop=t == 1)
                last.then_inc(s["kv_psum"], 1)
                if tail:
                    transpose_out(b - 1, tail_first)
                if more:
                    k_features(b + 1, 1 - k)
                if tail:
                    output(b - 1)
                pe.wait_ge(s["kv_sbuf"], 2 * b + 2)
                pe.wait_ge(s["q_sbuf"], 4 * b + 4)
                if tail:
                    pe.wait_ge(s["num_t"], b)
                for p in range(PAIRS):
                    row, half = 32 * (p % 4), p // 4
                    last = nc.tensor.matmul(ps[row:row + 32, 6, half * SEQ:(half + 1) * SEQ], B.kv0[:, p, :], B.qf[k][:, p, :],
                                            start=True, stop=True, tile_position=(0, row))
                last.then_inc(s["num_psum"], 1)
                if more:
                    values(b + 1, 1 - k)
                pe.wait_ge(s["num_t"], b + 1)
                if tail:
                    pe.wait_ge(s["num_sbuf"], b)
                for t in range(2):
                    for half in range(2):
                        last = nc.tensor.transpose(ps[:, 4, t * 256 + half * P:t * 256 + (half + 1) * P],
                                                   B.num_t[:, half * SEQ + t * P:half * SEQ + (t + 1) * P], B.ident[:, :])
                last.then_inc(s["nat_psum"], 1)

            q_features(0, 0, first=True)
            k_features(0, 0, first=True)
            values(0, 0, first=True)
            step(0, 0, True, False)
            with pe.Fori(0, BATCHES // 2 - 1) as i:
                for k in range(2):
                    step(2 * i + k + 1, 1 - k, True, True)
            step(BATCHES - 1, 1, False, True)
            transpose_out(BATCHES - 1)
            output(BATCHES - 1)

        @block.vector
        def _(dve):
            def k_bias(b, buffer):
                for j in range(4):
                    dve.wait_ge(s["k_psum"], 4 * b + j + 1)
                    nc.vector.tensor_tensor(B.kf[buffer][:, j // 2, (j % 2) * 512:(j % 2) * 512 + 512].rearrange("p (h f) -> p h f", f=FEAT),
                                            ps[:, 2 + j % 2, :].rearrange("p (h f) -> p h f", f=FEAT),
                                            B.bf_row[:, :].unsqueeze(1).to_broadcast([P, 8, FEAT]), ALU.add).then_inc(s["k_bias"], 1)

            def v_copy(b, buffer):
                dve.wait_ge(s["v_psum"], b + 1)
                nc.vector.tensor_copy(B.va[buffer][:, :, :, 0:8],
                                      ps[:, 5, 256:512].rearrange("p (t h d) -> p t h d", t=2, d=8)).then_inc(s["v_sbuf"], 1)

            def divide(b):
                dve.wait_ge(s["nat_psum"], b + 1)
                num = ps[:, 4, :].rearrange("p (a r) -> p a r", r=32)[:, :, 0:18].rearrange("p a (h c) -> p a h c", c=9)
                den = B.den[:, :].rearrange("p (a h) -> p a h", h=2)
                nc.vector.tensor_scalar(den, num[:, :, :, 8], 1e-6, None, ALU.max).then_inc(s["link"], 1)
                dve.wait_ge(s["link"], 2 * b + 1)
                nc.vector.reciprocal(B.den[:, :], B.den[:, :]).then_inc(s["link"], 1)
                dve.wait_ge(s["link"], 2 * b + 2)
                nc.vector.tensor_tensor(B.o_nat[:, :, :].rearrange("p t (a h d) -> p (t a) h d", h=2, d=8), num[:, :, :, 0:8],
                                        den.unsqueeze(3).to_broadcast([P, 2 * PAIRS, 2, 8]), ALU.mult).then_inc(s["num_sbuf"], 1)

            def add(b):
                dve.wait_ge(s["o_psum"], b + 1)
                xb = B.x_res[:, bass.ds(2 * b, 2), :]
                nc.vector.tensor_tensor(xb, xb, ps[:, 7, 256:512].rearrange("p (t d) -> p t d", d=D), ALU.add).then_inc(s["added"], 1)

            def step(b, k, more, tail):
                if tail:
                    divide(b - 1)
                dve.wait_ge(s["kv_psum"], b + 1)
                kv = ps[:, 5, 0:144].rearrange("p (a c) -> p a c", c=18)
                nc.vector.tensor_copy(B.kv0[0:64, :, 0:9], kv[0:64, :, 0:9]).then_inc(s["kv_sbuf"], 1)
                nc.vector.tensor_copy(B.kv0[64:128, :, 9:18], kv[64:128, :, 9:18]).then_inc(s["kv_sbuf"], 1)
                if more:
                    k_bias(b + 1, 1 - k)
                if tail:
                    add(b - 1)
                if more:
                    v_copy(b + 1, 1 - k)

            k_bias(0, 0)
            v_copy(0, 0)
            step(0, 0, True, False)
            with dve.Fori(0, BATCHES // 2 - 1) as i:
                for k in range(2):
                    step(2 * i + k + 1, 1 - k, True, True)
            step(BATCHES - 1, 1, False, True)
            divide(BATCHES - 1)
            add(BATCHES - 1)

        @block.sync
        def _(sp):
            for dst, src in ((B.w_kv_down[:, :], I["L1_attn_w_kv_down"]), (B.w_q[:, :], I["L1_attn_w_q"]),
                             (B.w_kv_up[:, :], I["L1_attn_w_kv_up"]), (B.w_out[:, :, :], I["L1_attn_w_out"].rearrange("(c p) d -> p c d", p=P))):
                sp.dma_start(dst, src).then_inc(s["w_next"], 16)
            sp.wait_ge(s["w_next"], 16 * 4 + first_experts(I, B, sp, 0, s["w_next"]))


def latent_attention(nc, I, B):
    ps = B.ps
    G = HEADS // 2
    PIECES_A, PIECES_V = 9, 4
    names = ("scattered x_staged proj_psum proj_a v_psum proj_v s_psum maxed exped p_psum p_sbuf summed normed y_psum y_sbuf "
             "o_psum added w_next")
    with phase(nc, B, "latent", names) as (block, s):

        def score_bank(g, hh):
            return (g % 2) * 2 + hh

        @block.sync
        def _(sp):
            loads = [(B.wq2[:, :], I["L2_attn_Wq"]), (B.wk2[:, :], I["L2_attn_Wk"]), (B.bq2[:, :], columns(I["L2_attn_bq"])),
                     (B.bk2[:, :], columns(I["L2_attn_bk"])), (B.bk2_row[:, :], row_on_all(I["L2_attn_bk"])),
                     (B.gain[:, :], row_on_all(I["L3_attn_gain"]))]
            loads += [(B.w3[:, n, :], w) for n, w in enumerate((I["L3_attn_w_q"], I["L3_attn_w_k"], I["L3_attn_w_v"], I["L3_attn_w_o"],
                                                                I["L3_ffn_W_r"], I["L3_ffn_W_k"], I["L3_ffn_W_v"]))]
            loads += [(B.mu[:, 0:1], columns(I["L3_ffn_mu_r"])), (B.mu[:, 1:2], columns(I["L3_ffn_mu_k"]))]
            for dst, src in loads:
                sp.dma_start(dst, src).then_inc(s["w_next"], 16)
            sp.wait_ge(s["w_next"], 16 * len(loads) + first_experts(I, B, sp, 1, s["w_next"]))

        @block.gpsimd
        def _(pool):
            scatter_rows(nc, pool, B, B.rows1, 1, EXPERTS * CAP1, s["scattered"])

        @block.tensor
        def _(pe):
            def projection(b, piece, parts):
                if piece >= 4:
                    pe.wait_ge(s["proj_a"], PIECES_A * b + piece - 3)
                bank = piece % 4
                for lo, hi, w, x in parts:
                    last = nc.tensor.matmul(ps[:, bank, lo:hi], w, x, start=True, stop=True)
                last.then_inc(s["proj_psum"], 1)

            def scores(b, g):
                n = G * b + g
                if g >= 2:
                    pe.wait_ge(s["exped"], n - 1)
                for hh in range(2):
                    rows = slice(HS * hh, HS * hh + HS)
                    bank = ps[:, score_bank(g, hh), :]
                    for q, lo, keys in ((1, 0, SEQ), (0, SEQ, P)):
                        nc.tensor.matmul(bank[:, lo:lo + keys], B.q_t[rows, g, q * P:(q + 1) * P], B.k_t[rows, g, 0:keys],
                                         start=q == 1, stop=False)
                    last = nc.tensor.matmul(bank[:, P:3 * P].rearrange("p (a k) -> p a k", a=2), B.ident_b[:, :],
                                            B.causal_b[:, :].unsqueeze(1).to_broadcast([P, 2, P]), start=False, stop=True)
                last.then_inc(s["s_psum"], 1)

            def transposes(b, g):
                n = G * b + g
                pe.wait_ge(s["normed"], n + 1)
                pe.wait_ge(s["p_sbuf"], n)
                if g == 0:
                    pe.wait_ge(s["proj_v"], PIECES_V * b + 2)
                for hh in range(2):
                    for j in range(3):
                        last = nc.tensor.transpose(ps[:, 4 + hh, j * P:(j + 1) * P], B.p_nat[:, g % 2, hh, j * P:(j + 1) * P],
                                                   B.ident[:, :])
                last.then_inc(s["p_psum"], 1)

            def values(b, g):
                n = G * b + g
                pe.wait_ge(s["p_sbuf"], n + 1)
                if g >= 2:
                    pe.wait_ge(s["y_sbuf"], n - 1)
                else:
                    pe.wait_ge(s["proj_v"], PIECES_V * (b + 1))
                for hh in range(2):
                    h = 2 * g + hh
                    y = ps[HS * hh:HS * hh + HS, 6 + g % 2, :]
                    p = B.p_t[:, g % 2, hh, :]
                    nc.tensor.matmul(y[:, 0:SEQ].rearrange("p (a q) -> p a q", a=2), B.v_nat[:, 0, h, :],
                                     p[:, 0:4 * P].rearrange("p (a q) -> p a q", a=4)[:, 0:3:2, :], start=True, stop=False)
                    last = nc.tensor.matmul(y[:, 0:P], B.v_nat[:, 1, h, :], p[:, P:2 * P], start=False, stop=True)
                last.then_inc(s["y_psum"], 1)

            def v_projection(b, c):
                t, half = c // 2, c % 2
                if c == 1:
                    pe.wait_ge(s["added"], b)
                nc.tensor.matmul(ps[:, 4 + c, :], B.latent[:, t * P:(t + 1) * P],
                                 B.w_kv_up[:, HEADS * HS + 512 * half:HEADS * HS + 512 * half + 512],
                                 start=True, stop=True).then_inc(s["v_psum"], 1)

            with pe.Fori(0, BATCHES) as b:
                pe.wait_ge(s["x_staged"], b + 1)
                pe.wait_ge(s["exped"], G * b)
                x = B.x_b[:, 0:SEQ]
                projection(b, 0, [(0, SEQ, B.w_kv_down[:, :], x)])
                for c in range(4):
                    projection(b, 1 + c, [(i * SEQ, (i + 1) * SEQ, B.w_q[:, (2 * c + i) * P:(2 * c + i + 1) * P], x)
                                          for i in range(2)])
                pe.wait_ge(s["proj_a"], PIECES_A * b + 1)
                for c in range(4):
                    projection(b, 5 + c, [(i * SEQ, (i + 1) * SEQ, B.w_kv_up[:, (2 * c + i) * P:(2 * c + i + 1) * P], B.latent[:, :])
                                          for i in range(2)])
                pe.wait_ge(s["proj_a"], PIECES_A * (b + 1))
                for g in range(G + LAG + 1):
                    if g < G:
                        scores(b, g)
                    if g < 3:
                        v_projection(b, g)
                    if LAG <= g < G + LAG:
                        transposes(b, g - LAG)
                    if g == 2:
                        v_projection(b, 3)
                    if g > LAG:
                        values(b, g - LAG - 1)
                for t in range(2):
                    for c in range(8):
                        pe.wait_ge(s["y_sbuf"], G * b + c + 1)
                        last = nc.tensor.matmul(ps[:, 5, t * P:(t + 1) * P], B.y_t[:, 1 - t, c, :], B.w_out[:, c, :],
                                                start=c == 0, stop=c == 7)
                last.then_inc(s["o_psum"], 1)

        @block.scalar
        def _(act):
            with act.Fori(0, BATCHES) as b:
                act.wait_ge(s["proj_psum"], PIECES_A * b)
                act.nop()
                nc.scalar.activation(B.x_b[:, 0:SEQ], B.xn_t[:, bass.ds(b * SEQ, SEQ)], ACT.Copy).then_inc(s["x_staged"], 1)
                act.wait_ge(s["proj_psum"], PIECES_A * b + 1)
                act.wait_ge(s["v_psum"], PIECES_V * b)
                nc.scalar.activation(B.latent[:, :], ps[:, 0, 0:SEQ], ACT.Copy).then_inc(s["proj_a"], 1)
                for piece in range(1, PIECES_A):
                    act.wait_ge(s["proj_psum"], PIECES_A * b + piece + 1)
                    dst, c, scale = (B.q_t, piece - 1, HS ** -0.5) if piece < 5 else (B.k_t, piece - 5, 1.0)
                    nc.scalar.activation(dst[:, 2 * c:2 * c + 2, :].rearrange("p a b -> p (a b)"), ps[:, piece % 4, :], ACT.Copy,
                                         scale=scale).then_inc(s["proj_a"], 1)
                for g in range(G + LAG + 1):
                    if g < G:
                        n = G * b + g
                        act.wait_ge(s["maxed"], n + 1)
                        if g >= 2:
                            act.wait_ge(s["p_psum"], n - 1)
                        for hh in range(2):
                            for q, lo, hi in ((1, 0, SEQ), (0, SEQ, 3 * P)):
                                last = nc.scalar.activation(B.p_nat[:, g % 2, hh, lo:hi], ps[:, score_bank(g, hh), lo:hi], ACT.Exp,
                                                            bias=B.neg_max[:, g % 2, q, hh:hh + 1],
                                                            accum_out=B.p_sum[:, g % 2, q, hh:hh + 1])
                        last.then_inc(s["exped"], 1)
                    if g > LAG:
                        k = g - LAG - 1
                        act.wait_ge(s["y_psum"], G * b + k + 1)
                        if k == 0:
                            act.wait_ge(s["o_psum"], b)
                        nc.scalar.activation(B.y_t[:, :, k, :], ps[:, 6 + k % 2, 0:SEQ].rearrange("p (t q) -> p t q", t=2),
                                             ACT.Copy).then_inc(s["y_sbuf"], 1)

        @block.vector
        def _(dve):
            def v_copy(b, c):
                t, half = c // 2, c % 2
                dve.wait_ge(s["v_psum"], PIECES_V * b + c + 1)
                nc.vector.tensor_copy(B.v_nat[:, t, 8 * half:8 * half + 8, :],
                                      ps[:, 4 + c, :].rearrange("p (h d) -> p h d", d=HS)).then_inc(s["proj_v"], 1)

            with dve.Fori(0, BATCHES) as b:
                for g in range(G + LAG):
                    if g < G:
                        n = G * b + g
                        dve.wait_ge(s["s_psum"], n + 1)
                        bank = ps[:, score_bank(g, 0):score_bank(g, 0) + 2, :]
                        nc.vector.tensor_reduce(B.neg_max[:, g % 2, 1, :], bank[:, :, 0:SEQ], AX.X, ALU.max, negate=True)
                        nc.vector.tensor_reduce(B.neg_max[:, g % 2, 0, :], bank[:, :, SEQ:3 * P], AX.X, ALU.max,
                                                negate=True).then_inc(s["maxed"], 1)
                    if g < 2:
                        v_copy(b, g)
                    if 1 <= g <= G:
                        k = g - 1
                        dve.wait_ge(s["exped"], G * b + k + 1)
                        nc.vector.reciprocal(B.p_sum[:, k % 2, :, :], B.p_sum[:, k % 2, :, :]).then_inc(s["summed"], 1)
                        dve.wait_ge(s["summed"], G * b + k + 1)
                        for hh in range(2):
                            for q, lo, hi in ((1, 0, SEQ), (0, SEQ, 3 * P)):
                                p = B.p_nat[:, k % 2, hh, lo:hi]
                                last = nc.vector.tensor_scalar(p, p, B.p_sum[:, k % 2, q, hh:hh + 1], None, ALU.mult)
                        last.then_inc(s["normed"], 1)
                    if g == 2:
                        v_copy(b, 2)
                    if LAG <= g < G + LAG:
                        k = g - LAG
                        dve.wait_ge(s["p_psum"], G * b + k + 1)
                        if k >= 2:
                            dve.wait_ge(s["y_psum"], G * b + k - 1)
                        nc.vector.tensor_copy(B.p_t[:, k % 2, :, 0:3 * P], ps[:, 4:6, 0:3 * P]).then_inc(s["p_sbuf"], 1)
                    if g == 2:
                        v_copy(b, 3)
                dve.wait_ge(s["o_psum"], b + 1)
                xb = B.x_res[:, bass.ds(2 * b, 2), :]
                nc.vector.tensor_tensor(xb, xb, ps[:, 5, 0:SEQ].rearrange("p (t d) -> p t d", d=D), ALU.add).then_inc(s["added"], 1)


def small_head_attention(nc, I, B):
    ps = B.ps
    G = HEADS // 2
    QUADS = HEADS // 4
    SCALE = float(D) ** -0.5
    ROWS = 9 * 8
    BACK = LAG + 3
    AT_QK, AT_V = LAG + 2, LAG + 1
    LOADS = 3 + 9
    names = ("link w_next scattered x_staged xv_staged qk_psum v_psum qk_sbuf split parts parts_out rows_in v_sbuf s_psum maxed exped p_psum p_sbuf "
             "y_psum y_sbuf n_psum y_norm added scaled v_zero v_one")
    with phase(nc, B, "small", names) as (block, s):

        def score_bank(g, hh):
            return (g % 2) * 2 + hh

        def batches(eng, step):
            step(0, 0, range(G), True, 2)
            with eng.Fori(0, 2) as i:
                for k in range(2):
                    step(2 * i + k + 1, 1 - k, range(G), False, 2)
            step(BATCHES - 3, 1, range(G), False, 2)
            step(BATCHES - 2, 0, range(G), False, 1)
            step(BATCHES - 1, 1, range(G + LAG + 2), False, 0)

        @block.sync
        def _(sp):
            def to_rows(b, k):
                sp.wait_ge(s["parts"], 2 * b + 2)
                sp.dma_start(B.parts_dram[0], B.parts[:, 0]).then_inc(s["parts_out"], 16)
                if not isinstance(b, int) or b >= 2:
                    sp.wait_ge(s["s_psum"], G * (b - 1))
                sp.dma_start(B.parts_dram[1], B.parts[:, 1]).then_inc(s["parts_out"], 16)
                sp.wait_ge(s["parts_out"], 32 * b + 32)
                for j in range(3):
                    sp.dma_start(B.q_rows[k][24 * j:24 * j + 24, :, :],
                                 B.parts_dram[0].rearrange("(h d) i q -> (d i) h q", d=8)).then_inc(s["rows_in"], 16)
                for j in range(3):
                    for i in range(3):
                        sp.dma_start(B.k_rows[k][24 * j + i:24 * j + 24:3, :, :],
                                     B.parts_dram[1][:, j, :].rearrange("(h d) q -> d h q", d=8)).then_inc(s["rows_in"], 16)

            to_rows(0, 0)
            to_rows(1, 1)
            weights = first_experts(I, B, sp, 2, s["w_next"])
            with sp.Fori(0, BATCHES // 2 - 1) as i:
                for k in range(2):
                    to_rows(2 * i + k + 2, k)
            sp.wait_ge(s["w_next"], weights)

        @block.gpsimd
        def _(pool):
            def split(b):
                pool.wait_ge(s["qk_sbuf"], 2 * b + 2)
                pool.wait_ge(s["rows_in"], 16 * LOADS * b)
                part = [B.parts[:, :, n, :] for n in range(3)]
                one = B.ones[:, 0:1].unsqueeze(2).to_broadcast([P, 2, SEQ])
                nc.gpsimd.tensor_tensor(part[0], B.qk2_t, one, ALU.mult).then_inc(s["split"], 1)
                pool.wait_ge(s["split"], 3 * b + 1)
                nc.gpsimd.tensor_tensor(B.qk2_rest, B.qk2_t, part[0], ALU.subtract).then_inc(s["split"], 1)
                pool.wait_ge(s["split"], 3 * b + 2)
                nc.gpsimd.tensor_tensor(part[1], B.qk2_rest, one, ALU.mult).then_inc(s["parts"], 1)
                pool.wait_ge(s["parts"], 2 * b + 1)
                nc.gpsimd.tensor_tensor(B.qk2_rest, B.qk2_rest, part[1], ALU.subtract).then_inc(s["split"], 1)
                pool.wait_ge(s["split"], 3 * b + 3)
                nc.gpsimd.tensor_tensor(part[2], B.qk2_rest, one, ALU.mult).then_inc(s["parts"], 1)

            for k in range(2):
                nc.gpsimd.memset(B.va2[k], 0.0).then_inc(s["v_zero"], 1)
            pool.wait_ge(s["v_zero"], 2)
            for k in range(2):
                nc.gpsimd.memset(B.va2[k][:, :, :, 8:9], 1.0).then_inc(s["v_one"], 1)
            split(0)
            split(1)
            scatter_rows(nc, pool, B, B.rows2, 1, EXPERTS * CAP2, s["scattered"])
            with pool.Fori(2, BATCHES) as b:
                split(b)

        @block.tensor
        def _(pe):
            def qk_projection(b):
                pe.wait_ge(s["x_staged"], b + 1)
                for n, w in enumerate((B.wq2, B.wk2)):
                    last = nc.tensor.matmul(ps[:, 7, n * SEQ:(n + 1) * SEQ], w[:, :], B.x_b[:, 0:SEQ], start=True, stop=True)
                last.then_inc(s["qk_psum"], 1)

            def v_projection(b):
                pe.wait_ge(s["xv_staged"], b + 1)
                for t in range(2):
                    last = nc.tensor.matmul(ps[:, 6, SEQ + t * P:SEQ + (t + 1) * P], B.x_v[:, t * P:(t + 1) * P], B.wk2[:, :],
                                            start=True, stop=True)
                last.then_inc(s["v_psum"], 1)

            def scores(b, k, g, first):
                if g >= 2 or not first:
                    pe.wait_ge(s["exped"], G * b + g - 1)
                for hh in range(2):
                    for q in range(2):
                        last = nc.tensor.matmul(ps[:, score_bank(g, hh), q * SEQ:(q + 1) * SEQ],
                                                B.q_rows[k][0:ROWS, 2 * g + hh, q * P:(q + 1) * P], B.k_rows[k][0:ROWS, 2 * g + hh, :],
                                                start=True, stop=True)
                last.then_inc(s["s_psum"], 1)

            def transposes(b, g):
                pe.wait_ge(s["exped"], G * b + g + 1)
                pe.wait_ge(s["p_sbuf"], G * b + g)
                for hh in range(2):
                    for j in range(4):
                        last = nc.tensor.transpose(ps[:, 4 + hh, j * P:(j + 1) * P], B.p_nat[:, g % 2, hh, j * P:(j + 1) * P],
                                                   B.ident[:, :])
                last.then_inc(s["p_psum"], 1)

            def values(b, k, g):
                va = B.va2[k if g >= 0 else 1 - k]
                pe.wait_ge(s["p_sbuf"], G * b + g + 1)
                if g % 2 == 0:
                    pe.wait_ge(s["y_sbuf"], QUADS * b + g // 2)
                for hh in range(2):
                    row = 32 * (2 * (g % 2) + hh)
                    p = B.p_t[:, g % 2, hh, :].rearrange("p (a q) -> p a q", a=4)
                    for t in range(2):
                        last = nc.tensor.matmul(ps[row:row + 32, 6, 0:SEQ].rearrange("p (a q) -> p a q", a=2),
                                                va[:, t, 2 * (g % G) + hh, :], p[:, t:4:2, :], start=t == 0, stop=t == 1,
                                                tile_position=(0, row))
                last.then_inc(s["y_psum"], 1)

            def back(b, quad):
                pe.wait_ge(s["y_sbuf"], QUADS * b + quad + 1)
                pe.wait_ge(s["y_norm"], QUADS * b + quad)
                for t in range(2):
                    last = nc.tensor.transpose(ps[:, 7, t * P:(t + 1) * P], B.yt2[:, t * P:(t + 1) * P], B.ident[:, :])
                last.then_inc(s["n_psum"], 1)

            def step(b, k, steps, first, following):
                pe.wait_ge(s["rows_in"], 16 * LOADS * (b + 1))
                for g in steps:
                    if g < G:
                        scores(b, k, g, first)
                    if g < G + LAG and (g >= LAG or not first):
                        transposes(b, g - LAG)
                    if (g - BACK) % 2 == 0 and (g >= BACK or not first):
                        if g == BACK and following >= 2:
                            pe.wait_ge(s["qk_sbuf"], 2 * b + 6)
                        back(b, (g - BACK) // 2)
                    if g == AT_V:
                        pe.wait_ge(s["v_sbuf"], b + 1)
                        if following >= 1:
                            pe.wait_ge(s["y_sbuf"], QUADS * b)
                            v_projection(b + 1)
                    if g == AT_QK and following >= 2:
                        pe.wait_ge(s["y_norm"], QUADS * b)
                        qk_projection(b + 2)
                    if g == AT_V + 2 and following >= 1:
                        pe.wait_ge(s["v_sbuf"], b + 2)
                    if g < G + LAG + 1 and (g > LAG or not first):
                        values(b, k, g - LAG - 1)

            pe.wait_ge(s["v_one"], 2)
            qk_projection(0)
            v_projection(0)
            pe.wait_ge(s["qk_sbuf"], 2)
            qk_projection(1)
            pe.wait_ge(s["qk_sbuf"], 4)
            batches(pe, step)

        @block.scalar
        def _(act):
            def stage(b):
                act.wait_ge(s["qk_psum"], b)
                act.nop()
                nc.scalar.activation(B.x_b[:, 0:SEQ], B.xn_t[:, bass.ds(b * SEQ, SEQ)], ACT.Copy).then_inc(s["x_staged"], 1)

            def stage_v(b):
                act.wait_ge(s["scaled"], 1)
                act.wait_ge(s["v_psum"], b)
                nc.scalar.activation(B.x_v, B.xn_t[:, bass.ds(b * SEQ, SEQ)], ACT.Copy).then_inc(s["xv_staged"], 1)

            def biased(b):
                act.wait_ge(s["qk_psum"], b + 1)
                act.wait_ge(s["parts"], 2 * b)
                nc.scalar.activation(B.qk2_t[:, 0, :], ps[:, 7, 0:SEQ], ACT.Identity, bias=B.bq2_scaled[:, :], scale=SCALE).then_inc(s["qk_sbuf"], 1)
                nc.scalar.activation(B.qk2_t[:, 1, :], ps[:, 7, SEQ:2 * SEQ], ACT.Identity, bias=B.bk2[:, :]).then_inc(s["qk_sbuf"], 1)

            def step(b, k, steps, first, following):
                for g in steps:
                    n = g - LAG - 1
                    if n % 2 == 1 and n < G and (n >= 0 or not first):
                        act.wait_ge(s["y_psum"], G * b + n + 1)
                        act.wait_ge(s["n_psum"], QUADS * b + n // 2)
                        nc.scalar.activation(B.yt2[:, :], ps[:, 6, 0:SEQ], ACT.Copy).then_inc(s["y_sbuf"], 1)
                    if g == AT_QK and following >= 2:
                        biased(b + 2)
                    if g < G:
                        act.wait_ge(s["maxed"], G * b + g + 1)
                        if g >= 2 or not first:
                            act.wait_ge(s["p_psum"], G * b + g - 1)
                        for hh in range(2):
                            for q in range(2):
                                last = nc.scalar.activation(B.p_nat[:, g % 2, hh, q * SEQ:(q + 1) * SEQ],
                                                            ps[:, score_bank(g, hh), q * SEQ:(q + 1) * SEQ], ACT.Exp,
                                                            bias=B.neg_max2[:, g % 2, 2 * hh + q:2 * hh + q + 1])
                        last.then_inc(s["exped"], 1)
                    if g == 0 and following >= 1:
                        stage_v(b + 1)
                    if g == 1 and following >= 2:
                        stage(b + 2)

            act.wait_ge(s["scaled"], 1)
            stage(0)
            stage_v(0)
            biased(0)
            stage(1)
            biased(1)
            batches(act, step)

        @block.vector
        def _(dve):
            def v_biased(b, k):
                dve.wait_ge(s["v_psum"], b + 1)
                nc.vector.tensor_tensor(B.va2[k][:, :, :, 0:8], ps[:, 6, SEQ:2 * SEQ].rearrange("p (t h d) -> p t h d", t=2, d=8),
                                        B.bk2_row[:, :].rearrange("p (h d) -> p h d", d=8).unsqueeze(1).to_broadcast([P, 2, HEADS, 8]),
                                        ALU.add).then_inc(s["v_sbuf"], 1)

            def normalise(b, quad):
                dve.wait_ge(s["n_psum"], QUADS * b + quad + 1)
                y = ps[:, 7, 0:SEQ].rearrange("p (t h r) -> p t h r", t=2, r=32)
                dve.wait_ge(s["y_norm"], QUADS * b + quad)
                nc.vector.reciprocal(B.rden2[:, :, :], y[:, :, :, 8]).then_inc(s["link"], 1)
                dve.wait_ge(s["link"], QUADS * b + quad + 1)
                head = 4 * (quad % QUADS)
                nc.vector.tensor_tensor(B.o_nat[:, :, :].rearrange("p t (h d) -> p t h d", d=8)[:, :, head:head + 4, :],
                                        y[:, :, :, 0:8], B.rden2[:, :, :].unsqueeze(3).to_broadcast([P, 2, 4, 8]),
                                        ALU.mult).then_inc(s["y_norm"], 1)

            def add(b):
                dve.wait_ge(s["y_norm"], QUADS * (b + 1))
                xb = B.x_res[:, bass.ds(2 * b, 2), :]
                nc.vector.tensor_tensor(xb, xb, B.o_nat[:, :, :], ALU.add).then_inc(s["added"], 1)
                dve.wait_ge(s["added"], b + 1)

            def step(b, k, steps, first, following):
                for g in steps:
                    if g < G:
                        dve.wait_ge(s["s_psum"], G * b + g + 1)
                        bank = ps[:, score_bank(g, 0):score_bank(g, 0) + 2, :].rearrange("p a (q k) -> p (a q) k", k=SEQ)
                        nc.vector.tensor_reduce(B.neg_max2[:, g % 2, :], bank, AX.X, ALU.max, negate=True).then_inc(s["maxed"], 1)
                    if g < G + LAG and (g >= LAG or not first):
                        n = g - LAG
                        dve.wait_ge(s["p_psum"], G * b + n + 1)
                        if n >= 2 or not first:
                            dve.wait_ge(s["y_psum"], G * b + n - 1)
                        nc.vector.tensor_copy(B.p_t[:, n % 2, :, :], ps[:, 4:6, :]).then_inc(s["p_sbuf"], 1)
                    if g == AT_V + 2 and following >= 1:
                        dve.wait_ge(s["y_sbuf"], QUADS * b + 1)
                        v_biased(b + 1, 1 - k)
                    if (g - BACK) % 2 == 0 and (g >= BACK or not first):
                        quad = (g - BACK) // 2
                        normalise(b, quad)
                        if quad == -1:
                            add(b - 1)
                        if quad == QUADS - 1:
                            add(b)

            nc.vector.tensor_scalar(B.bq2_scaled[:, :], B.bq2[:, :], SCALE, None, ALU.mult).then_inc(s["scaled"], 1)
            dve.wait_ge(s["v_one"], 2)
            v_biased(0, 0)
            batches(dve, step)


def mix_weights_act(nc, B, act, s):
    for n in range(4):
        nc.scalar.activation(B.squares3[:, n * P:(n + 1) * P], B.w3[:, n, :], ACT.Square).then_inc(s["w_squared"], 1)
    act.wait_ge(s["w_summed"], 1)
    nc.scalar.activation(B.w_norm[:, :], B.w_norm[:, :], ACT.Sqrt, scale=1.0 / D).then_inc(s["w_rooted"], 1)
    for n in range(2):
        act.wait_ge(s["wt_psum"], n + 1)
        m = 4 if n == 0 else 3
        nc.scalar.activation(B.w3_t[:, 4 * n:4 * n + m, :].rearrange("p a b -> p (a b)"), B.ps[:, 6 + n, 0:m * P],
                             ACT.Copy).then_inc(s["wt_sbuf"], 1)


def mix_weights_dve(nc, B, dve, s, link):
    dve.wait_ge(s["w_squared"], 4)
    nc.vector.tensor_reduce(B.w_norm[:, :], B.squares3.rearrange("p (n d) -> p n d", d=D), AX.X, ALU.add).then_inc(s["w_summed"], 1)
    link(nc.vector.tensor_scalar(B.gain_s[:, :], B.gain[:, :], float(D) ** -0.5, None, ALU.mult))
    link(nc.vector.tensor_scalar(B.mu[:, 2:4], B.mu[:, 0:2], -1.0, 1.0, ALU.mult, ALU.add))
    link(nc.vector.memset(B.x_pair[:, :, 0:1], 0.0))
    dve.wait_ge(s["w_rooted"], 1)
    link(nc.vector.tensor_scalar(B.w_norm[:, :], B.w_norm[:, :], 1e-4, None, ALU.add))
    link(nc.vector.reciprocal(B.w_norm[:, :], B.w_norm[:, :]))
    link(nc.vector.tensor_scalar(B.w_norm[:, :], B.w_norm[:, :], B.gain_s[:, :], None, ALU.mult))
    nc.vector.tensor_tensor(B.w3[:, 0:4, :], B.w3[:, 0:4, :], per_tile(B.w_norm[:, :], D), ALU.mult).then_inc(s["w_normed"], 1)


def mix_weights_pe(nc, B, pe, s):
    pe.wait_ge(s["w_normed"], 1)
    for n in range(7):
        last = nc.tensor.transpose(B.ps[:, 6 + n // 4, (n % 4) * P:(n % 4 + 1) * P], B.w3[:, n, :], B.ident[:, :])
        if n in (3, 6):
            last.then_inc(s["wt_psum"], 1)


def channel_attention_and_mix(nc, B, out):
    ps = B.ps
    names = ("x_staged qk_psum squared kept summed rooted link qk_norm v_psum v_sbuf s_psum masked shifted exped a_ready at_psum "
             "at_sbuf ot_psum ot_sbuf out_psum mixed_pre mixed r_psum k_psum tanhed k_sq kv_psum gated res stored added")
    STEPS = BATCHES // 2
    WIDE = 2 * SEQ
    with phase(nc, B, "channel", names) as (block, s):

        @block.sync
        def _(sp):
            with sp.Fori(0, STEPS) as i:
                sp.wait_ge(s["added"], i + 1)
                sp.dma_start(out[bass.ds(2 * i, 2)].rearrange("a (t p) d -> p (a t) d", p=P),
                             B.x_res[:, bass.ds(4 * i, 4), :]).then_inc(s["stored"], 16)
            sp.wait_ge(s["stored"], 16 * STEPS)

        @block.gpsimd
        def _(pool):
            with pool.Fori(0, STEPS) as i:
                pool.wait_ge(s["x_staged"], STEPS + i + 1)
                pool.wait_ge(s["mixed"], 2 * i)
                for n in range(2):
                    nc.gpsimd.tensor_tensor(B.mix_pre[n], B.x_pair[:, :, 0:SEQ], B.mu[:, 2 + n:3 + n].unsqueeze(2).to_broadcast([P, 2, SEQ]),
                                            ALU.mult).then_inc(s["mixed_pre"], 1)

        @block.scalar
        def _(act):
            def stage(i):
                act.nop()
                nc.scalar.activation(B.x_pair[:, :, 1:SEQ + 1], B.xn_t[:, bass.ds(i * WIDE, WIDE)].rearrange("p (a q) -> p a q", a=2),
                                     ACT.Copy).then_inc(s["x_staged"], 1)

            with act.Fori(0, STEPS // 2) as half:
                for k in range(2):
                    i = 2 * half + k
                    act.wait_ge(s["qk_psum"], i)
                    stage(i)
                    act.wait_ge(s["qk_psum"], i + 1)
                    act.wait_ge(s["summed"], i)
                    nc.scalar.activation(B.squares[:, :, :], ps[:, 2 * k:2 * k + 2, :], ACT.Square).then_inc(s["squared"], 1)
            act.wait_ge(s["summed"], STEPS)
            nc.scalar.activation(B.qk_len[:, :], B.qk_len[:, :], ACT.Sqrt, scale=1.0 / 8).then_inc(s["rooted"], 1)

            def step(i, more):
                act.wait_ge(s["v_psum"], i + 1)
                act.wait_ge(s["ot_psum"], i)
                nc.scalar.activation(B.v3_t, ps[:, 0, :], ACT.Copy).then_inc(s["v_sbuf"], 1)
                if more:
                    act.wait_ge(s["mixed"], 2 * i + 2)
                    stage(i + 1)
                act.wait_ge(s["shifted"], i + 1)
                for a in range(2):
                    last = nc.scalar.activation(B.a_nat[:, a, :], B.a_nat[:, a, :], ACT.Exp, bias=B.a_max[:, a:a + 1], scale=SEQ ** -0.5,
                                                accum_out=B.a_sum[:, a:a + 1])
                last.then_inc(s["exped"], 1)
                act.wait_ge(s["r_psum"], i + 1)
                act.wait_ge(s["gated"], i)
                nc.scalar.activation(B.r_gate, ps[:, 2, :], ACT.Tanh, scale=0.5).then_inc(s["tanhed"], 1)
                act.wait_ge(s["at_psum"], i + 1)
                nc.scalar.activation(B.a_t[:, :, :], ps[:, 4, 0:2 * P].rearrange("p (a k) -> p a k", a=2), ACT.Copy).then_inc(s["at_sbuf"], 1)
                act.wait_ge(s["ot_psum"], i + 1)
                act.wait_ge(s["out_psum"], i)
                nc.scalar.activation(B.o3_t, ps[:, 6, :], ACT.Copy).then_inc(s["ot_sbuf"], 1)

            act.wait_ge(s["qk_psum"], STEPS)
            stage(0)
            with act.Fori(0, STEPS - 1) as i:
                step(i, True)
            step(STEPS - 1, False)

        @block.tensor
        def _(pe):
            with pe.Fori(0, STEPS // 2) as half:
                for k in range(2):
                    pe.wait_ge(s["x_staged"], 2 * half + k + 1)
                    pe.wait_ge(s["kept"], 2 * half)
                    pe.wait_ge(s["squared"], 2 * half)
                    for t in range(4):
                        last = nc.tensor.matmul(ps[:, 2 * k + t // 2, (t % 2) * SEQ:(t % 2 + 1) * SEQ],
                                                B.x_pair[:, t // 2, 1 + (t % 2) * P:1 + (t % 2 + 1) * P],
                                                B.w3_t[:, 0:2, :].rearrange("p a b -> p (a b)"), start=True, stop=True)
                    last.then_inc(s["qk_psum"], 1)
            def values(i):
                pe.wait_ge(s["x_staged"], STEPS + i + 1)
                pe.wait_ge(s["v_sbuf"], i)
                nc.tensor.matmul(ps[:, 0, :].rearrange("p (a q) -> p a q", a=2), B.w3_t[:, 2, :], B.x_pair[:, :, 1:SEQ + 1],
                                 start=True, stop=True).then_inc(s["v_psum"], 1)

            def scores(i):
                pe.wait_ge(s["qk_norm"], i + 1)
                pe.wait_ge(s["masked"], i)
                for a in range(2):
                    for t in range(2):
                        qk = B.qk[:, 2 * a + t, :]
                        last = nc.tensor.matmul(ps[:, 1, a * P:(a + 1) * P], qk[:, 0:P], qk[:, P:2 * P], start=t == 0, stop=t == 1)
                last.then_inc(s["s_psum"], 1)

            def step(i, more):
                pe.wait_ge(s["mixed"], 2 * i + 2)
                pe.wait_ge(s["tanhed"], i)
                mix_r = B.mix[0].rearrange("p a q -> p (a q)")
                for t in range(4):
                    last = nc.tensor.matmul(ps[:, 2, t * P:(t + 1) * P], mix_r[:, t * P:(t + 1) * P], B.w3_t[:, 4, :],
                                            start=True, stop=True)
                last.then_inc(s["r_psum"], 1)
                pe.wait_ge(s["k_sq"], i)
                nc.tensor.matmul(ps[:, 3, :], B.w3_t[:, 5, :], B.mix[1].rearrange("p a q -> p (a q)"), start=True,
                                 stop=True).then_inc(s["k_psum"], 1)
                pe.wait_ge(s["a_ready"], i + 1)
                pe.wait_ge(s["at_sbuf"], i)
                for a in range(2):
                    last = nc.tensor.transpose(ps[:, 4, a * P:(a + 1) * P], B.a_nat[:, a, :], B.ident[:, :])
                last.then_inc(s["at_psum"], 1)
                pe.wait_ge(s["k_sq"], i + 1)
                pe.wait_ge(s["gated"], i)
                for t in range(4):
                    last = nc.tensor.matmul(ps[:, 5, t * P:(t + 1) * P], B.k_act[:, t * P:(t + 1) * P], B.w3_t[:, 6, :],
                                            start=True, stop=True)
                last.then_inc(s["kv_psum"], 1)
                if more:
                    values(i + 1)
                pe.wait_ge(s["at_sbuf"], i + 1)
                pe.wait_ge(s["v_sbuf"], i + 1)
                pe.wait_ge(s["ot_sbuf"], i)
                for a in range(2):
                    last = nc.tensor.matmul(ps[:, 6, a * SEQ:(a + 1) * SEQ], B.a_t[:, a, :], B.v3_t[:, a * SEQ:(a + 1) * SEQ],
                                            start=True, stop=True)
                last.then_inc(s["ot_psum"], 1)
                if more:
                    scores(i + 1)
                pe.wait_ge(s["ot_sbuf"], i + 1)
                pe.wait_ge(s["res"], i)
                for t in range(4):
                    last = nc.tensor.matmul(ps[:, 7, t * P:(t + 1) * P], B.o3_t[:, t * P:(t + 1) * P], B.w3_t[:, 3, :],
                                            start=True, stop=True)
                last.then_inc(s["out_psum"], 1)

            pe.wait_ge(s["kept"], STEPS)
            values(0)
            scores(0)
            with pe.Fori(0, STEPS - 1) as i:
                step(i, True)
            step(STEPS - 1, False)

        @block.vector
        def _(dve):
            HALF = float(0.5 / np.sqrt(0.5))
            HEAD_LENS = 4 * 2 * HEADS
            with dve.Fori(0, STEPS // 2) as half:
                for k in range(2):
                    i = 2 * half + k
                    dve.wait_ge(s["squared"], i + 1)
                    nc.vector.tensor_reduce(B.qk_len[:, bass.ds(i * HEAD_LENS, HEAD_LENS)],
                                            B.squares[:, :, :].rearrange("p a (h d) -> p (a h) d", d=8), AX.X, ALU.add).then_inc(s["summed"], 1)
                    nc.vector.tensor_copy(B.qk_all[:, bass.ds(2 * i, 2), :], ps[:, 2 * k:2 * k + 2, :]).then_inc(s["kept"], 1)
            dve.wait_ge(s["rooted"], 1)
            nc.vector.tensor_scalar(B.qk_len[:, :], B.qk_len[:, :], 1e-4, None, ALU.add).then_inc(s["link"], 1)
            dve.wait_ge(s["link"], 1)
            nc.vector.reciprocal(B.qk_len[:, :], B.qk_len[:, :]).then_inc(s["link"], 1)
            dve.wait_ge(s["link"], 2)

            def prepare(i):
                dve.wait_ge(s["s_psum"], i)
                nc.vector.tensor_tensor(B.qk[:, :, :].rearrange("p t (h d) -> p (t h) d", d=8),
                                        B.qk_all[:, bass.ds(2 * i, 2), :].rearrange("p t (h d) -> p (t h) d", d=8),
                                        per_tile(B.qk_len[:, bass.ds(i * HEAD_LENS, HEAD_LENS)], 8), ALU.mult).then_inc(s["qk_norm"], 1)
                for n in range(2):
                    dve.wait_ge(s["mixed_pre"], 2 * i + n + 1)
                    dve.wait_ge((s["r_psum"], s["k_psum"])[n], i)
                    nc.vector.scalar_tensor_tensor(out=B.mix[n], in0=B.x_pair[:, :, 1:SEQ + 1], scalar=B.mu[:, n:n + 1],
                                                   in1=B.mix_pre[n], op0=ALU.mult, op1=ALU.add).then_inc(s["mixed"], 1)

            def step(i, more):
                LINKS = 4
                n_link = [0]

                def link(ins, wait=True):
                    n_link[0] += 1
                    ins.then_inc(s["link"], 1)
                    if wait:
                        dve.wait_ge(s["link"], 2 + LINKS * i + n_link[0])

                dve.wait_ge(s["s_psum"], i + 1)
                dve.wait_ge(s["at_psum"], i)
                nc.vector.tensor_tensor(B.a_nat[:, :, :], ps[:, 1, 0:2 * P].rearrange("p (a k) -> p a k", a=2),
                                        B.not_same_head[:, :].unsqueeze(1).to_broadcast([P, 2, P]), ALU.add).then_inc(s["masked"], 1)
                dve.wait_ge(s["masked"], i + 1)
                link(nc.vector.tensor_reduce(B.a_max[:, :], B.a_nat[:, :, :], AX.X, ALU.max))
                nc.vector.tensor_scalar(B.a_max[:, :], B.a_max[:, :], -SEQ ** -0.5, None, ALU.mult).then_inc(s["shifted"], 1)
                dve.wait_ge(s["k_psum"], i + 1)
                dve.wait_ge(s["kv_psum"], i)
                link(nc.vector.tensor_scalar(B.k_act, ps[:, 3, :], 0.0, None, ALU.max), wait=False)
                dve.wait_ge(s["exped"], i + 1)
                link(nc.vector.reciprocal(B.a_sum[:, :], B.a_sum[:, :]))
                nc.vector.tensor_tensor(B.a_nat[:, :, :], B.a_nat[:, :, :], per_tile(B.a_sum[:, :], P), ALU.mult).then_inc(s["a_ready"], 1)
                nc.vector.tensor_tensor(B.k_act, B.k_act, B.k_act, ALU.mult).then_inc(s["k_sq"], 1)
                if more:
                    prepare(i + 1)
                dve.wait_ge(s["tanhed"], i + 1)
                dve.wait_ge(s["kv_psum"], i + 1)
                dve.wait_ge(s["added"], i)
                nc.vector.scalar_tensor_tensor(out=B.r_kv, in0=B.r_gate, scalar=1.0, in1=ps[:, 5, :], op0=ALU.add,
                                               op1=ALU.mult).then_inc(s["gated"], 1)
                xb, xn = B.x_res[:, bass.ds(4 * i, 4), :], B.xn[:, bass.ds(4 * i, 4), :]
                dve.wait_ge(s["out_psum"], i + 1)
                nc.vector.tensor_tensor(B.o3_nat, xn, ps[:, 7, :].rearrange("p (t d) -> p t d", d=D), ALU.add).then_inc(s["res"], 1)
                dve.wait_ge(s["res"], i + 1)
                link(nc.vector.scalar_tensor_tensor(out=B.o3_nat, in0=B.o3_nat, scalar=HALF, in1=xb, op0=ALU.mult, op1=ALU.add))
                dve.wait_ge(s["gated"], i + 1)
                nc.vector.scalar_tensor_tensor(out=xb, in0=B.r_kv.rearrange("p (t d) -> p t d", d=D), scalar=0.5, in1=B.o3_nat,
                                               op0=ALU.mult, op1=ALU.add).then_inc(s["added"], 1)
                assert n_link[0] == LINKS

            prepare(0)
            with dve.Fori(0, STEPS - 1) as i:
                step(i, True)
            step(STEPS - 1, False)


def expert_weights(I, layer):
    return {0: ((I["L0_ffn_gate_w"], I["L0_ffn_up_w"]), I["L0_ffn_down_w"], None, None),
            1: ((I["L1_ffn_W1"],), I["L1_ffn_W2"], I["L1_ffn_b1"], I["L1_ffn_b2"]),
            2: ((I["L2_ffn_w1"],), I["L2_ffn_w2"], I["L2_ffn_b1"], I["L2_ffn_b2"])}[layer]


def load_expert(I, B, sp, layer, e, k, done):
    up, down, _, _ = expert_weights(I, layer)
    for n, w in enumerate(up):
        sp.dma_start(B.w_up[:, k, n, :], w[bass.ds(e, 1)].rearrange("a d f -> d (a f)")).then_inc(done, 16)
    sp.dma_start(B.w_down[:, k, :, :], down[bass.ds(e, 1)].rearrange("a (c p) d -> p (a c) d", p=P)).then_inc(done, 16)


def first_experts(I, B, sp, layer, done):
    _, _, b_up, b_down = expert_weights(I, layer)
    for k in range(2):
        load_expert(I, B, sp, layer, k, k, done)
        if b_down is not None:
            sp.dma_start(B.b_down[:, k, :], b_down[bass.ds(k, 1)].broadcast_to([P, D])).then_inc(done, 16)
    if b_up is not None:
        sp.dma_start(B.b_rows[:, :], b_up.rearrange("e (c p) -> (e c) p", p=P)).then_inc(done, 16)
    return 16 * (6 if b_up is None else 7)


def experts(nc, I, B, layer, cap, rows_n, rows, outs):
    tiles = cap // rows_n
    gated = layer == 0
    half = cap // 2 if gated else cap
    names = ("w0 w1 xe0 xe1 b0 b1 xt_psum0 xt_psum1 xt h_psum h_act h y_psum0 y_psum1 y y_out0 y_out1 bt_psum bt bcol")
    ps = B.ps
    _, _, b_up, b_down = expert_weights(I, layer)
    n_w = 3 if gated else 2
    with phase(nc, B, f"experts{layer}", names) as (block, s):
        w_in, xe_in, b_in2 = (s["w0"], s["w1"]), (s["xe0"], s["xe1"]), (s["b0"], s["b1"])
        xt_psum, y_psum, y_out = (s["xt_psum0"], s["xt_psum1"]), (s["y_psum0"], s["y_psum1"]), (s["y_out0"], s["y_out1"])
        xt_view = ps[:, 0:2, :].rearrange("p a b -> p (a b)")
        y_view = ps[:, 6:8, :].rearrange("p a b -> p (a b)")
        steps = 8 if gated else 4
        TURNS = EXPERTS // 2

        def h_bank(m):
            return 2 + (m % 2) * 2 if gated else 2 + m

        @block.sync
        def _(sp):
            def rows_of(e, k):
                src = rows.rearrange("(e r) d -> e r d", e=EXPERTS)[bass.ds(e, 1)].rearrange("a (j p) d -> p (a j) d", p=rows_n)
                sp.dma_start(B.xe[0:rows_n, k, 0:tiles, :], src).then_inc(xe_in[k], 16)

            for k in range(2):
                rows_of(k, k)
            with sp.Fori(1, TURNS) as i:
                for k in range(2):
                    sp.wait_ge(xt_psum[k], i)
                    rows_of(2 * i + k, k)
                    sp.wait_ge(y_psum[k], i)
                    load_expert(I, B, sp, layer, 2 * i + k, k, w_in[k])
                    if not gated:
                        sp.wait_ge(y_out[k], 16 * i)
                        sp.dma_start(B.b_down[:, k, :], b_down[bass.ds(2 * i + k, 1)].broadcast_to([P, D])).then_inc(b_in2[k], 16)

        @block.tensor
        def _(pe):
            def transposes(i, k, first=False):
                pe.wait_ge(xe_in[k], 16 * i + 16)
                if not first:
                    pe.wait_ge(s["xt"], 2 * i + k)
                for j in range(tiles):
                    last = nc.tensor.transpose(xt_view[:, j * rows_n:(j + 1) * rows_n], B.xe[0:rows_n, k, j, :],
                                               B.ident[0:rows_n, 0:rows_n])
                last.then_inc(xt_psum[k], 1)

            def expert(i, k, more):
                n = 2 * i + k
                pe.wait_ge(s["xt"], n + 1)
                if not isinstance(i, int) or i > 0:
                    pe.wait_ge(w_in[k], 16 * n_w * i)
                for m in range(steps):
                    c, a = (m // 2, (m % 2) * half) if gated else (m, 0)
                    if gated and m >= 2:
                        pe.wait_ge(s["h"], steps * n + m - 1)
                    for g in range(2 if gated else 1):
                        last = nc.tensor.matmul(ps[:, h_bank(m) + g, 0:half], B.w_up[:, k, g, c * P:(c + 1) * P],
                                                B.xe_ts[k][:, a:a + half], start=True, stop=True)
                    last.then_inc(s["h_psum"], 1)
                if more:
                    transposes(i + k, 1 - k)
                pe.wait_ge(s["h"], steps * (n + 1))
                if k or not isinstance(i, int) or i > 0:
                    pe.wait_ge(s["y"], n)
                for j in range(tiles):
                    for c in range(FCH):
                        last = nc.tensor.matmul(y_view[0:rows_n, j * P:(j + 1) * P],
                                                B.h_t[:, c, j * rows_n:(j + 1) * rows_n], B.w_down[:, k, c, :],
                                                start=c == 0, stop=c == FCH - 1)
                last.then_inc(y_psum[k], 1)

            if not gated:
                nc.tensor.transpose(ps[:, 2, 0:EXPERTS * FCH], B.b_rows[:, :], B.ident[0:32, 0:32]).then_inc(s["bt_psum"], 1)
            transposes(0, 0, first=True)
            if not gated:
                pe.wait_ge(s["bt"], 1)
            with pe.Fori(0, TURNS - 1) as i:
                for k in range(2):
                    expert(i, k, True)
            expert(TURNS - 1, 0, True)
            expert(TURNS - 1, 1, False)

        @block.scalar
        def _(act):
            with act.Fori(0, TURNS) as i:
                for k in range(2):
                    n = 2 * i + k
                    if gated:
                        for m in range(steps):
                            act.wait_ge(s["h_psum"], steps * n + m + 1)
                            act.wait_ge(s["h"], steps * n + max(m - 1, 0))
                            nc.scalar.activation(B.h_gate[:, m % 2, 0:half], ps[:, h_bank(m), 0:half], ACT.Silu).then_inc(s["h_act"], 1)
                    else:
                        act.wait_ge(s["bcol"], n + 1)
                        act.wait_ge(y_psum[1 - k], i + k)
                        for m in range(steps):
                            act.wait_ge(s["h_psum"], steps * n + m + 1)
                            nc.scalar.activation(B.h_t[:, m, 0:cap], ps[:, h_bank(m), 0:cap], ACT.Gelu,
                                                 bias=B.b_up[:, k, m:m + 1]).then_inc(s["h"], 1)

        @block.vector
        def _(dve):
            def transposed(i, k):
                dve.wait_ge(xt_psum[k], i + 1)
                nc.vector.tensor_copy(B.xe_ts[k][:, 0:cap], xt_view[:, 0:cap]).then_inc(s["xt"], 1)

            def bias_columns(i, k):
                n = 2 * i + k
                if not isinstance(i, int) or i > 0:
                    dve.wait_ge(s["h"], steps * (n - 1))
                nc.vector.tensor_scalar(B.b_up[:, k, :], B.b_cols[:, bass.ds(n * FCH, FCH)], 0.0, None, ALU.add).then_inc(s["bcol"], 1)

            def expert(i, k, more):
                n = 2 * i + k
                if gated:
                    dve.wait_ge(y_psum[1 - k], i + k)
                    for m in range(steps):
                        c, a = m // 2, (m % 2) * half
                        dve.wait_ge(s["h_act"], steps * n + m + 1)
                        nc.vector.tensor_tensor(B.h_t[:, c, a:a + half], ps[:, h_bank(m) + 1, 0:half],
                                                B.h_gate[:, m % 2, 0:half], ALU.mult).then_inc(s["h"], 1)
                if more:
                    if not gated:
                        bias_columns(i + k, 1 - k)
                    transposed(i + k, 1 - k)
                dve.wait_ge(y_psum[k], i + 1)
                dve.wait_ge(y_out[k], 16 * i)
                src = y_view[0:rows_n, 0:tiles * P].rearrange("p (j d) -> p j d", d=P)
                if gated:
                    nc.vector.tensor_copy(B.ye[0:rows_n, k, 0:tiles, :], src).then_inc(s["y"], 1)
                else:
                    if not isinstance(i, int) or i > 0:
                        dve.wait_ge(b_in2[k], 16 * i)
                    nc.vector.tensor_tensor(B.ye[0:rows_n, k, 0:tiles, :], src,
                                            B.b_down[0:rows_n, k, :].unsqueeze(1).to_broadcast([rows_n, tiles, D]),
                                            ALU.add).then_inc(s["y"], 1)

            if not gated:
                dve.wait_ge(s["bt_psum"], 1)
                nc.vector.tensor_copy(B.b_cols[:, :], ps[:, 2, 0:EXPERTS * FCH]).then_inc(s["bt"], 1)
                dve.wait_ge(s["bt"], 1)
                bias_columns(0, 0)
            transposed(0, 0)
            with dve.Fori(0, TURNS - 1) as i:
                for k in range(2):
                    expert(i, k, True)
            expert(TURNS - 1, 0, True)
            expert(TURNS - 1, 1, False)

        @block.gpsimd
        def _(pool):
            with pool.Fori(0, TURNS) as i:
                for k in range(2):
                    n = 2 * i + k
                    pool.wait_ge(s["y"], n + 1)
                    pool.nop()
                    dst = outs.rearrange("(e r) d -> e r d", e=EXPERTS)[bass.ds(n, 1)].rearrange("a (j p) d -> p (a j) d", p=rows_n)
                    pool.dma_start(dst, B.ye[0:rows_n, k, 0:tiles, :]).then_inc(y_out[k], 16)
            for k in range(2):
                pool.wait_ge(y_out[k], 16 * TURNS)


class Buffers:
    pass


def build(nc, I, out):
    with ExitStack() as ctx:
        B = Buffers()
        B.used_semaphores = []

        def sb(name, shape, dt=F32):
            return ctx.enter_context(nc.sbuf_tensor(name, shape, dt))

        B.ps = ctx.enter_context(nc.psum_tensor("ps", [P, 8, 512], F32))
        B.x_res = sb("x_res", [P, TILES, D])
        B.xn = sb("xn", [P, TILES, D])
        B.xn_t = sb("xn_t", [P, TOKENS])
        B.ident = sb("ident", [P, P])
        B.ones = sb("ones", [P, P])
        B.same_head = sb("same_head", [P, P])
        B.not_same_head = sb("not_same_head", [P, P])
        B.same_expert = sb("same_expert", [P, P])
        B.low_expert = sb("low_expert", [P, P])
        B.bo_row = sb("bo_row", [P, P])
        B.te_val = sb("te_val", [P, P])
        B.te_keep = sb("te_keep", [P, P])
        B.te_junk = sb("te_junk", [P, P])
        B.te_tie = sb("te_tie", [P, P])
        B.te_rank = sb("te_rank", [P, P])
        B.te_slot = sb("te_slot", [P, P])
        B.wq0 = sb("wq0", [P, P])
        B.wk0 = sb("wk0", [P, P])
        B.wv0 = sb("wv0", [P, P])
        B.wo0 = sb("wo0", [P, P])
        B.ident_b = sb("ident_b", [P, P], BF16)
        B.causal_b = sb("causal_b", [P, P], BF16)
        B.router = sb("router", [P, 3, EXPERTS])
        B.bf_col = sb("bf_col", [P, 1])
        B.bf_row = sb("bf_row", [P, FEAT])
        B.wqf = sb("wqf", [P, HEADS * FEAT])
        B.wkf = sb("wkf", [P, HEADS * FEAT])
        B.wqt = sb("wqt", [P, 2, P])
        B.head_mask = sb("head_mask", [P, HEADS])
        B.expert_m8 = sb("expert_m8", [P, TILES, EXPERTS])
        B.r_a = sb("r_a", [P, TILES, EXPERTS])
        B.r_exp = sb("r_exp", [P, TILES, EXPERTS])
        B.r_prob = sb("r_prob", [P, TILES, EXPERTS])
        B.r_choice = sb("r_choice", [P, TILES, EXPERTS])
        B.r_one = sb("r_one", [P, 2, TILES, EXPERTS])
        B.int_a = sb("int_a", [P, P], I32)
        B.int_b = sb("int_b", [P, 1], I32)
        B.own_expert = sb("own_expert", [P, 1])
        B.gate_bits = sb("gate_bits", [P, GATE_BITS], I32)
        B.gate_bits_f = sb("gate_bits_f", [P, GATE_BITS])
        B.half_neg = sb("half_neg", [P, TILES])
        B.mean = sb("mean", [P, TILES])
        B.variance = sb("variance", [P, TILES])
        B.rstd = sb("rstd", [P, TILES])
        B.v_a = sb("v_a", [P, TILES])
        B.v_b = sb("v_b", [P, TILES])
        B.squares = sb("squares", [P, 2, 512])
        B.gate = sb("gate", [P, 2, TILES])
        B.to_slot = sb("to_slot", [P, 2, TILES], I32)
        B.from_slot = sb("from_slot", [P, 2, TILES], I32)
        B.c_count = sb("c_count", [P, 1])
        B.c_above = sb("c_above", [P, 1])
        B.c_ties = sb("c_ties", [P, 1])
        B.c_kept = sb("c_kept", [P, 1])
        B.c_room = sb("c_room", [P, 1])
        B.c_start = sb("c_start", [P, 1])
        B.thr = sb("thr", [P, 1], I32)
        B.thr_try = sb("thr_try", [P, 1], I32)
        B.thr_add = sb("thr_add", [P, 1], I32)
        B.x_b = sb("x_b", [P, SEQ + 1])
        B.va0 = sb("va0", [P, 2, HEADS, 9])
        B.kv0 = sb("kv0", [P, PAIRS, 32])
        B.den = sb("den", [P, 2 * HEADS])
        B.o_nat = sb("o_nat", [P, 2, D])
        B.o_t = sb("o_t", [P, 2, D])
        B.w_kv_down = sb("w_kv_down", [P, P])
        B.w_kv_up = sb("w_kv_up", [P, 2 * HEADS * HS])
        B.w_q = sb("w_q", [P, HEADS * HS])
        B.w_out = sb("w_out", [P, 8, D])
        B.latent = sb("latent", [P, SEQ])
        B.q_t = sb("q_t", [P, 8, SEQ])
        B.k_t = sb("k_t", [P, 8, SEQ])
        B.v_nat = sb("v_nat", [P, 2, HEADS, HS])
        B.neg_max = sb("neg_max", [P, 2, 2, 2])
        B.p_sum = sb("p_sum", [P, 2, 2, 2])
        B.p_nat = sb("p_nat", [P, 2, 2, 512])
        B.y_nat = sb("y_nat", [P, 2, HEADS * HS])
        B.y_t = sb("y_t", [P, 2, 8, P])
        B.p_t = sb("p_t", [P, 2, 2, 512])
        B.wq2 = sb("wq2", [P, P])
        B.wk2 = sb("wk2", [P, P])
        B.bk2_row = sb("bk2_row", [P, P])
        B.bq2 = sb("bq2", [P, 1])
        B.bk2 = sb("bk2", [P, 1])
        B.bq2_scaled = sb("bq2_scaled", [P, 1])
        B.q2_t = sb("q2_t", [P, SEQ])
        B.k2_t = sb("k2_t", [P, SEQ])
        B.neg_max2 = sb("neg_max2", [P, 2, 4])
        B.rden2 = sb("rden2", [P, 2, 4])
        B.gain = sb("gain", [P, 1])
        B.gain_s = sb("gain_s", [P, 1])
        B.w3 = sb("w3", [P, 7, D])
        B.w3_t = sb("w3_t", [P, 7, D])
        B.mu = sb("mu", [P, 4])
        B.w_norm = sb("w_norm", [P, 4])
        B.qk_len = sb("qk_len", [P, TILES * 2 * HEADS])
        B.qk = sb("qk", [P, 4, SEQ])
        B.a_nat = sb("a_nat", [P, 2, P])
        B.a_t = sb("a_t", [P, 2, P])
        B.a_max = sb("a_max", [P, 2])
        B.a_sum = sb("a_sum", [P, 2])
        B.xe = sb("xe", [P, 2, 5, D])
        B.xe_t = sb("xe_t", [P, CAP0])
        B.h_t = sb("h_t", [P, FCH, CAP0])
        B.h_gate = sb("h_gate", [P, 2, CAP0 // 2])
        B.w_up = sb("w_up", [P, 2, 2, FF])
        B.w_down = sb("w_down", [P, 2, FCH, D])
        B.ye = sb("ye", [P, 2, 5, D])
        B.b_rows = sb("b_rows", [EXPERTS * FCH, P])
        B.b_cols = sb("b_cols", [P, EXPERTS * FCH])
        B.b_up = sb("b_up", [P, 2, FCH])
        B.b_down = sb("b_down", [P, 2, D])
        arena = sb("arena", [P, 2 * TILES * D])
        B.qf = (arena[:, 0:PAIRS * SEQ].rearrange("p (a b) -> p a b", a=PAIRS), B.q_t)
        B.kf = (arena[:, PAIRS * SEQ:PAIRS * SEQ + 2 * HEADS * FEAT].rearrange("p (a b) -> p a b", a=2),
                B.k_t[:, :, :].rearrange("p a b -> p (a b)").rearrange("p (a b) -> p a b", a=2))
        B.va = (B.va0, B.v_nat[:, :, :, :].rearrange("p t h d -> p (t h d)")[:, 0:288].rearrange("p (t h d) -> p t h d", t=2, d=9))
        B.num_t = B.p_nat[:, 0, 0, :]
        B.xe_ts = (B.xe_t[:, :], B.y_t[:, 0, 0:5, :].rearrange("p a b -> p (a b)"))
        B.x_st = (B.x_b[:, 0:SEQ], B.latent[:, :])
        halves = (arena[:, 0:TILES * D], arena[:, TILES * D:2 * TILES * D])
        B.q_rows = tuple(t.bitcast(BF16).rearrange("p (h q) -> p h q", h=HEADS) for t in halves)
        B.k_rows = tuple(t[:, :, :].rearrange("p a b -> p (a b)").bitcast(BF16).rearrange("p (h q) -> p h q", h=HEADS)
                         for t in (B.q_t, B.k_t))
        B.x_v = B.v_nat[:, 1, 0:4, :].rearrange("p h d -> p (h d)")
        B.qk2_t = B.y_nat[:, 0, 0:512].rearrange("p (a q) -> p a q", a=2)
        B.qk2_rest = B.y_nat[:, 0, 512:1024].rearrange("p (a q) -> p a q", a=2)
        B.parts = B.y_nat[:, 1, 0:768].bitcast(BF16).rearrange("p (a i q) -> p a i q", a=2, i=3)
        B.parts_dram = nc.dram_tensor("parts", [2, P, 3, SEQ], BF16, kind="Internal").ap()
        B.back = arena[:, :].rearrange("p (k t d) -> p k t d", k=2, t=TILES)
        B.va2 = tuple(t[:, 0:2 * HEADS * 32].rearrange("p (t h c) -> p t h c", t=2, c=32) for t in (B.w_q, B.w_kv_up))
        B.yt2 = B.latent
        queries, keys, values = (t.rearrange("p a b -> p (a b)") for t in (B.q_t[:, :, :], B.k_t[:, :, :],
                                                                         B.v_nat[:, :, :, :].rearrange("p t h d -> p t (h d)")))
        pair = lambda ap: ap.rearrange("p (a q) -> p a q", a=2)
        B.mix_pre = (pair(queries[:, 0:512]), pair(queries[:, 512:1024]))
        B.mix = (pair(queries[:, 1024:1536]), pair(queries[:, 1536:2048]))
        B.k_act, B.r_gate, B.v3_t, B.o3_t = (keys[:, n * 512:(n + 1) * 512] for n in range(4))
        B.r_kv = values[:, 0:512]
        B.squares3 = keys[:, 0:512]
        B.o3_nat = values[:, 512:1024].rearrange("p (t d) -> p t d", d=D)
        B.x_pair = pair(values[:, 1024:1024 + 2 * (SEQ + 1)])
        B.qk_all = arena[:, :].rearrange("p (b q) -> p b q", b=BATCHES)
        B.zeros = B.q_t[:, :, :].rearrange("p a b -> p (a b)")[:, 0:1536]
        B.wf_diag = B.y_nat[:, 0, :]
        def slots(name, cap):
            return nc.dram_tensor(name, [EXPERTS * cap, D], F32, kind="Internal").ap()

        B.rows0 = slots("rows0", CAP0)
        B.rows1 = slots("rows1", CAP1)
        B.rows2 = slots("rows2", CAP2)
        B.outs0 = slots("outs0", CAP0)
        B.outs1 = slots("outs1", CAP1)
        B.outs2 = slots("outs2", CAP2)

        setup(nc, I, B)
        norm_and_route(nc, B, 0, CAP0)
        linear_attention(nc, I, B)
        experts(nc, I, B, 0, CAP0, ROWS0, B.rows0, B.outs0)
        norm_and_route(nc, B, 1, CAP1, B.outs0, 2, B.bo_row)
        latent_attention(nc, I, B)
        experts(nc, I, B, 1, CAP1, ROWS1, B.rows1, B.outs1)
        norm_and_route(nc, B, 2, CAP2, B.outs1, 1)
        small_head_attention(nc, I, B)
        experts(nc, I, B, 2, CAP2, ROWS2, B.rows2, B.outs2)
        norm_and_route(nc, B, 3, 0, B.outs2, 1)
        channel_attention_and_mix(nc, B, out)


_INS = ['L0_attn_x', 'L0_attn_Wq', 'L0_attn_Wk', 'L0_attn_Wv', 'L0_attn_Wo', 'L0_attn_bo', 'L0_attn_Wf', 'L0_attn_bf',
        'L0_ffn_router_gate', 'L0_ffn_gate_w', 'L0_ffn_up_w', 'L0_ffn_down_w', 'L1_attn_w_kv_down', 'L1_attn_w_kv_up',
        'L1_attn_w_q', 'L1_attn_w_out', 'L1_ffn_wg', 'L1_ffn_W1', 'L1_ffn_b1', 'L1_ffn_W2', 'L1_ffn_b2', 'L2_attn_Wq',
        'L2_attn_bq', 'L2_attn_Wk', 'L2_attn_bk', 'L2_ffn_router_w', 'L2_ffn_w1', 'L2_ffn_b1', 'L2_ffn_w2', 'L2_ffn_b2',
        'L3_attn_gain', 'L3_attn_w_q', 'L3_attn_w_k', 'L3_attn_w_v', 'L3_attn_w_o', 'L3_ffn_W_r', 'L3_ffn_W_k',
        'L3_ffn_W_v', 'L3_ffn_mu_r', 'L3_ffn_mu_k']


def kernel(**inputs):
    import concourse.bacc as bacc
    from concourse.bass_utils import run_bass_kernel_spmd as run

    nc = bacc.Bacc("TRN2", target_bir_lowering=False, num_devices=1)
    arrays, ins = {}, {}
    for name in _INS:
        a = np.ascontiguousarray(inputs[name])
        arrays[f"in_{name}"] = a
        ins[name] = nc.dram_tensor(f"in_{name}", a.shape, mybir.dt.from_np(a.dtype), kind="ExternalInput").ap()
    out = nc.dram_tensor("out", [BATCHES, SEQ, D], F32, kind="ExternalOutput").ap()
    build(nc, ins, out)
    return run(nc, [arrays], core_ids=[0]).results[0]["out"]
```

```python
from contextlib import ExitStack, contextmanager

import numpy as np
import concourse.bass as bass
from concourse import mybir

ALU = mybir.AluOpType
ACT = mybir.ActivationFunctionType
AX = mybir.AxisListType
F32 = mybir.dt.float32
BF16 = mybir.dt.bfloat16
I32 = mybir.dt.int32

P = 128
BATCHES = 8
SEQ = 256
D = 128
TOKENS = BATCHES * SEQ
TILES = TOKENS // P
HEADS = 16
EXPERTS = 8
FF = 512
FCH = FF // P
NEG = -1e30
LN_EPS = 1e-5
PAD_SLOT = 1 << 16

FEAT = 64
PAIRS = HEADS // 2
HS = 64
LAG = 2
CAP0 = int(1.25 * ((TOKENS * 2 + EXPERTS - 1) // EXPERTS))
CAP1 = int(TOKENS / EXPERTS * 1.25) + 1
CAP2 = int(np.ceil(1.5 * TOKENS / EXPERTS))
ROWS0, ROWS1, ROWS2 = 128, 107, 128
GATE_BITS = 30
ROUND_BITS = 3
ROUNDS = GATE_BITS // ROUND_BITS
TRIES = 2 ** ROUND_BITS - 1


@contextmanager
def phase(nc, B, stage, names):
    handles = {n: nc.alloc_semaphore(f"{stage}_{n}") for n in names.split()}
    if B.used_semaphores:
        nc.clear_and_free_semaphores(B.used_semaphores)
    B.used_semaphores = list(handles.values())
    with nc.Block() as block:
        yield block, handles


def per_tile(ap, n):
    return ap.unsqueeze(2).to_broadcast([ap.shape[0], ap.shape[1], n])


def columns(vector):
    return vector.rearrange("(p a) -> p a", a=1)


def row_on_all(vector, n=P):
    return vector.rearrange("(a d) -> a d", a=1).broadcast_to([n, vector.shape[0]])


def setup(nc, I, B):
    with phase(nc, B, "setup", "x_in made ints const") as (block, s):

        @block.sync
        def _(sp):
            sp.dma_start(B.x_res[:, :, :], I["L0_attn_x"].rearrange("b (t p) d -> p (b t) d", p=P)).then_inc(s["x_in"], 16)
            sp.wait_ge(s["x_in"], 16)

        @block.gpsimd
        def _(pool):
            nc.gpsimd.memset(B.ident[:, :], 0.0).then_inc(s["made"], 1)
            nc.gpsimd.memset(B.ones[:, :], 1.0).then_inc(s["made"], 1)
            nc.gpsimd.memset(B.ident_b[:, :], 0.0).then_inc(s["made"], 1)
            nc.gpsimd.memset(B.causal_b[:, :], 0.0).then_inc(s["made"], 1)
            pool.wait_ge(s["made"], 4)
            for m in (B.ident, B.ident_b):
                nc.gpsimd.affine_select(out=m[:, :], in_=m[:, :], compare_op=ALU.not_equal, fill=1.0, base=0,
                                        pattern=[[-1, P]], channel_multiplier=1).then_inc(s["made"], 1)
            nc.gpsimd.affine_select(out=B.causal_b[:, :], in_=B.causal_b[:, :], compare_op=ALU.is_ge, fill=NEG, base=0,
                                    pattern=[[-1, P]], channel_multiplier=1).then_inc(s["made"], 1)
            v = B.same_head[:, :].rearrange("p (h j) -> p h j", j=8)
            ones = B.ones[:, :].rearrange("p (h j) -> p h j", j=8)
            nc.gpsimd.affine_select(out=v, in_=ones, compare_op=ALU.is_ge, fill=0.0, base=0,
                                    pattern=[[-8, HEADS], [0, 8]], channel_multiplier=1).then_inc(s["made"], 1)
            pool.wait_ge(s["made"], 8)
            nc.gpsimd.affine_select(out=v, in_=v, compare_op=ALU.is_ge, fill=0.0, base=7,
                                    pattern=[[8, HEADS], [0, 8]], channel_multiplier=-1).then_inc(s["made"], 1)
            nc.gpsimd.iota(B.expert_m8[:, :, :], pattern=[[0, TILES], [1, EXPERTS]], base=-EXPERTS, channel_multiplier=0,
                           allow_small_or_imprecise_dtypes=True).then_inc(s["ints"], 1)
            nc.gpsimd.iota(B.int_a[:, :], pattern=[[1, P]], base=P, channel_multiplier=-1).then_inc(s["ints"], 1)
            nc.gpsimd.iota(B.int_b[:, :], pattern=[[0, 1]], base=0, channel_multiplier=1).then_inc(s["ints"], 1)
            for va in B.va:
                nc.gpsimd.memset(va[:, :, :, 8:9], 1.0).then_inc(s["ints"], 1)
            nc.gpsimd.memset(B.kv0[:, :, :], 0.0).then_inc(s["ints"], 1)
            nc.gpsimd.memset(B.half_neg[:, :], -0.5).then_inc(s["ints"], 1)
            nc.gpsimd.memset(B.zeros[:, :], 0.0).then_inc(s["ints"], 1)
            nc.gpsimd.memset(B.wf_diag[:, :], 0.0).then_inc(s["ints"], 1)
            pool.wait_ge(s["const"], 3)
            nc.gpsimd.affine_select(out=B.low_expert[:, :], in_=B.same_expert[:, :], compare_op=ALU.is_gt, fill=0.0,
                                    base=0, pattern=[[1, P]], channel_multiplier=-1).then_inc(s["ints"], 1)

        @block.vector
        def _(dve):
            for n in range(ROUNDS):
                for j in range(TRIES):
                    nc.vector.memset(B.gate_bits[:, TRIES * n + j:TRIES * n + j + 1], (j + 1) << (GATE_BITS - ROUND_BITS * (n + 1)))
            dve.wait_ge(s["ints"], 3)
            nc.vector.tensor_scalar(B.int_a[:, :], B.int_a[:, :], 7, None, ALU.bitwise_and).then_inc(s["const"], 1)
            nc.vector.tensor_scalar(B.int_b[:, :], B.int_b[:, :], 7, None, ALU.bitwise_and).then_inc(s["const"], 1)
            dve.wait_ge(s["const"], 2)
            nc.vector.tensor_scalar(B.same_expert[:, :], B.int_a[:, :], 0.0, None, ALU.is_equal).then_inc(s["const"], 1)
            nc.vector.tensor_copy(B.own_expert[:, :], B.int_b[:, :]).then_inc(s["const"], 1)
            dve.wait_ge(s["made"], 9)
            nc.vector.tensor_scalar(B.not_same_head[:, :], B.same_head[:, :], -1.0, -NEG, ALU.add, ALU.mult).then_inc(s["const"], 1)


def first_weights_sync(nc, I, B, sp, s):
    sp.dma_start(B.router[:, 0, :], I["L0_ffn_router_gate"]).then_inc(s["router_in"], 16)
    sp.dma_start(B.router[:, 1, :], I["L1_ffn_wg"]).then_inc(s["router_in"], 16)
    sp.dma_start(B.router[:, 2, :], I["L2_ffn_router_w"].rearrange("e d -> d e"),
                 allow_slow_non_contiguous=True).then_inc(s["router_in"], 16)
    for dst, src in ((B.wq0, I["L0_attn_Wq"]), (B.wk0, I["L0_attn_Wk"]), (B.wv0, I["L0_attn_Wv"]), (B.wo0, I["L0_attn_Wo"])):
        sp.dma_start(dst[:, :], src).then_inc(s["w_in"], 16)
    for half in range(2):
        sp.dma_start(B.bf_col[half * FEAT:(half + 1) * FEAT, :], columns(I["L0_attn_bf"])).then_inc(s["w_in"], 16)
    sp.dma_start(B.bf_row[:, :], row_on_all(I["L0_attn_bf"])).then_inc(s["w_in"], 16)
    sp.dma_start(B.bo_row[:, :], row_on_all(I["L0_attn_bo"])).then_inc(s["w_in"], 16)
    for h in range(HEADS):
        sp.dma_start(B.wf_diag[8 * h:8 * h + 8, h * FEAT:(h + 1) * FEAT], I["L0_attn_Wf"]).then_inc(s["wf_ready"], 16)
    for rows, cap, parts in ((B.rows0, CAP0, 4), (B.rows1, CAP1, 2), (B.rows2, CAP2, 2)):
        n = EXPERTS * cap * D // P // parts
        flat = rows.rearrange("r d -> (r d)").rearrange("(p a) -> p a", p=P)
        for k in range(parts):
            sp.dma_start(flat[:, k * n:(k + 1) * n], B.zeros[:, 0:n]).then_inc(s["rows_zero"], 16)
    sp.wait_ge(s["rows_zero"], 16 * 8)


def first_weights_pe(nc, B, pe, s):
    pe.wait_ge(s["w_in"], 16 * 8)
    for n, w in enumerate((B.wq0, B.wk0)):
        nc.tensor.transpose(B.ps[:, 6, n * P:(n + 1) * P], w[:, :], B.ident[:, :]).then_inc(s["wt_psum"], 1)
    pe.wait_ge(s["wt_sbuf"], 1)
    pe.wait_ge(s["wf_ready"], 16 * HEADS)
    for n in range(4):
        if n >= 2:
            pe.wait_ge(s["feat_sbuf"], n - 1)
        nc.tensor.matmul(B.ps[:, 6 + n % 2, :], B.wqt[:, n // 2, :], B.wf_diag[:, (n % 2) * 512:(n % 2) * 512 + 512],
                         start=True, stop=True).then_inc(s["feat_psum"], 1)


def first_weights_act(nc, B, act, s):
    act.wait_ge(s["wt_psum"], 2)
    nc.scalar.activation(B.wqt[:, :, :], B.ps[:, 6, 0:256].rearrange("p (a b) -> p a b", a=2),
                         ACT.Copy).then_inc(s["wt_sbuf"], 1)
    for n in range(4):
        w, half = (B.wqf, B.wkf)[n // 2], n % 2
        act.wait_ge(s["feat_psum"], n + 1)
        nc.scalar.activation(w[:, half * 512:half * 512 + 512], B.ps[:, 6 + n % 2, :], ACT.Copy).then_inc(s["feat_sbuf"], 1)


def norm_and_route(nc, I, B, layer, cap, outs=None, choices=0, bias=None):
    ps_t, ps_log, ps_te, ps_col = B.ps[:, 0:2, :], B.ps[:, 2, 0:P], B.ps[:, 3, 0:P], B.ps[:, 4, :]
    ps_te2 = B.ps[:, 5, 0:P]
    with phase(nc, B, f"route{layer}", "link centred squared var rstd xn xt_psum xt logits shifted exp onehot te_psum counted "
                   "total loop_cnt loop_tot slots_te slots_tok in0 in1 in2 in3 w_squared w_summed w_rooted w_normed wt_psum "
                   "wt_sbuf router_in w_in wf_ready rows_zero feat_psum feat_sbuf") as (block, s):
        GROUPS, PER = 4, TILES // 4
        landed = (s["in0"], s["in1"], s["in2"], s["in3"])

        if layer == 0:
            @block.sync
            def _(sp):
                first_weights_sync(nc, I, B, sp, s)

        @block.scalar
        def _(act):
            def transposed(g):
                act.wait_ge(s["xt_psum"], g + 1)
                nc.scalar.activation(B.xn_t[:, g * 512:(g + 1) * 512], ps_t[:, g % 2, :], ACT.Copy).then_inc(s["xt"], 1)

            if layer == 3:
                mix_weights_act(nc, B, act, s)
            for g in range(GROUPS):
                act.wait_ge(s["centred"], g + 1)
                if g >= 2:
                    act.wait_ge(s["var"], g - 1)
                nc.scalar.activation(B.squares[:, g % 2, :], B.xn[:, g * PER:(g + 1) * PER, :].rearrange("p t d -> p (t d)"),
                                     ACT.Square).then_inc(s["squared"], 1)
                if g >= 1:
                    transposed(g - 1)
            transposed(GROUPS - 1)
            if layer < 3:
                act.wait_ge(s["shifted"], 1)
                nc.scalar.activation(B.r_exp[:, :, :], B.r_a[:, :, :], ACT.Exp).then_inc(s["exp"], 1)
            if layer == 0:
                first_weights_act(nc, B, act, s)

        @block.gpsimd
        def _(pool):
            for t in range(TILES if choices else 0):
                for k in range(choices):
                    nc.gpsimd.indirect_dma_start(B.back[:, k, t, :], None, outs,
                                                 bass.IndirectOffsetOnAxis(ap=B.from_slot[:, k, t:t + 1], axis=0)).then_inc(landed[t // PER], 16)
            for g in range(GROUPS):
                pool.wait_ge(s["var"], g + 1)
                t = slice(g * PER, (g + 1) * PER)
                nc.gpsimd.tensor_tensor(B.rstd[:, t], B.variance[:, t], B.half_neg[:, 0:PER], ALU.pow).then_inc(s["rstd"], 1)

        @block.tensor
        def _(pe):
            def logits(g):
                pe.wait_ge(s["xt"], g + 1)
                if layer == 0 and g == 0:
                    pe.wait_ge(s["router_in"], 16 * 3)
                for t in range(g * PER, (g + 1) * PER):
                    last = nc.tensor.matmul(ps_log[:, t * EXPERTS:(t + 1) * EXPERTS], B.xn_t[:, t * P:(t + 1) * P],
                                            B.router[:, layer, :], start=True, stop=True)
                last.then_inc(s["logits"], 1)

            if layer == 3:
                mix_weights_pe(nc, B, pe, s)
            for g in range(GROUPS):
                pe.wait_ge(s["xn"], g + 1)
                if g >= 2:
                    pe.wait_ge(s["xt"], g - 1)
                for j in range(PER):
                    last = nc.tensor.transpose(ps_t[:, g % 2, j * P:(j + 1) * P], B.xn[:, g * PER + j, :], B.ident[:, :])
                last.then_inc(s["xt_psum"], 1)
                if layer < 3 and g >= 1:
                    logits(g - 1)
            if layer == 3:
                return
            logits(GROUPS - 1)
            if layer == 0:
                first_weights_pe(nc, B, pe, s)
            pe.wait_ge(s["onehot"], 1)
            nc.tensor.transpose(ps_te, B.r_choice[:, :, :].rearrange("p t e -> p (t e)"), B.ident[:, :]).then_inc(s["te_psum"], 1)
            if layer == 0:
                with pe.Fori(0, ROUNDS) as n:
                    pe.wait_ge(s["loop_cnt"], n + 1)
                    nc.tensor.matmul(ps_col[:, 4:4 + TRIES], B.same_expert[:, :], B.c_count[:, :], start=True,
                                     stop=True).then_inc(s["loop_tot"], 1)
                pe.wait_ge(s["counted"], 1)
                nc.tensor.matmul(ps_col[:, 1:2], B.same_expert[:, :], B.c_above[:, :], start=True, stop=True).then_inc(s["total"], 1)
                pe.wait_ge(s["counted"], 2)
                nc.tensor.matmul(ps_col[:, 2:3], B.low_expert[:, :], B.c_ties[:, :], start=True, stop=True).then_inc(s["total"], 1)
            k = 2 if layer == 0 else 0
            pe.wait_ge(s["counted"], k + 1)
            nc.tensor.matmul(ps_col[:, 3:4], B.low_expert[:, :], B.c_kept[:, :], start=True, stop=True).then_inc(s["total"], 1)
            pe.wait_ge(s["slots_te"], 1)
            nc.tensor.transpose(ps_te2, B.te_slot[:, :], B.ident[:, :]).then_inc(s["slots_tok"], 1)

        @block.vector
        def _(dve):
            n_link = [0]

            def link(ins):
                n_link[0] += 1
                ins.then_inc(s["link"], 1)
                dve.wait_ge(s["link"], n_link[0])

            def group(g):
                return slice(g * PER, (g + 1) * PER)

            def combine(g):
                t = group(g)
                dve.wait_ge(landed[g], 16 * PER * choices)
                for k in range(choices):
                    link(nc.vector.tensor_tensor(B.back[:, k, t, :], B.back[:, k, t, :], per_tile(B.gate[:, k, t], D), ALU.mult))
                    link(nc.vector.tensor_tensor(B.x_res[:, t, :], B.x_res[:, t, :], B.back[:, k, t, :], ALU.add))

            def centre(g):
                t = group(g)
                link(nc.vector.tensor_reduce(B.mean[:, t], B.x_res[:, t, :], AX.X, ALU.add))
                link(nc.vector.tensor_scalar(B.mean[:, t], B.mean[:, t], -1.0 / D, None, ALU.mult))
                nc.vector.tensor_tensor(B.xn[:, t, :], B.x_res[:, t, :], per_tile(B.mean[:, t], D), ALU.add).then_inc(s["centred"], 1)

            def spread(g):
                t = group(g)
                dve.wait_ge(s["squared"], g + 1)
                link(nc.vector.tensor_reduce(B.variance[:, t], B.squares[:, g % 2, :].rearrange("p (t d) -> p t d", d=D),
                                             AX.X, ALU.add))
                nc.vector.tensor_scalar(B.variance[:, t], B.variance[:, t], 1.0 / D, LN_EPS, ALU.mult, ALU.add).then_inc(s["var"], 1)

            def scale(g):
                t = group(g)
                dve.wait_ge(s["rstd"], g + 1)
                nc.vector.tensor_tensor(B.xn[:, t, :], B.xn[:, t, :], per_tile(B.rstd[:, t], D), ALU.mult).then_inc(s["xn"], 1)

            if bias is not None:
                link(nc.vector.tensor_tensor(B.x_res[:, :, :], B.x_res[:, :, :],
                                             bias[:, :].unsqueeze(1).to_broadcast([P, TILES, D]), ALU.add))
            if layer == 3:
                mix_weights_dve(nc, B, dve, s, link)
            for g in range(GROUPS + 2):
                if g < GROUPS:
                    if choices:
                        combine(g)
                    centre(g)
                if 1 <= g <= GROUPS:
                    spread(g - 1)
                if g >= 2:
                    scale(g - 2)
            if layer == 3:
                return

            def first_largest(choice, best, among):
                link(nc.vector.tensor_reduce(best, among, AX.X, ALU.max))
                link(nc.vector.tensor_tensor(B.r_a[:, :, :], among, per_tile(best, EXPERTS), ALU.is_equal))
                link(nc.vector.tensor_tensor(B.r_a[:, :, :], B.r_a[:, :, :], B.expert_m8[:, :, :], ALU.mult))
                link(nc.vector.tensor_reduce(B.v_a[:, :], B.r_a[:, :, :], AX.X, ALU.min))
                link(nc.vector.tensor_tensor(choice, B.expert_m8[:, :, :], per_tile(B.v_a[:, :], EXPERTS), ALU.is_equal))

            dve.wait_ge(s["logits"], GROUPS)
            lg = ps_log.rearrange("p (t e) -> p t e", e=EXPERTS)
            link(nc.vector.tensor_reduce(B.v_a[:, :], lg, AX.X, ALU.max))
            nc.vector.tensor_tensor(B.r_a[:, :, :], lg, per_tile(B.v_a[:, :], EXPERTS), ALU.subtract).then_inc(s["shifted"], 1)
            dve.wait_ge(s["exp"], 1)
            link(nc.vector.tensor_reduce(B.v_a[:, :], B.r_exp[:, :, :], AX.X, ALU.add))
            link(nc.vector.reciprocal(B.v_b[:, :], B.v_a[:, :]))
            link(nc.vector.tensor_tensor(B.r_prob[:, :, :], B.r_exp[:, :, :], per_tile(B.v_b[:, :], EXPERTS), ALU.mult))
            first_largest(B.r_one[:, 0], B.gate[:, 0, :], B.r_prob[:, :, :])
            te, keep = B.te_val, B.te_keep
            unused = B.squares[:, :, :].rearrange("p a b -> p (a b)").rearrange("p (j t) -> p j t", t=P)
            if layer == 0:
                link(nc.vector.scalar_tensor_tensor(out=B.r_exp[:, :, :], in0=B.r_one[:, 0], scalar=-2.0, in1=B.r_prob[:, :, :],
                                                    op0=ALU.mult, op1=ALU.add))
                first_largest(B.r_one[:, 1], B.gate[:, 1, :], B.r_exp[:, :, :])
                link(nc.vector.tensor_tensor(B.v_a[:, :], B.gate[:, 0, :], B.gate[:, 1, :], ALU.add))
                link(nc.vector.tensor_scalar(B.v_a[:, :], B.v_a[:, :], 1e-9, None, ALU.add))
                link(nc.vector.reciprocal(B.v_b[:, :], B.v_a[:, :]))
                for k in range(2):
                    link(nc.vector.tensor_tensor(B.gate[:, k, :], B.gate[:, k, :], B.v_b[:, :], ALU.mult))
                link(nc.vector.tensor_tensor(B.r_a[:, :, :], B.r_one[:, 0], per_tile(B.gate[:, 0, :], EXPERTS), ALU.mult))
                link(nc.vector.tensor_tensor(B.r_choice[:, :, :], B.r_one[:, 1], per_tile(B.gate[:, 1, :], EXPERTS), ALU.mult))
                nc.vector.tensor_tensor(B.r_choice[:, :, :], B.r_choice[:, :, :], B.r_a[:, :, :], ALU.add).then_inc(s["onehot"], 1)
                dve.wait_ge(s["te_psum"], 1)
                link(nc.vector.tensor_copy(te[:, :], ps_te))
                link(nc.vector.memset(B.thr[:, :], 0))
                base = n_link[0]
                with dve.Fori(0, ROUNDS) as n:
                    nc.vector.tensor_tensor(B.thr_try[:, :], B.thr[:, 0:1].to_broadcast([P, TRIES]),
                                            B.gate_bits[:, bass.ds(TRIES * n, TRIES)], ALU.bitwise_or).then_inc(s["link"], 1)
                    dve.wait_ge(s["link"], base + 3 * n + 1)
                    for j in range(TRIES):
                        last = nc.vector.tensor_scalar(unused[:, j, :], te[:, :], B.thr_try[:, j:j + 1].bitcast(F32), None, ALU.is_ge, ALU.add,
                                                       accum_out=B.c_count[:, j:j + 1])
                    last.then_inc(s["loop_cnt"], 1)
                    dve.wait_ge(s["loop_tot"], n + 1)
                    nc.vector.scalar_tensor_tensor(out=B.thr[:, 1:1 + TRIES].bitcast(F32), in0=ps_col[:, 4:4 + TRIES], scalar=float(cap),
                                                   in1=B.thr_try[:, :].bitcast(F32), op0=ALU.is_ge, op1=ALU.mult).then_inc(s["link"], 1)
                    dve.wait_ge(s["link"], base + 3 * n + 2)
                    nc.vector.tensor_reduce(B.thr[:, 0:1].bitcast(F32), B.thr[:, :].bitcast(F32), AX.X, ALU.max).then_inc(s["link"], 1)
                    dve.wait_ge(s["link"], base + 3 * n + 3)
                n_link[0] = base + 3 * ROUNDS
                thr = B.thr[:, 0:1].bitcast(F32)
                nc.vector.tensor_scalar(keep[:, :], te[:, :], thr, None, ALU.is_gt, ALU.add,
                                        accum_out=B.c_above[:, :]).then_inc(s["counted"], 1)
                link(nc.vector.tensor_scalar(B.te_tie[:, :], te[:, :], thr, None, ALU.is_equal))
                link(nc.vector.scalar_tensor_tensor(out=B.te_tie[:, :], in0=te[:, :], scalar=0.0, in1=B.te_tie[:, :],
                                                    op0=ALU.is_gt, op1=ALU.mult))
                nc.vector.tensor_reduce(B.c_ties[:, :], B.te_tie[:, :], AX.X, ALU.add).then_inc(s["counted"], 1)
                dve.wait_ge(s["total"], 2)
                link(nc.vector.tensor_scalar(B.c_room[:, :], ps_col[:, 1:2], -1.0, float(cap), ALU.mult, ALU.add))
                link(nc.vector.tensor_copy(B.c_start[:, :], ps_col[:, 2:3]))
                link(nc.vector.tensor_tensor_scan(B.te_rank[:, :], B.ones[:, :], B.te_tie[:, :], B.c_start[:, :],
                                                  ALU.mult, ALU.add))
                link(nc.vector.scalar_tensor_tensor(out=B.te_tie[:, :], in0=B.te_rank[:, :], scalar=B.c_room[:, :],
                                                    in1=B.te_tie[:, :], op0=ALU.is_le, op1=ALU.mult))
                link(nc.vector.tensor_tensor(keep[:, :], keep[:, :], B.te_tie[:, :], ALU.add))
            else:
                link(nc.vector.tensor_copy(B.r_choice[:, :, :], B.r_one[:, 0]))
                nc.vector.memset(B.thr[:, :], 0).then_inc(s["onehot"], 1)
                dve.wait_ge(s["te_psum"], 1)
                link(nc.vector.tensor_copy(keep[:, :], ps_te))
            nc.vector.tensor_reduce(B.c_kept[:, :], keep[:, :], AX.X, ALU.add).then_inc(s["counted"], 1)
            dve.wait_ge(s["total"], 3 if layer == 0 else 1)
            link(nc.vector.tensor_copy(B.c_start[:, :], ps_col[:, 3:4]))
            link(nc.vector.tensor_tensor_scan(B.te_rank[:, :], B.ones[:, :], keep[:, :], B.c_start[:, :], ALU.mult, ALU.add))
            if layer > 0:
                link(nc.vector.scalar_tensor_tensor(out=keep[:, :], in0=B.te_rank[:, :], scalar=float(cap), in1=keep[:, :],
                                                    op0=ALU.is_le, op1=ALU.mult))
            link(nc.vector.tensor_scalar(B.c_room[:, :], B.own_expert[:, :], float(cap), None, ALU.mult))
            nc.vector.scalar_tensor_tensor(out=B.te_slot[:, :], in0=B.te_rank[:, :], scalar=B.c_room[:, :], in1=keep[:, :],
                                           op0=ALU.add, op1=ALU.mult).then_inc(s["slots_te"], 1)
            dve.wait_ge(s["slots_tok"], 1)
            for k in range(2 if layer == 0 else 1):
                link(nc.vector.tensor_tensor(B.r_a[:, :, :], ps_te2.rearrange("p (t e) -> p t e", e=EXPERTS), B.r_one[:, k], ALU.mult))
                link(nc.vector.tensor_reduce(B.v_a[:, :], B.r_a[:, :, :], AX.X, ALU.add))
                link(nc.vector.scalar_tensor_tensor(out=B.gate[:, k, :], in0=B.v_a[:, :], scalar=0.0, in1=B.gate[:, k, :],
                                                    op0=ALU.is_gt, op1=ALU.mult))
                link(nc.vector.tensor_scalar(B.v_b[:, :], B.v_a[:, :], 0.0, float(PAD_SLOT), ALU.is_equal, ALU.mult))
                link(nc.vector.scalar_tensor_tensor(out=B.to_slot[:, k, :], in0=B.v_a[:, :], scalar=-1.0, in1=B.v_b[:, :],
                                                    op0=ALU.add, op1=ALU.add))
                link(nc.vector.tensor_scalar(B.from_slot[:, k, :], B.v_a[:, :], -1.0, 0.0, ALU.add, ALU.max))


def scatter_rows(nc, pool, B, rows, choices, total, done):
    for k in range(choices):
        for t in range(TILES):
            nc.gpsimd.indirect_dma_start(rows, bass.IndirectOffsetOnAxis(ap=B.to_slot[:, k, t:t + 1], axis=0),
                                         B.xn[:, t, :], None, bounds_check=total - 1, oob_is_err=False).then_inc(done, 16)
    pool.wait_ge(done, 16 * choices * TILES)


def linear_attention(nc, I, B):
    names = ("link scattered x_staged q_psum q_sbuf k_psum k_bias k_relu v_psum v_sbuf kv_psum kv_sbuf num_psum num_t nat_psum "
             "num_sbuf t_psum t_sbuf o_psum added w_next")
    ps = B.ps
    with phase(nc, B, "linear", names) as (block, s):

        @block.gpsimd
        def _(pool):
            scatter_rows(nc, pool, B, B.rows0, 2, EXPERTS * CAP0, s["scattered"])

        @block.scalar
        def _(act):
            def stage(b, buffer):
                act.nop()
                nc.scalar.activation(B.x_st[buffer], B.xn_t[:, bass.ds(b * SEQ, SEQ)], ACT.Copy).then_inc(s["x_staged"], 1)

            def q_features(b, buffer):
                for j in range(4):
                    act.wait_ge(s["q_psum"], 4 * b + j + 1)
                    nc.scalar.activation(B.qf[buffer][:, 2 * j:2 * j + 2, :].rearrange("p a b -> p (a b)"), ps[:, j % 2, :], ACT.Relu,
                                         bias=B.bf_col[:, :]).then_inc(s["q_sbuf"], 1)

            def k_features(b, buffer):
                for j in range(4):
                    act.wait_ge(s["k_bias"], 4 * b + j + 1)
                    v = B.kf[buffer][:, j // 2, (j % 2) * 512:(j % 2) * 512 + 512]
                    nc.scalar.activation(v, v, ACT.Relu).then_inc(s["k_relu"], 1)

            def output(b):
                act.wait_ge(s["t_psum"], b + 1)
                nc.scalar.activation(B.o_t[:, :, :].rearrange("p a b -> p (a b)"), ps[:, 7, 0:256], ACT.Copy).then_inc(s["t_sbuf"], 1)

            def step(b, k, more, tail):
                if more:
                    if tail:
                        act.wait_ge(s["v_psum"], b)
                    stage(b + 1, 1 - k)
                    q_features(b + 1, 1 - k)
                if tail:
                    output(b - 1)
                if more:
                    k_features(b + 1, 1 - k)
                act.wait_ge(s["num_psum"], b + 1)
                nc.scalar.activation(B.num_t[:, :], ps[:, 6, :], ACT.Copy).then_inc(s["num_t"], 1)

            stage(0, 0)
            q_features(0, 0)
            k_features(0, 0)
            step(0, 0, True, False)
            with act.Fori(0, BATCHES // 2 - 1) as i:
                for k in range(2):
                    step(2 * i + k + 1, 1 - k, True, True)
            step(BATCHES - 1, 1, False, True)
            output(BATCHES - 1)

        @block.tensor
        def _(pe):
            def q_features(b, buffer, first=False):
                pe.wait_ge(s["x_staged"], b + 1)
                for j in range(4):
                    if j >= 2 or not first:
                        pe.wait_ge(s["q_sbuf"], 4 * b + j - 1)
                    for i in range(2):
                        last = nc.tensor.matmul(ps[:, j % 2, i * SEQ:(i + 1) * SEQ], B.wqf[:, (2 * j + i) * P:(2 * j + i + 1) * P],
                                                B.x_st[buffer], start=True, stop=True)
                    last.then_inc(s["q_psum"], 1)

            def k_features(b, buffer, first=False):
                for j in range(4):
                    if j >= 2 or not first:
                        pe.wait_ge(s["k_bias"], 4 * b + j - 1)
                    nc.tensor.matmul(ps[:, 2 + j % 2, :], B.x_st[buffer][:, (j // 2) * P:(j // 2 + 1) * P],
                                     B.wkf[:, (j % 2) * 512:(j % 2) * 512 + 512], start=True, stop=True).then_inc(s["k_psum"], 1)

            def values(b, buffer, first=False):
                if not first:
                    pe.wait_ge(s["v_sbuf"], b)
                for t in range(2):
                    last = nc.tensor.matmul(ps[:, 5, 256 + t * P:256 + (t + 1) * P], B.x_st[buffer][:, t * P:(t + 1) * P], B.wv0[:, :],
                                            start=True, stop=True)
                last.then_inc(s["v_psum"], 1)

            def transpose_out(b, first=False):
                pe.wait_ge(s["num_sbuf"], b + 1)
                if not first:
                    pe.wait_ge(s["added"], b)
                for t in range(2):
                    last = nc.tensor.transpose(ps[:, 7, t * P:(t + 1) * P], B.o_nat[:, t, :], B.ident[:, :])
                last.then_inc(s["t_psum"], 1)

            def output(b):
                pe.wait_ge(s["t_sbuf"], b + 1)
                for t in range(2):
                    last = nc.tensor.matmul(ps[:, 7, 256 + t * P:256 + (t + 1) * P], B.o_t[:, t, :], B.wo0[:, :],
                                            start=True, stop=True)
                last.then_inc(s["o_psum"], 1)

            def step(b, k, more, tail, tail_first=False):
                if more:
                    q_features(b + 1, 1 - k)
                pe.wait_ge(s["v_sbuf"], b + 1)
                pe.wait_ge(s["k_relu"], 4 * b + 4)
                for p in range(PAIRS):
                    for t in range(2):
                        last = nc.tensor.matmul(ps[:, 5, 18 * p:18 * p + 18], B.kf[k][:, t, p * P:(p + 1) * P],
                                                B.va[k][:, t, 2 * p:2 * p + 2, :].rearrange("p a b -> p (a b)"),
                                                start=t == 0, stop=t == 1)
                last.then_inc(s["kv_psum"], 1)
                if tail:
                    transpose_out(b - 1, tail_first)
                if more:
                    k_features(b + 1, 1 - k)
                if tail:
                    output(b - 1)
                pe.wait_ge(s["kv_sbuf"], 2 * b + 2)
                pe.wait_ge(s["q_sbuf"], 4 * b + 4)
                if tail:
                    pe.wait_ge(s["num_t"], b)
                for p in range(PAIRS):
                    row, half = 32 * (p % 4), p // 4
                    last = nc.tensor.matmul(ps[row:row + 32, 6, half * SEQ:(half + 1) * SEQ], B.kv0[:, p, :], B.qf[k][:, p, :],
                                            start=True, stop=True, tile_position=(0, row))
                last.then_inc(s["num_psum"], 1)
                if more:
                    values(b + 1, 1 - k)
                pe.wait_ge(s["num_t"], b + 1)
                if tail:
                    pe.wait_ge(s["num_sbuf"], b)
                for t in range(2):
                    for half in range(2):
                        last = nc.tensor.transpose(ps[:, 4, t * 256 + half * P:t * 256 + (half + 1) * P],
                                                   B.num_t[:, half * SEQ + t * P:half * SEQ + (t + 1) * P], B.ident[:, :])
                last.then_inc(s["nat_psum"], 1)

            q_features(0, 0, first=True)
            k_features(0, 0, first=True)
            values(0, 0, first=True)
            step(0, 0, True, False)
            with pe.Fori(0, BATCHES // 2 - 1) as i:
                for k in range(2):
                    step(2 * i + k + 1, 1 - k, True, True)
            step(BATCHES - 1, 1, False, True)
            transpose_out(BATCHES - 1)
            output(BATCHES - 1)

        @block.vector
        def _(dve):
            def k_bias(b, buffer):
                for j in range(4):
                    dve.wait_ge(s["k_psum"], 4 * b + j + 1)
                    nc.vector.tensor_tensor(B.kf[buffer][:, j // 2, (j % 2) * 512:(j % 2) * 512 + 512].rearrange("p (h f) -> p h f", f=FEAT),
                                            ps[:, 2 + j % 2, :].rearrange("p (h f) -> p h f", f=FEAT),
                                            B.bf_row[:, :].unsqueeze(1).to_broadcast([P, 8, FEAT]), ALU.add).then_inc(s["k_bias"], 1)

            def v_copy(b, buffer):
                dve.wait_ge(s["v_psum"], b + 1)
                nc.vector.tensor_copy(B.va[buffer][:, :, :, 0:8],
                                      ps[:, 5, 256:512].rearrange("p (t h d) -> p t h d", t=2, d=8)).then_inc(s["v_sbuf"], 1)

            def divide(b):
                dve.wait_ge(s["nat_psum"], b + 1)
                num = ps[:, 4, :].rearrange("p (a r) -> p a r", r=32)[:, :, 0:18].rearrange("p a (h c) -> p a h c", c=9)
                den = B.den[:, :].rearrange("p (a h) -> p a h", h=2)
                nc.vector.tensor_scalar(den, num[:, :, :, 8], 1e-6, None, ALU.max).then_inc(s["link"], 1)
                dve.wait_ge(s["link"], 2 * b + 1)
                nc.vector.reciprocal(B.den[:, :], B.den[:, :]).then_inc(s["link"], 1)
                dve.wait_ge(s["link"], 2 * b + 2)
                nc.vector.tensor_tensor(B.o_nat[:, :, :].rearrange("p t (a h d) -> p (t a) h d", h=2, d=8), num[:, :, :, 0:8],
                                        den.unsqueeze(3).to_broadcast([P, 2 * PAIRS, 2, 8]), ALU.mult).then_inc(s["num_sbuf"], 1)

            def add(b):
                dve.wait_ge(s["o_psum"], b + 1)
                xb = B.x_res[:, bass.ds(2 * b, 2), :]
                nc.vector.tensor_tensor(xb, xb, ps[:, 7, 256:512].rearrange("p (t d) -> p t d", d=D), ALU.add).then_inc(s["added"], 1)

            def step(b, k, more, tail):
                if tail:
                    divide(b - 1)
                dve.wait_ge(s["kv_psum"], b + 1)
                kv = ps[:, 5, 0:144].rearrange("p (a c) -> p a c", c=18)
                nc.vector.tensor_copy(B.kv0[0:64, :, 0:9], kv[0:64, :, 0:9]).then_inc(s["kv_sbuf"], 1)
                nc.vector.tensor_copy(B.kv0[64:128, :, 9:18], kv[64:128, :, 9:18]).then_inc(s["kv_sbuf"], 1)
                if more:
                    k_bias(b + 1, 1 - k)
                if tail:
                    add(b - 1)
                if more:
                    v_copy(b + 1, 1 - k)

            k_bias(0, 0)
            v_copy(0, 0)
            step(0, 0, True, False)
            with dve.Fori(0, BATCHES // 2 - 1) as i:
                for k in range(2):
                    step(2 * i + k + 1, 1 - k, True, True)
            step(BATCHES - 1, 1, False, True)
            divide(BATCHES - 1)
            add(BATCHES - 1)

        @block.sync
        def _(sp):
            for dst, src in ((B.w_kv_down[:, :], I["L1_attn_w_kv_down"]), (B.w_q[:, :], I["L1_attn_w_q"]),
                             (B.w_kv_up[:, :], I["L1_attn_w_kv_up"]), (B.w_out[:, :, :], I["L1_attn_w_out"].rearrange("(c p) d -> p c d", p=P))):
                sp.dma_start(dst, src).then_inc(s["w_next"], 16)
            sp.wait_ge(s["w_next"], 16 * 4 + first_experts(I, B, sp, 0, s["w_next"]))


def latent_attention(nc, I, B):
    ps = B.ps
    G = HEADS // 2
    PIECES = 9
    names = ("scattered x_staged proj_psum proj_sbuf v_psum v_act v_dve s_psum maxed exped p_psum p_sbuf summed normed y_psum y_sbuf "
             "o_psum added w_next")
    with phase(nc, B, "latent", names) as (block, s):

        def score_bank(g, hh):
            return (g % 2) * 2 + hh

        SLOTS = (("qk", 0), ("qk", 1), ("qk", 2), ("qk", 3), ("qk", 4), ("qk", 5), ("out", 0), ("qk", 6),
                 ("qk", 7), ("qk", 8), ("v", 0), ("v", 1), ("v", 2), ("v", 3), None, None)

        def batches(eng, step):
            step(0, 0, range(G), True, False)
            with eng.Fori(0, BATCHES // 2 - 1) as i:
                for k in range(2):
                    step(2 * i + k + 1, 1 - k, range(G), False, False)
            step(BATCHES - 1, 1, range(G + LAG + 2), False, True)

        def slot(g, end):
            return SLOTS[2 * g + end] if g < G else None

        @block.sync
        def _(sp):
            loads = [(B.wq2[:, :], I["L2_attn_Wq"]), (B.wk2[:, :], I["L2_attn_Wk"]), (B.bq2[:, :], columns(I["L2_attn_bq"])),
                     (B.bk2[:, :], columns(I["L2_attn_bk"])), (B.bk2_row[:, :], row_on_all(I["L2_attn_bk"])),
                     (B.gain[:, :], row_on_all(I["L3_attn_gain"]))]
            loads += [(B.w3[:, n, :], w) for n, w in enumerate((I["L3_attn_w_q"], I["L3_attn_w_k"], I["L3_attn_w_v"], I["L3_attn_w_o"],
                                                                I["L3_ffn_W_r"], I["L3_ffn_W_k"], I["L3_ffn_W_v"]))]
            loads += [(B.mu[:, 0:1], columns(I["L3_ffn_mu_r"])), (B.mu[:, 1:2], columns(I["L3_ffn_mu_k"]))]
            for dst, src in loads:
                sp.dma_start(dst, src).then_inc(s["w_next"], 16)
            sp.wait_ge(s["w_next"], 16 * len(loads) + first_experts(I, B, sp, 1, s["w_next"]))

        @block.gpsimd
        def _(pool):
            scatter_rows(nc, pool, B, B.rows1, 1, EXPERTS * CAP1, s["scattered"])

        @block.tensor
        def _(pe):
            def projection(b, k, piece, bank):
                if piece == 0:
                    pe.wait_ge(s["x_staged"], b + 1)
                if piece == 5:
                    pe.wait_ge(s["proj_sbuf"], PIECES * b + 1)
                x, y = B.x_b[:, 0:SEQ], B.latent[:, :]
                if piece == 0:
                    last = nc.tensor.matmul(ps[:, bank, 0:SEQ], B.w_kv_down[:, :], x, start=True, stop=True)
                else:
                    for i in range(2):
                        c = 2 * ((piece - 1) % 4) + i
                        w = (B.w_q if piece < 5 else B.w_kv_up)[:, c * P:(c + 1) * P]
                        last = nc.tensor.matmul(ps[:, bank, i * SEQ:(i + 1) * SEQ], w, x if piece < 5 else y, start=True, stop=True)
                last.then_inc(s["proj_psum"], 1)

            def v_projection(c, bank):
                t, half = c // 2, c % 2
                nc.tensor.matmul(ps[:, bank, :], B.latent[:, t * P:(t + 1) * P],
                                 B.w_kv_up[:, HEADS * HS + 512 * half:HEADS * HS + 512 * half + 512],
                                 start=True, stop=True).then_inc(s["v_psum"], 1)

            def output(b):
                for t in range(2):
                    for c in range(8):
                        if t == 0:
                            pe.wait_ge(s["y_sbuf"], G * b + c + 1)
                        last = nc.tensor.matmul(ps[:, 7, t * P:(t + 1) * P], B.y_t[:, 1 - t, c, :], B.w_out[:, c, :],
                                                start=c == 0, stop=c == 7)
                last.then_inc(s["o_psum"], 1)

            def through_bank_7(b, k, what, first, last):
                kind, n = what
                if kind == "out":
                    if not first:
                        if not last:
                            pe.wait_ge(s["proj_sbuf"], PIECES * (b + 1) + 6)
                        output(b - 1)
                    return
                if last:
                    return
                if kind == "qk":
                    if n == 0:
                        pe.wait_ge(s["v_dve"], 2 * (b + 1))
                    elif n == 6 and not first:
                        pe.wait_ge(s["added"], b)
                    else:
                        pe.wait_ge(s["proj_sbuf"], PIECES * (b + 1) + n)
                    projection(b + 1, 1 - k, n, 7)
                else:
                    if n == 0:
                        pe.wait_ge(s["proj_sbuf"], PIECES * (b + 2))
                    elif n < 3:
                        pe.wait_ge(s["v_act"], 2 * (b + 1) + n)
                    else:
                        pe.wait_ge(s["v_dve"], 2 * (b + 1) + 1)
                    v_projection(n, 7)

            def scores(b, k, g, first):
                n = G * b + g
                if g >= 2 or not first:
                    pe.wait_ge(s["exped"], n - 1)
                for hh in range(2):
                    rows = slice(HS * hh, HS * hh + HS)
                    bank = ps[:, score_bank(g, hh), :]
                    for q, lo, keys in ((1, 0, SEQ), (0, SEQ, P)):
                        nc.tensor.matmul(bank[:, lo:lo + keys], B.q_ts[k][rows, g, q * P:(q + 1) * P], B.k_ts[k][rows, g, 0:keys],
                                         start=q == 1, stop=False)
                    last = nc.tensor.matmul(bank[:, P:3 * P].rearrange("p (a k) -> p a k", a=2), B.ident_b[:, :],
                                            B.causal_b[:, :].unsqueeze(1).to_broadcast([P, 2, P]), start=False, stop=True)
                last.then_inc(s["s_psum"], 1)

            def transposes(b, g):
                n = G * b + g
                pe.wait_ge(s["normed"], n + 1)
                pe.wait_ge(s["p_sbuf"], n)
                for hh in range(2):
                    for j in range(3):
                        last = nc.tensor.transpose(ps[:, 4 + hh, j * P:(j + 1) * P], B.p_nat[:, g % 2, hh, j * P:(j + 1) * P],
                                                   B.ident[:, :])
                last.then_inc(s["p_psum"], 1)

            def values(b, k, g):
                v = B.v_nats[k if g >= 0 else 1 - k]
                pe.wait_ge(s["p_sbuf"], G * b + g + 1)
                pe.wait_ge(s["y_sbuf"], G * b + g)
                for hh in range(2):
                    h = 2 * (g % G) + hh
                    y = ps[HS * hh:HS * hh + HS, 6, :]
                    p = B.p_t[:, g % 2, hh, :]
                    nc.tensor.matmul(y[:, 0:SEQ].rearrange("p (a q) -> p a q", a=2), v[:, 0, h, :],
                                     p[:, 0:4 * P].rearrange("p (a q) -> p a q", a=4)[:, 0:3:2, :], start=True, stop=False)
                    last = nc.tensor.matmul(y[:, 0:P], v[:, 1, h, :], p[:, P:2 * P], start=False, stop=True)
                last.then_inc(s["y_psum"], 1)

            def step(b, k, steps, first, last):
                pe.wait_ge(s["proj_sbuf"], PIECES * (b + 1))
                for g in steps:
                    if g < G:
                        scores(b, k, g, first)
                    if slot(g, 0):
                        through_bank_7(b, k, slot(g, 0), first, last)
                    if g < G + LAG and (g >= LAG or not first):
                        transposes(b, g - LAG)
                    if g == LAG + 1:
                        pe.wait_ge(s["v_act"], 2 * (b + 1))
                        pe.wait_ge(s["v_dve"], 2 * (b + 1))
                    if g < G + LAG + 1 and (g > LAG or not first):
                        values(b, k, g - LAG - 1)
                    if slot(g, 1):
                        through_bank_7(b, k, slot(g, 1), first, last)
                if last:
                    output(b)

            for piece in range(PIECES):
                if piece >= 4:
                    pe.wait_ge(s["proj_sbuf"], piece - 3)
                projection(0, 0, piece, piece % 4)
            for c in range(4):
                v_projection(c, 4 + c)
            batches(pe, step)

        @block.scalar
        def _(act):
            def stage(b):
                act.wait_ge(s["proj_psum"], PIECES * b)
                act.nop()
                nc.scalar.activation(B.x_b[:, 0:SEQ], B.xn_t[:, bass.ds(b * SEQ, SEQ)], ACT.Copy).then_inc(s["x_staged"], 1)

            def projected(b, k, piece, bank):
                act.wait_ge(s["proj_psum"], PIECES * b + piece + 1)
                if piece == 0:
                    act.wait_ge(s["v_psum"], 4 * b)
                    nc.scalar.activation(B.latent[:, :], ps[:, bank, 0:SEQ], ACT.Copy).then_inc(s["proj_sbuf"], 1)
                    return
                dst, c, scale = (B.q_ts[k], piece - 1, HS ** -0.5) if piece < 5 else (B.k_ts[k], piece - 5, 1.0)
                nc.scalar.activation(dst[:, 2 * c:2 * c + 2, :].rearrange("p a b -> p (a b)"), ps[:, bank, :], ACT.Copy,
                                     scale=scale).then_inc(s["proj_sbuf"], 1)

            def v_copy(b, k, c, bank):
                t, half = c // 2, c % 2
                act.wait_ge(s["v_psum"], 4 * b + c + 1)
                nc.scalar.activation(B.v_nats[k][:, t, 8 * half:8 * half + 8, :], ps[:, bank, :].rearrange("p (h d) -> p h d", d=HS),
                                     ACT.Copy).then_inc(s["v_act"], 1)

            def from_bank_7(b, k, what):
                if what and what[0] == "qk":
                    projected(b + 1, 1 - k, what[1], 7)
                if what and what[0] == "v" and what[1] < 2:
                    v_copy(b + 1, 1 - k, what[1], 7)

            def exponentials(b, g, first):
                n = G * b + g
                act.wait_ge(s["maxed"], n + 1)
                if g >= 2 or not first:
                    act.wait_ge(s["p_psum"], n - 1)
                for hh in range(2):
                    for q, lo, hi in ((1, 0, SEQ), (0, SEQ, 3 * P)):
                        last = nc.scalar.activation(B.p_nat[:, g % 2, hh, lo:hi], ps[:, score_bank(g, hh), lo:hi], ACT.Exp,
                                                    bias=B.neg_max[:, g % 2, q, hh:hh + 1], accum_out=B.p_sum[:, g % 2, q, hh:hh + 1])
                last.then_inc(s["exped"], 1)

            def y_copy(b, g, first):
                act.wait_ge(s["y_psum"], G * b + g + 1)
                if g == 0 and not first:
                    act.wait_ge(s["o_psum"], b)
                nc.scalar.activation(B.y_t[:, :, g % G, :], ps[:, 6, 0:SEQ].rearrange("p (t q) -> p t q", t=2),
                                     ACT.Copy).then_inc(s["y_sbuf"], 1)

            def step(b, k, steps, first, last):
                if not last:
                    stage(b + 1)
                for g in steps:
                    if slot(g, 0) and not last:
                        from_bank_7(b, k, slot(g, 0))
                    if g < G:
                        exponentials(b, g, first)
                    if g < G + LAG + 1 and (g > LAG or not first):
                        y_copy(b, g - LAG - 1, first)
                    if slot(g, 1) and not last:
                        from_bank_7(b, k, slot(g, 1))

            stage(0)
            for piece in range(PIECES):
                projected(0, 0, piece, piece % 4)
            for c in range(2):
                v_copy(0, 0, c, 4 + c)
            batches(act, step)

        @block.vector
        def _(dve):
            def v_copy(b, k, c, bank):
                t, half = c // 2, c % 2
                dve.wait_ge(s["v_psum"], 4 * b + c + 1)
                nc.vector.tensor_copy(B.v_nats[k][:, t, 8 * half:8 * half + 8, :],
                                      ps[:, bank, :].rearrange("p (h d) -> p h d", d=HS)).then_inc(s["v_dve"], 1)

            def from_bank_7(b, k, what, first, last):
                if what and what[0] == "v" and what[1] >= 2 and not last:
                    v_copy(b + 1, 1 - k, what[1], 7)
                if what and what[0] == "out" and not first:
                    add(b - 1)

            def add(b):
                dve.wait_ge(s["o_psum"], b + 1)
                xb = B.x_res[:, bass.ds(2 * b, 2), :]
                nc.vector.tensor_tensor(xb, xb, ps[:, 7, 0:SEQ].rearrange("p (t d) -> p t d", d=D), ALU.add).then_inc(s["added"], 1)

            def maxima(b, g):
                dve.wait_ge(s["s_psum"], G * b + g + 1)
                bank = ps[:, score_bank(g, 0):score_bank(g, 0) + 2, :]
                nc.vector.tensor_reduce(B.neg_max[:, g % 2, 1, :], bank[:, :, 0:SEQ], AX.X, ALU.max, negate=True)
                nc.vector.tensor_reduce(B.neg_max[:, g % 2, 0, :], bank[:, :, SEQ:3 * P], AX.X, ALU.max,
                                        negate=True).then_inc(s["maxed"], 1)

            def normalise(b, g):
                dve.wait_ge(s["exped"], G * b + g + 1)
                nc.vector.reciprocal(B.p_sum[:, g % 2, :, :], B.p_sum[:, g % 2, :, :]).then_inc(s["summed"], 1)
                dve.wait_ge(s["summed"], G * b + g + 1)
                for hh in range(2):
                    for q, lo, hi in ((1, 0, SEQ), (0, SEQ, 3 * P)):
                        p = B.p_nat[:, g % 2, hh, lo:hi]
                        last = nc.vector.tensor_scalar(p, p, B.p_sum[:, g % 2, q, hh:hh + 1], None, ALU.mult)
                last.then_inc(s["normed"], 1)

            def p_copy(b, g, first):
                dve.wait_ge(s["p_psum"], G * b + g + 1)
                if g >= 2 or not first:
                    dve.wait_ge(s["y_psum"], G * b + g - 1)
                nc.vector.tensor_copy(B.p_t[:, g % 2, :, 0:3 * P], ps[:, 4:6, 0:3 * P]).then_inc(s["p_sbuf"], 1)

            def step(b, k, steps, first, last):
                for g in steps:
                    if g < G:
                        maxima(b, g)
                    if g < G + 1 and (g >= 1 or not first):
                        normalise(b, g - 1)
                    if g < G + LAG and (g >= LAG or not first):
                        p_copy(b, g - LAG, first)
                    from_bank_7(b, k, slot(g, 0), first, last)
                    from_bank_7(b, k, slot(g, 1), first, last)
                if last:
                    add(b)

            for c in range(2, 4):
                v_copy(0, 0, c, 4 + c)
            batches(dve, step)


def small_head_attention(nc, I, B):
    ps = B.ps
    G = HEADS // 2
    QUADS = HEADS // 4
    SCALE = float(D) ** -0.5
    ROWS = 9 * 8
    BACK = LAG + 3
    AT_QK, AT_V = LAG + 2, LAG + 1
    LOADS = 3 + 9
    names = ("link w_next scattered x_staged xv_staged qk_psum v_psum qk_sbuf split parts parts_out rows_in v_sbuf s_psum maxed exped p_psum p_sbuf p_sbuf_act "
             "y_psum y_sbuf n_psum y_norm added scaled v_zero v_one")
    with phase(nc, B, "small", names) as (block, s):

        def score_bank(g, hh):
            return (g % 2) * 2 + hh

        def batches(eng, step):
            step(0, 0, range(G), True, 2)
            with eng.Fori(0, 2) as i:
                for k in range(2):
                    step(2 * i + k + 1, 1 - k, range(G), False, 2)
            step(BATCHES - 3, 1, range(G), False, 2)
            step(BATCHES - 2, 0, range(G), False, 1)
            step(BATCHES - 1, 1, range(G + LAG + 2), False, 0)

        @block.sync
        def _(sp):
            def to_rows(b, k):
                sp.wait_ge(s["parts"], 2 * b + 2)
                sp.dma_start(B.parts_dram[0], B.parts[:, 0]).then_inc(s["parts_out"], 16)
                if not isinstance(b, int) or b >= 2:
                    sp.wait_ge(s["s_psum"], G * (b - 1))
                sp.dma_start(B.parts_dram[1], B.parts[:, 1]).then_inc(s["parts_out"], 16)
                sp.wait_ge(s["parts_out"], 32 * b + 32)
                for j in range(3):
                    sp.dma_start(B.q_rows[k][24 * j:24 * j + 24, :, :],
                                 B.parts_dram[0].rearrange("(h d) i q -> (d i) h q", d=8)).then_inc(s["rows_in"], 16)
                for j in range(3):
                    for i in range(3):
                        sp.dma_start(B.k_rows[k][24 * j + i:24 * j + 24:3, :, :],
                                     B.parts_dram[1][:, j, :].rearrange("(h d) q -> d h q", d=8)).then_inc(s["rows_in"], 16)

            to_rows(0, 0)
            to_rows(1, 1)
            weights = first_experts(I, B, sp, 2, s["w_next"])
            with sp.Fori(0, BATCHES // 2 - 1) as i:
                for k in range(2):
                    to_rows(2 * i + k + 2, k)
            sp.wait_ge(s["w_next"], weights)

        @block.gpsimd
        def _(pool):
            def split(b):
                pool.wait_ge(s["qk_sbuf"], 2 * b + 2)
                pool.wait_ge(s["rows_in"], 16 * LOADS * b)
                part = [B.parts[:, :, n, :] for n in range(3)]
                one = B.ones[:, 0:1].unsqueeze(2).to_broadcast([P, 2, SEQ])
                nc.gpsimd.tensor_tensor(part[0], B.qk2_t, one, ALU.mult).then_inc(s["split"], 1)
                pool.wait_ge(s["split"], 3 * b + 1)
                nc.gpsimd.tensor_tensor(B.qk2_rest, B.qk2_t, part[0], ALU.subtract).then_inc(s["split"], 1)
                pool.wait_ge(s["split"], 3 * b + 2)
                nc.gpsimd.tensor_tensor(part[1], B.qk2_rest, one, ALU.mult).then_inc(s["parts"], 1)
                pool.wait_ge(s["parts"], 2 * b + 1)
                nc.gpsimd.tensor_tensor(B.qk2_rest, B.qk2_rest, part[1], ALU.subtract).then_inc(s["split"], 1)
                pool.wait_ge(s["split"], 3 * b + 3)
                nc.gpsimd.tensor_tensor(part[2], B.qk2_rest, one, ALU.mult).then_inc(s["parts"], 1)

            for k in range(2):
                nc.gpsimd.memset(B.va2[k], 0.0).then_inc(s["v_zero"], 1)
            pool.wait_ge(s["v_zero"], 2)
            for k in range(2):
                nc.gpsimd.memset(B.va2[k][:, :, :, 8:9], 1.0).then_inc(s["v_one"], 1)
            split(1)
            scatter_rows(nc, pool, B, B.rows2, 1, EXPERTS * CAP2, s["scattered"])
            with pool.Fori(2, BATCHES) as b:
                split(b)

        @block.tensor
        def _(pe):
            def qk_projection(b):
                pe.wait_ge(s["x_staged"], b + 1)
                for n, w in enumerate((B.wq2, B.wk2)):
                    last = nc.tensor.matmul(ps[:, 7, n * SEQ:(n + 1) * SEQ], w[:, :], B.x_b[:, 0:SEQ], start=True, stop=True)
                last.then_inc(s["qk_psum"], 1)

            def v_projection(b):
                pe.wait_ge(s["xv_staged"], b + 1)
                for t in range(2):
                    last = nc.tensor.matmul(ps[:, 6, SEQ + t * P:SEQ + (t + 1) * P], B.x_v[:, t * P:(t + 1) * P], B.wk2[:, :],
                                            start=True, stop=True)
                last.then_inc(s["v_psum"], 1)

            def scores(b, k, g, first):
                if g >= 2 or not first:
                    pe.wait_ge(s["exped"], G * b + g - 1)
                for hh in range(2):
                    for q in range(2):
                        last = nc.tensor.matmul(ps[:, score_bank(g, hh), q * SEQ:(q + 1) * SEQ],
                                                B.q_rows[k][0:ROWS, 2 * g + hh, q * P:(q + 1) * P], B.k_rows[k][0:ROWS, 2 * g + hh, :],
                                                start=True, stop=True)
                last.then_inc(s["s_psum"], 1)

            def transposes(b, g):
                pe.wait_ge(s["exped"], G * b + g + 1)
                pe.wait_ge(s["p_sbuf"], G * b + g)
                pe.wait_ge(s["p_sbuf_act"], G * b + g)
                for hh in range(2):
                    for j in range(4):
                        last = nc.tensor.transpose(ps[:, 4 + hh, j * P:(j + 1) * P], B.p_nat[:, g % 2, hh, j * P:(j + 1) * P],
                                                   B.ident[:, :])
                last.then_inc(s["p_psum"], 1)

            def values(b, k, g):
                va = B.va2[k if g >= 0 else 1 - k]
                pe.wait_ge(s["p_sbuf"], G * b + g + 1)
                pe.wait_ge(s["p_sbuf_act"], G * b + g + 1)
                if g % 2 == 0:
                    pe.wait_ge(s["y_sbuf"], QUADS * b + g // 2)
                for hh in range(2):
                    row = 32 * (2 * (g % 2) + hh)
                    p = B.p_t[:, g % 2, hh, :].rearrange("p (a q) -> p a q", a=4)
                    for t in range(2):
                        last = nc.tensor.matmul(ps[row:row + 32, 6, 0:SEQ].rearrange("p (a q) -> p a q", a=2),
                                                va[:, t, 2 * (g % G) + hh, :], p[:, t:4:2, :], start=t == 0, stop=t == 1,
                                                tile_position=(0, row))
                last.then_inc(s["y_psum"], 1)

            def back(b, quad):
                pe.wait_ge(s["y_sbuf"], QUADS * b + quad + 1)
                pe.wait_ge(s["y_norm"], QUADS * b + quad)
                for t in range(2):
                    last = nc.tensor.transpose(ps[:, 7, t * P:(t + 1) * P], B.yt2[:, t * P:(t + 1) * P], B.ident[:, :])
                last.then_inc(s["n_psum"], 1)

            def step(b, k, steps, first, following):
                pe.wait_ge(s["rows_in"], 16 * LOADS * (b + 1))
                for g in steps:
                    if g < G:
                        scores(b, k, g, first)
                    if g < G + LAG and (g >= LAG or not first):
                        transposes(b, g - LAG)
                    if (g - BACK) % 2 == 0 and (g >= BACK or not first):
                        if g == BACK and following >= 2:
                            pe.wait_ge(s["qk_sbuf"], 2 * b + 6)
                        back(b, (g - BACK) // 2)
                    if g == AT_V:
                        pe.wait_ge(s["v_sbuf"], b + 1)
                        if following >= 1:
                            pe.wait_ge(s["y_sbuf"], QUADS * b)
                            v_projection(b + 1)
                    if g == AT_QK and following >= 2:
                        pe.wait_ge(s["y_norm"], QUADS * b)
                        qk_projection(b + 2)
                    if g == AT_V + 2 and following >= 1:
                        pe.wait_ge(s["v_sbuf"], b + 2)
                    if g < G + LAG + 1 and (g > LAG or not first):
                        values(b, k, g - LAG - 1)

            pe.wait_ge(s["v_one"], 2)
            qk_projection(0)
            v_projection(0)
            pe.wait_ge(s["qk_sbuf"], 2)
            qk_projection(1)
            pe.wait_ge(s["qk_sbuf"], 4)
            batches(pe, step)

        @block.scalar
        def _(act):
            def stage(b):
                act.wait_ge(s["qk_psum"], b)
                act.nop()
                nc.scalar.activation(B.x_b[:, 0:SEQ], B.xn_t[:, bass.ds(b * SEQ, SEQ)], ACT.Copy).then_inc(s["x_staged"], 1)

            def stage_v(b):
                act.wait_ge(s["scaled"], 1)
                act.wait_ge(s["v_psum"], b)
                nc.scalar.activation(B.x_v, B.xn_t[:, bass.ds(b * SEQ, SEQ)], ACT.Copy).then_inc(s["xv_staged"], 1)

            def biased(b):
                act.wait_ge(s["qk_psum"], b + 1)
                act.wait_ge(s["parts"], 2 * b)
                nc.scalar.activation(B.qk2_t[:, 0, :], ps[:, 7, 0:SEQ], ACT.Identity, bias=B.bq2_scaled[:, :], scale=SCALE).then_inc(s["qk_sbuf"], 1)
                nc.scalar.activation(B.qk2_t[:, 1, :], ps[:, 7, SEQ:2 * SEQ], ACT.Identity, bias=B.bk2[:, :]).then_inc(s["qk_sbuf"], 1)

            def step(b, k, steps, first, following):
                for g in steps:
                    if g < G + LAG and (g >= LAG or not first):
                        n = g - LAG
                        act.wait_ge(s["p_psum"], G * b + n + 1)
                        if n >= 2 or not first:
                            act.wait_ge(s["y_psum"], G * b + n - 1)
                        nc.scalar.activation(B.p_t[:, n % 2, 1, :], ps[:, 5, :], ACT.Copy).then_inc(s["p_sbuf_act"], 1)
                    if g < G:
                        act.wait_ge(s["maxed"], G * b + g + 1)
                        if g >= 2 or not first:
                            act.wait_ge(s["p_psum"], G * b + g - 1)
                        for hh in range(2):
                            for q in range(2):
                                last = nc.scalar.activation(B.p_nat[:, g % 2, hh, q * SEQ:(q + 1) * SEQ],
                                                            ps[:, score_bank(g, hh), q * SEQ:(q + 1) * SEQ], ACT.Exp,
                                                            bias=B.neg_max2[:, g % 2, 2 * hh + q:2 * hh + q + 1])
                        last.then_inc(s["exped"], 1)
                    n = g - LAG - 1
                    if n % 2 == 1 and n < G and (n >= 0 or not first):
                        act.wait_ge(s["y_psum"], G * b + n + 1)
                        act.wait_ge(s["n_psum"], QUADS * b + n // 2)
                        nc.scalar.activation(B.yt2[:, :], ps[:, 6, 0:SEQ], ACT.Copy).then_inc(s["y_sbuf"], 1)
                    if g == AT_QK and following >= 2:
                        biased(b + 2)
                    if g == 0 and following >= 1:
                        stage_v(b + 1)
                    if g == 1 and following >= 2:
                        stage(b + 2)

            act.wait_ge(s["scaled"], 1)
            stage(0)
            stage_v(0)
            biased(0)
            stage(1)
            biased(1)
            batches(act, step)

        @block.vector
        def _(dve):
            def v_biased(b, k):
                dve.wait_ge(s["v_psum"], b + 1)
                nc.vector.tensor_tensor(B.va2[k][:, :, :, 0:8], ps[:, 6, SEQ:2 * SEQ].rearrange("p (t h d) -> p t h d", t=2, d=8),
                                        B.bk2_row[:, :].rearrange("p (h d) -> p h d", d=8).unsqueeze(1).to_broadcast([P, 2, HEADS, 8]),
                                        ALU.add).then_inc(s["v_sbuf"], 1)

            def normalise(b, quad):
                dve.wait_ge(s["n_psum"], QUADS * b + quad + 1)
                y = ps[:, 7, 0:SEQ].rearrange("p (t h r) -> p t h r", t=2, r=32)
                dve.wait_ge(s["y_norm"], QUADS * b + quad)
                nc.vector.reciprocal(B.rden2[:, :, :], y[:, :, :, 8]).then_inc(s["link"], 1)
                dve.wait_ge(s["link"], QUADS * b + quad + 1)
                head = 4 * (quad % QUADS)
                nc.vector.tensor_tensor(B.o_nat[:, :, :].rearrange("p t (h d) -> p t h d", d=8)[:, :, head:head + 4, :],
                                        y[:, :, :, 0:8], B.rden2[:, :, :].unsqueeze(3).to_broadcast([P, 2, 4, 8]),
                                        ALU.mult).then_inc(s["y_norm"], 1)

            def add(b):
                dve.wait_ge(s["y_norm"], QUADS * (b + 1))
                xb = B.x_res[:, bass.ds(2 * b, 2), :]
                nc.vector.tensor_tensor(xb, xb, B.o_nat[:, :, :], ALU.add).then_inc(s["added"], 1)
                dve.wait_ge(s["added"], b + 1)

            def step(b, k, steps, first, following):
                for g in steps:
                    if g < G:
                        dve.wait_ge(s["s_psum"], G * b + g + 1)
                        bank = ps[:, score_bank(g, 0):score_bank(g, 0) + 2, :].rearrange("p a (q k) -> p (a q) k", k=SEQ)
                        nc.vector.tensor_reduce(B.neg_max2[:, g % 2, :], bank, AX.X, ALU.max, negate=True).then_inc(s["maxed"], 1)
                    if g < G + LAG and (g >= LAG or not first):
                        n = g - LAG
                        dve.wait_ge(s["p_psum"], G * b + n + 1)
                        if n >= 2 or not first:
                            dve.wait_ge(s["y_psum"], G * b + n - 1)
                        nc.vector.tensor_copy(B.p_t[:, n % 2, 0, :], ps[:, 4, :]).then_inc(s["p_sbuf"], 1)
                    if g == AT_V + 2 and following >= 1:
                        dve.wait_ge(s["y_sbuf"], QUADS * b + 1)
                        v_biased(b + 1, 1 - k)
                    if (g - BACK) % 2 == 0 and (g >= BACK or not first):
                        quad = (g - BACK) // 2
                        normalise(b, quad)
                        if quad == -1:
                            add(b - 1)
                        if quad == QUADS - 1:
                            add(b)

            nc.vector.tensor_scalar(B.bq2_scaled[:, :], B.bq2[:, :], SCALE, None, ALU.mult).then_inc(s["scaled"], 1)
            dve.wait_ge(s["v_one"], 2)
            v_biased(0, 0)
            part = [B.parts[:, :, n, :] for n in range(3)]
            dve.wait_ge(s["qk_sbuf"], 2)
            nc.vector.tensor_copy(part[0], B.qk2_t).then_inc(s["split"], 1)
            dve.wait_ge(s["split"], 1)
            nc.vector.tensor_tensor(B.qk2_rest, B.qk2_t, part[0], ALU.subtract).then_inc(s["split"], 1)
            dve.wait_ge(s["split"], 2)
            nc.vector.tensor_copy(part[1], B.qk2_rest).then_inc(s["parts"], 1)
            dve.wait_ge(s["parts"], 1)
            nc.vector.tensor_tensor(B.qk2_rest, B.qk2_rest, part[1], ALU.subtract).then_inc(s["split"], 1)
            dve.wait_ge(s["split"], 3)
            nc.vector.tensor_copy(part[2], B.qk2_rest).then_inc(s["parts"], 1)
            batches(dve, step)


def mix_weights_act(nc, B, act, s):
    for n in range(4):
        nc.scalar.activation(B.squares3[:, n * P:(n + 1) * P], B.w3[:, n, :], ACT.Square).then_inc(s["w_squared"], 1)
    act.wait_ge(s["w_summed"], 1)
    nc.scalar.activation(B.w_norm[:, :], B.w_norm[:, :], ACT.Sqrt, scale=1.0 / D).then_inc(s["w_rooted"], 1)
    for n in range(2):
        act.wait_ge(s["wt_psum"], n + 1)
        m = 4 if n == 0 else 3
        nc.scalar.activation(B.w3_t[:, 4 * n:4 * n + m, :].rearrange("p a b -> p (a b)"), B.ps[:, 6 + n, 0:m * P],
                             ACT.Copy).then_inc(s["wt_sbuf"], 1)


def mix_weights_dve(nc, B, dve, s, link):
    dve.wait_ge(s["w_squared"], 4)
    nc.vector.tensor_reduce(B.w_norm[:, :], B.squares3.rearrange("p (n d) -> p n d", d=D), AX.X, ALU.add).then_inc(s["w_summed"], 1)
    link(nc.vector.tensor_scalar(B.gain_s[:, :], B.gain[:, :], float(D) ** -0.5, None, ALU.mult))
    link(nc.vector.tensor_scalar(B.mu[:, 2:4], B.mu[:, 0:2], -1.0, 1.0, ALU.mult, ALU.add))
    link(nc.vector.memset(B.x_pair[:, :, 0:1], 0.0))
    dve.wait_ge(s["w_rooted"], 1)
    link(nc.vector.tensor_scalar(B.w_norm[:, :], B.w_norm[:, :], 1e-4, None, ALU.add))
    link(nc.vector.reciprocal(B.w_norm[:, :], B.w_norm[:, :]))
    link(nc.vector.tensor_scalar(B.w_norm[:, :], B.w_norm[:, :], B.gain_s[:, :], None, ALU.mult))
    nc.vector.tensor_tensor(B.w3[:, 0:4, :], B.w3[:, 0:4, :], per_tile(B.w_norm[:, :], D), ALU.mult).then_inc(s["w_normed"], 1)


def mix_weights_pe(nc, B, pe, s):
    pe.wait_ge(s["w_normed"], 1)
    for n in range(7):
        last = nc.tensor.transpose(B.ps[:, 6 + n // 4, (n % 4) * P:(n % 4 + 1) * P], B.w3[:, n, :], B.ident[:, :])
        if n in (3, 6):
            last.then_inc(s["wt_psum"], 1)


def channel_attention_and_mix(nc, B, out):
    ps = B.ps
    names = ("x_staged qk_psum squared kept summed rooted link qk_norm v_psum v_sbuf s_psum masked shifted exped a_ready at_psum "
             "at_sbuf ot_psum ot_sbuf out_psum mixed_pre mixed r_psum k_psum tanhed k_sq kv_psum gated res stored added")
    STEPS = BATCHES // 2
    WIDE = 2 * SEQ
    with phase(nc, B, "channel", names) as (block, s):

        @block.sync
        def _(sp):
            with sp.Fori(0, STEPS) as i:
                sp.wait_ge(s["added"], i + 1)
                sp.dma_start(out[bass.ds(2 * i, 2)].rearrange("a (t p) d -> p (a t) d", p=P),
                             B.x_res[:, bass.ds(4 * i, 4), :]).then_inc(s["stored"], 16)
            sp.wait_ge(s["stored"], 16 * STEPS)

        @block.gpsimd
        def _(pool):
            with pool.Fori(0, STEPS) as i:
                pool.wait_ge(s["x_staged"], STEPS + i + 1)
                pool.wait_ge(s["mixed"], 2 * i)
                for n in range(2):
                    nc.gpsimd.tensor_tensor(B.mix_pre[n], B.x_pair[:, :, 0:SEQ], B.mu[:, 2 + n:3 + n].unsqueeze(2).to_broadcast([P, 2, SEQ]),
                                            ALU.mult).then_inc(s["mixed_pre"], 1)

        @block.scalar
        def _(act):
            def stage(i):
                act.nop()
                nc.scalar.activation(B.x_pair[:, :, 1:SEQ + 1], B.xn_t[:, bass.ds(i * WIDE, WIDE)].rearrange("p (a q) -> p a q", a=2),
                                     ACT.Copy).then_inc(s["x_staged"], 1)

            with act.Fori(0, STEPS // 2) as half:
                for k in range(2):
                    i = 2 * half + k
                    act.wait_ge(s["qk_psum"], i)
                    stage(i)
                    act.wait_ge(s["qk_psum"], i + 1)
                    act.wait_ge(s["summed"], i)
                    nc.scalar.activation(B.squares[:, :, :], ps[:, 2 * k:2 * k + 2, :], ACT.Square).then_inc(s["squared"], 1)
            act.wait_ge(s["summed"], STEPS)
            nc.scalar.activation(B.qk_len[:, :], B.qk_len[:, :], ACT.Sqrt, scale=1.0 / 8).then_inc(s["rooted"], 1)

            def step(i, more):
                act.wait_ge(s["v_psum"], i + 1)
                act.wait_ge(s["ot_psum"], i)
                nc.scalar.activation(B.v3_t, ps[:, 0, :], ACT.Copy).then_inc(s["v_sbuf"], 1)
                if more:
                    act.wait_ge(s["mixed"], 2 * i + 2)
                    stage(i + 1)
                act.wait_ge(s["shifted"], i + 1)
                for a in range(2):
                    last = nc.scalar.activation(B.a_nat[:, a, :], B.a_nat[:, a, :], ACT.Exp, bias=B.a_max[:, a:a + 1], scale=SEQ ** -0.5,
                                                accum_out=B.a_sum[:, a:a + 1])
                last.then_inc(s["exped"], 1)
                act.wait_ge(s["r_psum"], i + 1)
                act.wait_ge(s["gated"], i)
                nc.scalar.activation(B.r_gate, ps[:, 2, :], ACT.Tanh, scale=0.5).then_inc(s["tanhed"], 1)
                act.wait_ge(s["at_psum"], i + 1)
                nc.scalar.activation(B.a_t[:, :, :], ps[:, 4, 0:2 * P].rearrange("p (a k) -> p a k", a=2), ACT.Copy).then_inc(s["at_sbuf"], 1)
                act.wait_ge(s["ot_psum"], i + 1)
                act.wait_ge(s["out_psum"], i)
                nc.scalar.activation(B.o3_t, ps[:, 6, :], ACT.Copy).then_inc(s["ot_sbuf"], 1)

            act.wait_ge(s["qk_psum"], STEPS)
            stage(0)
            with act.Fori(0, STEPS - 1) as i:
                step(i, True)
            step(STEPS - 1, False)

        @block.tensor
        def _(pe):
            with pe.Fori(0, STEPS // 2) as half:
                for k in range(2):
                    pe.wait_ge(s["x_staged"], 2 * half + k + 1)
                    pe.wait_ge(s["kept"], 2 * half)
                    pe.wait_ge(s["squared"], 2 * half)
                    for t in range(4):
                        last = nc.tensor.matmul(ps[:, 2 * k + t // 2, (t % 2) * SEQ:(t % 2 + 1) * SEQ],
                                                B.x_pair[:, t // 2, 1 + (t % 2) * P:1 + (t % 2 + 1) * P],
                                                B.w3_t[:, 0:2, :].rearrange("p a b -> p (a b)"), start=True, stop=True)
                    last.then_inc(s["qk_psum"], 1)
            def values(i):
                pe.wait_ge(s["x_staged"], STEPS + i + 1)
                pe.wait_ge(s["v_sbuf"], i)
                nc.tensor.matmul(ps[:, 0, :].rearrange("p (a q) -> p a q", a=2), B.w3_t[:, 2, :], B.x_pair[:, :, 1:SEQ + 1],
                                 start=True, stop=True).then_inc(s["v_psum"], 1)

            def scores(i):
                pe.wait_ge(s["qk_norm"], i + 1)
                pe.wait_ge(s["masked"], i)
                for a in range(2):
                    for t in range(2):
                        qk = B.qk[:, 2 * a + t, :]
                        last = nc.tensor.matmul(ps[:, 1, a * P:(a + 1) * P], qk[:, 0:P], qk[:, P:2 * P], start=t == 0, stop=t == 1)
                last.then_inc(s["s_psum"], 1)

            def step(i, more):
                pe.wait_ge(s["mixed"], 2 * i + 2)
                pe.wait_ge(s["tanhed"], i)
                mix_r = B.mix[0].rearrange("p a q -> p (a q)")
                for t in range(4):
                    last = nc.tensor.matmul(ps[:, 2, t * P:(t + 1) * P], mix_r[:, t * P:(t + 1) * P], B.w3_t[:, 4, :],
                                            start=True, stop=True)
                last.then_inc(s["r_psum"], 1)
                pe.wait_ge(s["k_sq"], i)
                nc.tensor.matmul(ps[:, 3, :], B.w3_t[:, 5, :], B.mix[1].rearrange("p a q -> p (a q)"), start=True,
                                 stop=True).then_inc(s["k_psum"], 1)
                pe.wait_ge(s["a_ready"], i + 1)
                pe.wait_ge(s["at_sbuf"], i)
                for a in range(2):
                    last = nc.tensor.transpose(ps[:, 4, a * P:(a + 1) * P], B.a_nat[:, a, :], B.ident[:, :])
                last.then_inc(s["at_psum"], 1)
                pe.wait_ge(s["k_sq"], i + 1)
                pe.wait_ge(s["gated"], i)
                for t in range(4):
                    last = nc.tensor.matmul(ps[:, 5, t * P:(t + 1) * P], B.k_act[:, t * P:(t + 1) * P], B.w3_t[:, 6, :],
                                            start=True, stop=True)
                last.then_inc(s["kv_psum"], 1)
                if more:
                    values(i + 1)
                pe.wait_ge(s["at_sbuf"], i + 1)
                pe.wait_ge(s["v_sbuf"], i + 1)
                pe.wait_ge(s["ot_sbuf"], i)
                for a in range(2):
                    last = nc.tensor.matmul(ps[:, 6, a * SEQ:(a + 1) * SEQ], B.a_t[:, a, :], B.v3_t[:, a * SEQ:(a + 1) * SEQ],
                                            start=True, stop=True)
                last.then_inc(s["ot_psum"], 1)
                if more:
                    scores(i + 1)
                pe.wait_ge(s["ot_sbuf"], i + 1)
                pe.wait_ge(s["res"], i)
                for t in range(4):
                    last = nc.tensor.matmul(ps[:, 7, t * P:(t + 1) * P], B.o3_t[:, t * P:(t + 1) * P], B.w3_t[:, 3, :],
                                            start=True, stop=True)
                last.then_inc(s["out_psum"], 1)

            pe.wait_ge(s["kept"], STEPS)
            values(0)
            scores(0)
            with pe.Fori(0, STEPS - 1) as i:
                step(i, True)
            step(STEPS - 1, False)

        @block.vector
        def _(dve):
            HALF = float(0.5 / np.sqrt(0.5))
            HEAD_LENS = 4 * 2 * HEADS
            with dve.Fori(0, STEPS // 2) as half:
                for k in range(2):
                    i = 2 * half + k
                    dve.wait_ge(s["squared"], i + 1)
                    nc.vector.tensor_reduce(B.qk_len[:, bass.ds(i * HEAD_LENS, HEAD_LENS)],
                                            B.squares[:, :, :].rearrange("p a (h d) -> p (a h) d", d=8), AX.X, ALU.add).then_inc(s["summed"], 1)
                    nc.vector.tensor_copy(B.qk_all[:, bass.ds(2 * i, 2), :], ps[:, 2 * k:2 * k + 2, :]).then_inc(s["kept"], 1)
            dve.wait_ge(s["rooted"], 1)
            nc.vector.tensor_scalar(B.qk_len[:, :], B.qk_len[:, :], 1e-4, None, ALU.add).then_inc(s["link"], 1)
            dve.wait_ge(s["link"], 1)
            nc.vector.reciprocal(B.qk_len[:, :], B.qk_len[:, :]).then_inc(s["link"], 1)
            dve.wait_ge(s["link"], 2)

            def prepare(i):
                dve.wait_ge(s["s_psum"], i)
                nc.vector.tensor_tensor(B.qk[:, :, :].rearrange("p t (h d) -> p (t h) d", d=8),
                                        B.qk_all[:, bass.ds(2 * i, 2), :].rearrange("p t (h d) -> p (t h) d", d=8),
                                        per_tile(B.qk_len[:, bass.ds(i * HEAD_LENS, HEAD_LENS)], 8), ALU.mult).then_inc(s["qk_norm"], 1)
                for n in range(2):
                    dve.wait_ge(s["mixed_pre"], 2 * i + n + 1)
                    dve.wait_ge((s["r_psum"], s["k_psum"])[n], i)
                    nc.vector.scalar_tensor_tensor(out=B.mix[n], in0=B.x_pair[:, :, 1:SEQ + 1], scalar=B.mu[:, n:n + 1],
                                                   in1=B.mix_pre[n], op0=ALU.mult, op1=ALU.add).then_inc(s["mixed"], 1)

            def step(i, more):
                LINKS = 4
                n_link = [0]

                def link(ins, wait=True):
                    n_link[0] += 1
                    ins.then_inc(s["link"], 1)
                    if wait:
                        dve.wait_ge(s["link"], 2 + LINKS * i + n_link[0])

                dve.wait_ge(s["s_psum"], i + 1)
                dve.wait_ge(s["at_psum"], i)
                nc.vector.tensor_tensor(B.a_nat[:, :, :], ps[:, 1, 0:2 * P].rearrange("p (a k) -> p a k", a=2),
                                        B.not_same_head[:, :].unsqueeze(1).to_broadcast([P, 2, P]), ALU.add).then_inc(s["masked"], 1)
                dve.wait_ge(s["masked"], i + 1)
                link(nc.vector.tensor_reduce(B.a_max[:, :], B.a_nat[:, :, :], AX.X, ALU.max))
                nc.vector.tensor_scalar(B.a_max[:, :], B.a_max[:, :], -SEQ ** -0.5, None, ALU.mult).then_inc(s["shifted"], 1)
                dve.wait_ge(s["k_psum"], i + 1)
                dve.wait_ge(s["kv_psum"], i)
                link(nc.vector.tensor_scalar(B.k_act, ps[:, 3, :], 0.0, None, ALU.max), wait=False)
                dve.wait_ge(s["exped"], i + 1)
                link(nc.vector.reciprocal(B.a_sum[:, :], B.a_sum[:, :]))
                nc.vector.tensor_tensor(B.a_nat[:, :, :], B.a_nat[:, :, :], per_tile(B.a_sum[:, :], P), ALU.mult).then_inc(s["a_ready"], 1)
                nc.vector.tensor_tensor(B.k_act, B.k_act, B.k_act, ALU.mult).then_inc(s["k_sq"], 1)
                if more:
                    prepare(i + 1)
                dve.wait_ge(s["tanhed"], i + 1)
                dve.wait_ge(s["kv_psum"], i + 1)
                dve.wait_ge(s["added"], i)
                nc.vector.scalar_tensor_tensor(out=B.r_kv, in0=B.r_gate, scalar=1.0, in1=ps[:, 5, :], op0=ALU.add,
                                               op1=ALU.mult).then_inc(s["gated"], 1)
                xb, xn = B.x_res[:, bass.ds(4 * i, 4), :], B.xn[:, bass.ds(4 * i, 4), :]
                dve.wait_ge(s["out_psum"], i + 1)
                nc.vector.tensor_tensor(B.o3_nat, xn, ps[:, 7, :].rearrange("p (t d) -> p t d", d=D), ALU.add).then_inc(s["res"], 1)
                dve.wait_ge(s["res"], i + 1)
                link(nc.vector.scalar_tensor_tensor(out=B.o3_nat, in0=B.o3_nat, scalar=HALF, in1=xb, op0=ALU.mult, op1=ALU.add))
                dve.wait_ge(s["gated"], i + 1)
                nc.vector.scalar_tensor_tensor(out=xb, in0=B.r_kv.rearrange("p (t d) -> p t d", d=D), scalar=0.5, in1=B.o3_nat,
                                               op0=ALU.mult, op1=ALU.add).then_inc(s["added"], 1)
                assert n_link[0] == LINKS

            prepare(0)
            with dve.Fori(0, STEPS - 1) as i:
                step(i, True)
            step(STEPS - 1, False)


def expert_weights(I, layer):
    return {0: ((I["L0_ffn_gate_w"], I["L0_ffn_up_w"]), I["L0_ffn_down_w"], None, None),
            1: ((I["L1_ffn_W1"],), I["L1_ffn_W2"], I["L1_ffn_b1"], I["L1_ffn_b2"]),
            2: ((I["L2_ffn_w1"],), I["L2_ffn_w2"], I["L2_ffn_b1"], I["L2_ffn_b2"])}[layer]


def load_expert(I, B, sp, layer, e, k, done):
    up, down, _, _ = expert_weights(I, layer)
    for n, w in enumerate(up):
        sp.dma_start(B.w_up[:, k, n, :], w[bass.ds(e, 1)].rearrange("a d f -> d (a f)")).then_inc(done, 16)
    sp.dma_start(B.w_down[:, k, :, :], down[bass.ds(e, 1)].rearrange("a (c p) d -> p (a c) d", p=P)).then_inc(done, 16)


def first_experts(I, B, sp, layer, done):
    _, _, b_up, b_down = expert_weights(I, layer)
    for k in range(2):
        load_expert(I, B, sp, layer, k, k, done)
        if b_down is not None:
            sp.dma_start(B.b_down[:, k, :], b_down[bass.ds(k, 1)].broadcast_to([P, D])).then_inc(done, 16)
    if b_up is not None:
        sp.dma_start(B.b_rows[:, :], b_up.rearrange("e (c p) -> (e c) p", p=P)).then_inc(done, 16)
    return 16 * (6 if b_up is None else 7)


def experts(nc, I, B, layer, cap, rows_n, rows, outs):
    tiles = cap // rows_n
    gated = layer == 0
    half = cap // 2 if gated else cap
    names = ("w0 w1 xe0 xe1 b0 b1 xt_psum0 xt_psum1 xt h_psum h_act h y_psum0 y_psum1 y y_out0 y_out1 bt_psum bt bcol")
    ps = B.ps
    _, _, b_up, b_down = expert_weights(I, layer)
    n_w = 3 if gated else 2
    with phase(nc, B, f"experts{layer}", names) as (block, s):
        w_in, xe_in, b_in2 = (s["w0"], s["w1"]), (s["xe0"], s["xe1"]), (s["b0"], s["b1"])
        xt_psum, y_psum, y_out = (s["xt_psum0"], s["xt_psum1"]), (s["y_psum0"], s["y_psum1"]), (s["y_out0"], s["y_out1"])
        xt_view = ps[:, 0:2, :].rearrange("p a b -> p (a b)")
        y_view = ps[:, 6:8, :].rearrange("p a b -> p (a b)")
        steps = 8 if gated else 4
        TURNS = EXPERTS // 2

        def h_bank(m):
            return 2 + (m % 2) * 2 if gated else 2 + m

        @block.sync
        def _(sp):
            def rows_of(e, k):
                src = rows.rearrange("(e r) d -> e r d", e=EXPERTS)[bass.ds(e, 1)].rearrange("a (j p) d -> p (a j) d", p=rows_n)
                sp.dma_start(B.xe[0:rows_n, k, 0:tiles, :], src).then_inc(xe_in[k], 16)

            for k in range(2):
                rows_of(k, k)
            with sp.Fori(1, TURNS) as i:
                for k in range(2):
                    sp.wait_ge(xt_psum[k], i)
                    rows_of(2 * i + k, k)
                    sp.wait_ge(y_psum[k], i)
                    load_expert(I, B, sp, layer, 2 * i + k, k, w_in[k])
                    if not gated:
                        sp.wait_ge(y_out[k], 16 * i)
                        sp.dma_start(B.b_down[:, k, :], b_down[bass.ds(2 * i + k, 1)].broadcast_to([P, D])).then_inc(b_in2[k], 16)

        @block.tensor
        def _(pe):
            def transposes(i, k, first=False):
                pe.wait_ge(xe_in[k], 16 * i + 16)
                if not first:
                    pe.wait_ge(s["xt"], 2 * i + k)
                for j in range(tiles):
                    last = nc.tensor.transpose(xt_view[:, j * rows_n:(j + 1) * rows_n], B.xe[0:rows_n, k, j, :],
                                               B.ident[0:rows_n, 0:rows_n])
                last.then_inc(xt_psum[k], 1)

            def expert(i, k, more):
                n = 2 * i + k
                pe.wait_ge(s["xt"], n + 1)
                if not isinstance(i, int) or i > 0:
                    pe.wait_ge(w_in[k], 16 * n_w * i)
                for m in range(steps):
                    c, a = (m // 2, (m % 2) * half) if gated else (m, 0)
                    if gated and m >= 2:
                        pe.wait_ge(s["h"], steps * n + m - 1)
                    for g in range(2 if gated else 1):
                        last = nc.tensor.matmul(ps[:, h_bank(m) + g, 0:half], B.w_up[:, k, g, c * P:(c + 1) * P],
                                                B.xe_ts[k][:, a:a + half], start=True, stop=True)
                    last.then_inc(s["h_psum"], 1)
                if more:
                    transposes(i + k, 1 - k)
                pe.wait_ge(s["h"], steps * (n + 1))
                if k or not isinstance(i, int) or i > 0:
                    pe.wait_ge(s["y"], n)
                for j in range(tiles):
                    for c in range(FCH):
                        last = nc.tensor.matmul(y_view[0:rows_n, j * P:(j + 1) * P],
                                                B.h_t[:, c, j * rows_n:(j + 1) * rows_n], B.w_down[:, k, c, :],
                                                start=c == 0, stop=c == FCH - 1)
                last.then_inc(y_psum[k], 1)

            if not gated:
                nc.tensor.transpose(ps[:, 2, 0:EXPERTS * FCH], B.b_rows[:, :], B.ident[0:32, 0:32]).then_inc(s["bt_psum"], 1)
            transposes(0, 0, first=True)
            if not gated:
                pe.wait_ge(s["bt"], 1)
            with pe.Fori(0, TURNS - 1) as i:
                for k in range(2):
                    expert(i, k, True)
            expert(TURNS - 1, 0, True)
            expert(TURNS - 1, 1, False)

        @block.scalar
        def _(act):
            with act.Fori(0, TURNS) as i:
                for k in range(2):
                    n = 2 * i + k
                    if gated:
                        for m in range(steps):
                            act.wait_ge(s["h_psum"], steps * n + m + 1)
                            act.wait_ge(s["h"], steps * n + max(m - 1, 0))
                            nc.scalar.activation(B.h_gate[:, m % 2, 0:half], ps[:, h_bank(m), 0:half], ACT.Silu).then_inc(s["h_act"], 1)
                    else:
                        act.wait_ge(s["bcol"], n + 1)
                        act.wait_ge(y_psum[1 - k], i + k)
                        for m in range(steps):
                            act.wait_ge(s["h_psum"], steps * n + m + 1)
                            nc.scalar.activation(B.h_t[:, m, 0:cap], ps[:, h_bank(m), 0:cap], ACT.Gelu,
                                                 bias=B.b_up[:, k, m:m + 1]).then_inc(s["h"], 1)

        @block.vector
        def _(dve):
            def transposed(i, k):
                dve.wait_ge(xt_psum[k], i + 1)
                nc.vector.tensor_copy(B.xe_ts[k][:, 0:cap], xt_view[:, 0:cap]).then_inc(s["xt"], 1)

            def bias_columns(i, k):
                n = 2 * i + k
                if not isinstance(i, int) or i > 0:
                    dve.wait_ge(s["h"], steps * (n - 1))
                nc.vector.tensor_scalar(B.b_up[:, k, :], B.b_cols[:, bass.ds(n * FCH, FCH)], 0.0, None, ALU.add).then_inc(s["bcol"], 1)

            def expert(i, k, more):
                n = 2 * i + k
                if gated:
                    dve.wait_ge(y_psum[1 - k], i + k)
                    for m in range(steps):
                        c, a = m // 2, (m % 2) * half
                        dve.wait_ge(s["h_act"], steps * n + m + 1)
                        nc.vector.tensor_tensor(B.h_t[:, c, a:a + half], ps[:, h_bank(m) + 1, 0:half],
                                                B.h_gate[:, m % 2, 0:half], ALU.mult).then_inc(s["h"], 1)
                if more:
                    if not gated:
                        bias_columns(i + k, 1 - k)
                    transposed(i + k, 1 - k)
                dve.wait_ge(y_psum[k], i + 1)
                dve.wait_ge(y_out[k], 16 * i)
                src = y_view[0:rows_n, 0:tiles * P].rearrange("p (j d) -> p j d", d=P)
                if gated:
                    nc.vector.tensor_copy(B.ye[0:rows_n, k, 0:tiles, :], src).then_inc(s["y"], 1)
                else:
                    if not isinstance(i, int) or i > 0:
                        dve.wait_ge(b_in2[k], 16 * i)
                    nc.vector.tensor_tensor(B.ye[0:rows_n, k, 0:tiles, :], src,
                                            B.b_down[0:rows_n, k, :].unsqueeze(1).to_broadcast([rows_n, tiles, D]),
                                            ALU.add).then_inc(s["y"], 1)

            if not gated:
                dve.wait_ge(s["bt_psum"], 1)
                nc.vector.tensor_copy(B.b_cols[:, :], ps[:, 2, 0:EXPERTS * FCH]).then_inc(s["bt"], 1)
                dve.wait_ge(s["bt"], 1)
                bias_columns(0, 0)
            transposed(0, 0)
            with dve.Fori(0, TURNS - 1) as i:
                for k in range(2):
                    expert(i, k, True)
            expert(TURNS - 1, 0, True)
            expert(TURNS - 1, 1, False)

        @block.gpsimd
        def _(pool):
            with pool.Fori(0, TURNS) as i:
                for k in range(2):
                    n = 2 * i + k
                    pool.wait_ge(s["y"], n + 1)
                    pool.nop()
                    dst = outs.rearrange("(e r) d -> e r d", e=EXPERTS)[bass.ds(n, 1)].rearrange("a (j p) d -> p (a j) d", p=rows_n)
                    pool.dma_start(dst, B.ye[0:rows_n, k, 0:tiles, :]).then_inc(y_out[k], 16)
            for k in range(2):
                pool.wait_ge(y_out[k], 16 * TURNS)


class Buffers:
    pass


def build(nc, I, out):
    with ExitStack() as ctx:
        B = Buffers()
        B.used_semaphores = []

        def sb(name, shape, dt=F32):
            return ctx.enter_context(nc.sbuf_tensor(name, shape, dt))

        B.ps = ctx.enter_context(nc.psum_tensor("ps", [P, 8, 512], F32))
        B.x_res = sb("x_res", [P, TILES, D])
        B.xn = sb("xn", [P, TILES, D])
        B.xn_t = sb("xn_t", [P, TOKENS])
        B.ident = sb("ident", [P, P])
        B.ones = sb("ones", [P, P])
        B.same_head = sb("same_head", [P, P])
        B.not_same_head = sb("not_same_head", [P, P])
        B.same_expert = sb("same_expert", [P, P])
        B.low_expert = sb("low_expert", [P, P])
        B.bo_row = sb("bo_row", [P, P])
        B.te_val = sb("te_val", [P, P])
        B.te_keep = sb("te_keep", [P, P])
        B.te_tie = sb("te_tie", [P, P])
        B.te_rank = sb("te_rank", [P, P])
        B.te_slot = sb("te_slot", [P, P])
        B.wq0 = sb("wq0", [P, P])
        B.wk0 = sb("wk0", [P, P])
        B.wv0 = sb("wv0", [P, P])
        B.wo0 = sb("wo0", [P, P])
        B.ident_b = sb("ident_b", [P, P], BF16)
        B.causal_b = sb("causal_b", [P, P], BF16)
        B.router = sb("router", [P, 3, EXPERTS])
        B.bf_col = sb("bf_col", [P, 1])
        B.bf_row = sb("bf_row", [P, FEAT])
        B.wqf = sb("wqf", [P, HEADS * FEAT])
        B.wkf = sb("wkf", [P, HEADS * FEAT])
        B.wqt = sb("wqt", [P, 2, P])
        B.expert_m8 = sb("expert_m8", [P, TILES, EXPERTS])
        B.r_a = sb("r_a", [P, TILES, EXPERTS])
        B.r_exp = sb("r_exp", [P, TILES, EXPERTS])
        B.r_prob = sb("r_prob", [P, TILES, EXPERTS])
        B.r_choice = sb("r_choice", [P, TILES, EXPERTS])
        B.r_one = sb("r_one", [P, 2, TILES, EXPERTS])
        B.int_a = sb("int_a", [P, P], I32)
        B.int_b = sb("int_b", [P, 1], I32)
        B.own_expert = sb("own_expert", [P, 1])
        B.gate_bits = sb("gate_bits", [P, TRIES * ROUNDS], I32)
        B.half_neg = sb("half_neg", [P, TILES])
        B.mean = sb("mean", [P, TILES])
        B.variance = sb("variance", [P, TILES])
        B.rstd = sb("rstd", [P, TILES])
        B.v_a = sb("v_a", [P, TILES])
        B.v_b = sb("v_b", [P, TILES])
        B.squares = sb("squares", [P, 2, 512])
        B.gate = sb("gate", [P, 2, TILES])
        B.to_slot = sb("to_slot", [P, 2, TILES], I32)
        B.from_slot = sb("from_slot", [P, 2, TILES], I32)
        B.c_count = sb("c_count", [P, TRIES])
        B.c_above = sb("c_above", [P, 1])
        B.c_ties = sb("c_ties", [P, 1])
        B.c_kept = sb("c_kept", [P, 1])
        B.c_room = sb("c_room", [P, 1])
        B.c_start = sb("c_start", [P, 1])
        B.thr = sb("thr", [P, 1 + TRIES], I32)
        B.thr_try = sb("thr_try", [P, TRIES], I32)
        B.x_b = sb("x_b", [P, SEQ + 1])
        B.va0 = sb("va0", [P, 2, HEADS, 9])
        B.kv0 = sb("kv0", [P, PAIRS, 32])
        B.den = sb("den", [P, 2 * HEADS])
        B.o_nat = sb("o_nat", [P, 2, D])
        B.o_t = sb("o_t", [P, 2, D])
        B.w_kv_down = sb("w_kv_down", [P, P])
        B.w_kv_up = sb("w_kv_up", [P, 2 * HEADS * HS])
        B.w_q = sb("w_q", [P, HEADS * HS])
        B.w_out = sb("w_out", [P, 8, D])
        B.latent = sb("latent", [P, SEQ])
        B.q_t = sb("q_t", [P, 8, SEQ])
        B.k_t = sb("k_t", [P, 8, SEQ])
        B.v_nat = sb("v_nat", [P, 2, HEADS, HS])
        B.neg_max = sb("neg_max", [P, 2, 2, 2])
        B.p_sum = sb("p_sum", [P, 2, 2, 2])
        B.p_nat = sb("p_nat", [P, 2, 2, 512])
        B.y_nat = sb("y_nat", [P, 2, HEADS * HS])
        B.y_t = sb("y_t", [P, 2, 8, P])
        B.p_t = sb("p_t", [P, 2, 2, 512])
        B.wq2 = sb("wq2", [P, P])
        B.wk2 = sb("wk2", [P, P])
        B.bk2_row = sb("bk2_row", [P, P])
        B.bq2 = sb("bq2", [P, 1])
        B.bk2 = sb("bk2", [P, 1])
        B.bq2_scaled = sb("bq2_scaled", [P, 1])
        B.neg_max2 = sb("neg_max2", [P, 2, 4])
        B.rden2 = sb("rden2", [P, 2, 4])
        B.gain = sb("gain", [P, 1])
        B.gain_s = sb("gain_s", [P, 1])
        B.w3 = sb("w3", [P, 7, D])
        B.w3_t = sb("w3_t", [P, 7, D])
        B.mu = sb("mu", [P, 4])
        B.w_norm = sb("w_norm", [P, 4])
        B.qk_len = sb("qk_len", [P, TILES * 2 * HEADS])
        B.qk = sb("qk", [P, 4, SEQ])
        B.a_nat = sb("a_nat", [P, 2, P])
        B.a_t = sb("a_t", [P, 2, P])
        B.a_max = sb("a_max", [P, 2])
        B.a_sum = sb("a_sum", [P, 2])
        B.xe = sb("xe", [P, 2, 5, D])
        B.xe_t = sb("xe_t", [P, CAP0])
        B.h_t = sb("h_t", [P, FCH, CAP0])
        B.h_gate = sb("h_gate", [P, 2, CAP0 // 2])
        B.w_up = sb("w_up", [P, 2, 2, FF])
        B.w_down = sb("w_down", [P, 2, FCH, D])
        B.ye = sb("ye", [P, 2, 5, D])
        B.b_rows = sb("b_rows", [EXPERTS * FCH, P])
        B.b_cols = sb("b_cols", [P, EXPERTS * FCH])
        B.b_up = sb("b_up", [P, 2, FCH])
        B.b_down = sb("b_down", [P, 2, D])
        arena = sb("arena", [P, 2 * TILES * D])
        B.qf = (arena[:, 0:PAIRS * SEQ].rearrange("p (a b) -> p a b", a=PAIRS), B.q_t)
        B.kf = (arena[:, PAIRS * SEQ:PAIRS * SEQ + 2 * HEADS * FEAT].rearrange("p (a b) -> p a b", a=2),
                B.k_t[:, :, :].rearrange("p a b -> p (a b)").rearrange("p (a b) -> p a b", a=2))
        B.va = (B.va0, B.v_nat[:, :, :, :].rearrange("p t h d -> p (t h d)")[:, 0:288].rearrange("p (t h d) -> p t h d", t=2, d=9))
        B.num_t = B.p_nat[:, 0, 0, :]
        B.xe_ts = (B.xe_t[:, :], B.y_t[:, 0, 0:5, :].rearrange("p a b -> p (a b)"))
        B.x_st = (B.x_b[:, 0:SEQ], B.latent[:, :])
        halves = (arena[:, 0:TILES * D], arena[:, TILES * D:2 * TILES * D])
        B.q_rows = tuple(t.bitcast(BF16).rearrange("p (h q) -> p h q", h=HEADS) for t in halves)
        B.k_rows = tuple(t[:, :, :].rearrange("p a b -> p (a b)").bitcast(BF16).rearrange("p (h q) -> p h q", h=HEADS)
                         for t in (B.q_t, B.k_t))
        B.x_v = B.v_nat[:, 1, 0:4, :].rearrange("p h d -> p (h d)")
        B.qk2_t = B.y_nat[:, 0, 0:512].rearrange("p (a q) -> p a q", a=2)
        B.qk2_rest = B.y_nat[:, 0, 512:1024].rearrange("p (a q) -> p a q", a=2)
        B.parts = B.y_nat[:, 1, 0:768].bitcast(BF16).rearrange("p (a i q) -> p a i q", a=2, i=3)
        B.parts_dram = nc.dram_tensor("parts", [2, P, 3, SEQ], BF16, kind="Internal").ap()
        B.back = arena[:, :].rearrange("p (k t d) -> p k t d", k=2, t=TILES)
        B.va2 = tuple(t[:, 0:2 * HEADS * 32].rearrange("p (t h c) -> p t h c", t=2, c=32) for t in (B.w_q, B.w_kv_up))
        B.yt2 = B.latent
        queries, keys, values = (t.rearrange("p a b -> p (a b)") for t in (B.q_t[:, :, :], B.k_t[:, :, :],
                                                                         B.v_nat[:, :, :, :].rearrange("p t h d -> p t (h d)")))
        pair = lambda ap: ap.rearrange("p (a q) -> p a q", a=2)
        B.mix_pre = (pair(queries[:, 0:512]), pair(queries[:, 512:1024]))
        B.mix = (pair(queries[:, 1024:1536]), pair(queries[:, 1536:2048]))
        B.k_act, B.r_gate, B.v3_t, B.o3_t = (keys[:, n * 512:(n + 1) * 512] for n in range(4))
        B.r_kv = values[:, 0:512]
        B.squares3 = keys[:, 0:512]
        B.o3_nat = values[:, 512:1024].rearrange("p (t d) -> p t d", d=D)
        B.x_pair = pair(values[:, 1024:1024 + 2 * (SEQ + 1)])
        B.qk_all = arena[:, :].rearrange("p (b q) -> p b q", b=BATCHES)
        def heads_by(t, a):
            return t.rearrange("p (a b) -> p a b", a=a)
        B.q_ts = (B.q_t, heads_by(arena[:, 0:TILES * D], 8))
        B.k_ts = (B.k_t, heads_by(arena[:, TILES * D:2 * TILES * D], 8))
        B.v_nats = (B.v_nat, B.y_nat[:, :, :].rearrange("p t (h d) -> p t h d", d=HS))
        B.zeros = B.q_t[:, :, :].rearrange("p a b -> p (a b)")[:, 0:1536]
        B.wf_diag = B.y_nat[:, 0, :]
        def slots(name, cap):
            return nc.dram_tensor(name, [EXPERTS * cap, D], F32, kind="Internal").ap()

        B.rows0 = slots("rows0", CAP0)
        B.rows1 = slots("rows1", CAP1)
        B.rows2 = slots("rows2", CAP2)
        B.outs0 = slots("outs0", CAP0)
        B.outs1 = slots("outs1", CAP1)
        B.outs2 = slots("outs2", CAP2)

        setup(nc, I, B)
        norm_and_route(nc, I, B, 0, CAP0)
        linear_attention(nc, I, B)
        experts(nc, I, B, 0, CAP0, ROWS0, B.rows0, B.outs0)
        norm_and_route(nc, I, B, 1, CAP1, B.outs0, 2, B.bo_row)
        latent_attention(nc, I, B)
        experts(nc, I, B, 1, CAP1, ROWS1, B.rows1, B.outs1)
        norm_and_route(nc, I, B, 2, CAP2, B.outs1, 1)
        small_head_attention(nc, I, B)
        experts(nc, I, B, 2, CAP2, ROWS2, B.rows2, B.outs2)
        norm_and_route(nc, I, B, 3, 0, B.outs2, 1)
        channel_attention_and_mix(nc, B, out)


_INS = ['L0_attn_x', 'L0_attn_Wq', 'L0_attn_Wk', 'L0_attn_Wv', 'L0_attn_Wo', 'L0_attn_bo', 'L0_attn_Wf', 'L0_attn_bf',
        'L0_ffn_router_gate', 'L0_ffn_gate_w', 'L0_ffn_up_w', 'L0_ffn_down_w', 'L1_attn_w_kv_down', 'L1_attn_w_kv_up',
        'L1_attn_w_q', 'L1_attn_w_out', 'L1_ffn_wg', 'L1_ffn_W1', 'L1_ffn_b1', 'L1_ffn_W2', 'L1_ffn_b2', 'L2_attn_Wq',
        'L2_attn_bq', 'L2_attn_Wk', 'L2_attn_bk', 'L2_ffn_router_w', 'L2_ffn_w1', 'L2_ffn_b1', 'L2_ffn_w2', 'L2_ffn_b2',
        'L3_attn_gain', 'L3_attn_w_q', 'L3_attn_w_k', 'L3_attn_w_v', 'L3_attn_w_o', 'L3_ffn_W_r', 'L3_ffn_W_k',
        'L3_ffn_W_v', 'L3_ffn_mu_r', 'L3_ffn_mu_k']


def kernel(**inputs):
    import concourse.bacc as bacc
    from concourse.bass_utils import run_bass_kernel_spmd as run

    nc = bacc.Bacc("TRN2", target_bir_lowering=False, num_devices=1)
    arrays, ins = {}, {}
    for name in _INS:
        a = np.ascontiguousarray(inputs[name])
        arrays[f"in_{name}"] = a
        ins[name] = nc.dram_tensor(f"in_{name}", a.shape, mybir.dt.from_np(a.dtype), kind="ExternalInput").ap()
    out = nc.dram_tensor("out", [BATCHES, SEQ, D], F32, kind="ExternalOutput").ap()
    build(nc, ins, out)
    return run(nc, [arrays], core_ids=[0]).results[0]["out"]
```
